# Optimizing a Trainium2 kernel written in Bass

```python
import numpy as np
import jax
import jax.numpy as jnp

def _softmax(x, axis=-1):
    return jax.nn.softmax(x, axis=axis)

def _gelu(x):
    return jax.nn.gelu(x, approximate=True)

def _silu(x):
    return jax.nn.silu(x)

def _sigmoid(x):
    return jax.nn.sigmoid(x)

def _layernorm(x, axis=-1, eps=1e-05):
    m = jnp.mean(x, axis=axis, keepdims=True)
    v = jnp.var(x, axis=axis, keepdims=True)
    return (x - m) / jnp.sqrt(v + eps)

def _scatter_add(tgt, idx, src, axis=0):
    return tgt.at[idx].add(src)

def _segment_sum(src, seg, n):
    return jax.ops.segment_sum(src, seg, n)
kernel_name = 'mk_early_fusion_embed_d1_tok_img1024_r4_4e25eb'

def setup_inputs(seed: int=0):
    np.random.seed(seed)
    _w = jnp.asarray

    def _rec_inputs():
        import jax
        import jax.numpy as jnp
        _rk = jax.random.key(seed)
        x = -0.00016672 + 0.999947 * jax.random.normal(jax.random.fold_in(_rk, 1), (64, 3, 96, 96), jnp.float32)
        x_txt = jax.random.randint(jax.random.fold_in(_rk, 51), (64, 77), 0, 127999, jnp.int32)
        return (x, x_txt)
    x, x_txt = _rec_inputs()

    def _L0_tok_setup():
        import jax, jax.numpy as jnp
        import numpy as np
        IMG = 96
        PATCH = 16
        C_IN = 3
        EMBED = 256
        NPH = IMG // PATCH
        NUM_PATCHES = NPH * NPH
        PATCH_DIM = PATCH * PATCH * C_IN
        key = jax.random.key(seed)
        k_x, k_w, k_b, k_cls, k_pos = jax.random.split(key, 5)
        x = jax.random.normal(k_x, (64, C_IN, IMG, IMG), dtype=jnp.float32)
        W = jax.random.normal(k_w, (EMBED, PATCH_DIM), dtype=jnp.float32) * (1.0 / np.sqrt(PATCH_DIM))
        b = jax.random.normal(k_b, (EMBED,), dtype=jnp.float32) * 0.01
        cls_token = jax.random.normal(k_cls, (1, 1, EMBED), dtype=jnp.float32) * 0.02
        pos_embed = jax.random.normal(k_pos, (1, NUM_PATCHES + 1, EMBED), dtype=jnp.float32) * 0.02
        return {'x': x, 'W': W, 'b': b, 'cls_token': cls_token, 'pos_embed': pos_embed}
    _L0_tok_all = _L0_tok_setup()
    _L0_tok_in = {k: v for k, v in _L0_tok_all.items() if k in ('W', 'b', 'cls_token', 'pos_embed')}
    del _L0_tok_all

    def _L0_txt_setup():
        import jax, jax.numpy as jnp
        import numpy as np
        import math
        VOCAB = 32000
        D_MODEL = 256
        CUTOFFS = [5000, 15000, VOCAB]
        B, S = (8, 1024)
        key = jax.random.key(seed)
        ks = jax.random.split(key, 6)
        input_ids = jax.random.randint(ks[0], (B, S), 0, VOCAB)
        emb0 = jax.random.normal(ks[1], (5000, 256), jnp.float32)
        emb0 = emb0.at[0].set(0.0)
        emb1 = jax.random.normal(ks[2], (10000, 64), jnp.float32)
        emb2 = jax.random.normal(ks[3], (17000, 64), jnp.float32)
        proj1 = jax.random.normal(ks[4], (256, 64), jnp.float32) * 0.02
        proj2 = jax.random.normal(ks[5], (256, 64), jnp.float32) * 0.02
        return {'input_ids': input_ids, 'emb0': emb0, 'emb1': emb1, 'emb2': emb2, 'proj1': proj1, 'proj2': proj2}
    _L0_txt_all = _L0_txt_setup()
    _L0_txt_in = {k: v for k, v in _L0_txt_all.items() if k in ('emb0', 'emb1', 'emb2', 'proj1', 'proj2')}
    del _L0_txt_all

    def _L0_attn_setup():
        import jax, jax.numpy as jnp
        import numpy as np
        SEQ_LEN, BATCH, H, N = (1024, 8, 256, 16)

        def _to_c(t):
            return t[..., 0] + 1j * t[..., 1]

        def _s4_kernel(log_dt, inv_w_real, w_imaginary, B, P, C, L):
            dt = jnp.exp(log_dt)
            w = (-jnp.exp(inv_w_real) + 1j * w_imaginary) * dt
            Bc = _to_c(B)
            Cc = _to_c(C)
            Pc = _to_c(P)
            Qc = jnp.conj(Pc)
            Bcat = jnp.concatenate([Bc[None], Pc], axis=0)
            Ccat = jnp.concatenate([Cc[None], Qc], axis=0)
            v = Bcat[:, None] * Ccat[None]
            M = L // 2 + 1
            omega = jnp.exp(-2j * jnp.pi / L * jnp.arange(M)).astype(jnp.complex64)
            z = 2 * (1 - omega) / (1 + omega)
            cauchy = 1.0 / (z[None, None, :] - w[:, :, None])
            r = jnp.einsum('abhn,hnm->abhm', v, cauchy)
            r = r * dt[None, None]
            k_f = r[:1, :1] - r[:1, 1:] * r[1:, :1] / (1 + r[1:, 1:])
            k_f = k_f * 2 / (1 + omega)
            k = jnp.fft.irfft(k_f, n=L, axis=-1)[..., :L]
            return k[0, 0]
        key = jax.random.key(seed)
        ks = jax.random.split(key, 8)
        H_, N_ = (H, N)
        x = jax.random.normal(ks[0], (SEQ_LEN, BATCH, H_), dtype=jnp.float32)
        log_dt = jax.random.normal(ks[1], (H_, 1), dtype=jnp.float32) * 0.5 - 4.6
        inv_w_real = jax.random.normal(ks[2], (H_, N_), dtype=jnp.float32)
        w_imaginary = jax.random.normal(ks[3], (H_, N_), dtype=jnp.float32)
        B = jax.random.normal(ks[4], (H_, N_, 2), dtype=jnp.float32)
        P = jax.random.normal(ks[5], (1, H_, N_, 2), dtype=jnp.float32)
        C = jax.random.normal(ks[6], (H_, N_, 2), dtype=jnp.float32)
        D = jax.random.normal(ks[7], (H_,), dtype=jnp.float32)
        return {'x': x, 'log_dt': log_dt, 'inv_w_real': inv_w_real, 'w_imaginary': w_imaginary, 'B': B, 'P': P, 'C': C, 'D': D}
    _L0_attn_all = _L0_attn_setup()
    _L0_attn_in = {k: v for k, v in _L0_attn_all.items() if k in ('log_dt', 'inv_w_real', 'w_imaginary', 'B', 'P', 'C', 'D')}
    del _L0_attn_all

    def _L0_ffn_setup():
        import jax, jax.numpy as jnp
        import numpy as np
        D_MODEL = 256
        N_EXPERTS = 8
        TOP_K = 2
        FFN_HIDDEN = 4 * D_MODEL
        key = jax.random.key(seed)
        ks = jax.random.split(key, 6)

        def xavier(k, shape):
            fan_in, fan_out = (shape[-2], shape[-1])
            lim = jnp.sqrt(6.0 / (fan_in + fan_out))
            return jax.random.uniform(k, shape, jnp.float32, -lim, lim)
        x = jax.random.normal(ks[0], (4, 512, D_MODEL), jnp.float32)
        w_gate = xavier(ks[1], (N_EXPERTS, D_MODEL))
        W1 = xavier(ks[2], (N_EXPERTS, D_MODEL, FFN_HIDDEN))
        b1 = jnp.zeros((N_EXPERTS, FFN_HIDDEN), jnp.float32)
        W2 = xavier(ks[3], (N_EXPERTS, FFN_HIDDEN, D_MODEL))
        b2 = jnp.zeros((N_EXPERTS, D_MODEL), jnp.float32)
        return {'x': x, 'w_gate': w_gate, 'W1': W1, 'b1': b1, 'W2': W2, 'b2': b2}
    _L0_ffn_all = _L0_ffn_setup()
    _L0_ffn_in = {k: v for k, v in _L0_ffn_all.items() if k in ('w_gate', 'W1', 'b1', 'W2', 'b2')}
    del _L0_ffn_all
    return {'x': x, 'x_txt': x_txt, 'L0_tok_W': _L0_tok_in['W'], 'L0_tok_b': _L0_tok_in['b'], 'L0_tok_cls_token': _L0_tok_in['cls_token'], 'L0_tok_pos_embed': _L0_tok_in['pos_embed'], 'L0_txt_emb0': _L0_txt_in['emb0'], 'L0_txt_emb1': _L0_txt_in['emb1'], 'L0_txt_emb2': _L0_txt_in['emb2'], 'L0_txt_proj1': _L0_txt_in['proj1'], 'L0_txt_proj2': _L0_txt_in['proj2'], 'L0_attn_log_dt': _L0_attn_in['log_dt'], 'L0_attn_inv_w_real': _L0_attn_in['inv_w_real'], 'L0_attn_w_imaginary': _L0_attn_in['w_imaginary'], 'L0_attn_B': _L0_attn_in['B'], 'L0_attn_P': _L0_attn_in['P'], 'L0_attn_C': _L0_attn_in['C'], 'L0_attn_D': _L0_attn_in['D'], 'L0_ffn_w_gate': _L0_ffn_in['w_gate'], 'L0_ffn_W1': _L0_ffn_in['W1'], 'L0_ffn_b1': _L0_ffn_in['b1'], 'L0_ffn_W2': _L0_ffn_in['W2'], 'L0_ffn_b2': _L0_ffn_in['b2']}

def reference(x, x_txt, L0_tok_W, L0_tok_b, L0_tok_cls_token, L0_tok_pos_embed, L0_txt_emb0, L0_txt_emb1, L0_txt_emb2, L0_txt_proj1, L0_txt_proj2, L0_attn_log_dt, L0_attn_inv_w_real, L0_attn_w_imaginary, L0_attn_B, L0_attn_P, L0_attn_C, L0_attn_D, L0_ffn_w_gate, L0_ffn_W1, L0_ffn_b1, L0_ffn_W2, L0_ffn_b2):
    import jax
    import jax.numpy as jnp

    def _L0_tok_ref(x, W, b, cls_token, pos_embed):
        import jax, jax.numpy as jnp
        import numpy as np
        IMG = 96
        PATCH = 16
        C_IN = 3
        EMBED = 256
        NPH = IMG // PATCH
        NUM_PATCHES = NPH * NPH
        PATCH_DIM = PATCH * PATCH * C_IN
        B, C, H, Wd = x.shape
        nph, npw = (H // PATCH, Wd // PATCH)
        patches = x.reshape(B, C, nph, PATCH, npw, PATCH)
        patches = patches.transpose(0, 2, 4, 1, 3, 5)
        patches = patches.reshape(B, nph * npw, C * PATCH * PATCH)
        proj = jnp.einsum('bnd,ed->bne', patches, W) + b
        cls = jnp.broadcast_to(cls_token, (B, 1, cls_token.shape[-1]))
        out = jnp.concatenate([cls, proj], axis=1) + pos_embed
        return out

    def _L0_txt_ref(input_ids, emb0, emb1, emb2, proj1, proj2):
        import jax, jax.numpy as jnp
        import numpy as np
        import math
        VOCAB = 32000
        D_MODEL = 256
        CUTOFFS = [5000, 15000, VOCAB]
        B, S = (8, 1024)
        d_model = emb0.shape[1]
        starts = [0, CUTOFFS[0], CUTOFFS[1]]
        ends = CUTOFFS
        tables = [emb0, emb1, emb2]
        projs = [None, proj1, proj2]
        out = jnp.zeros(input_ids.shape + (d_model,), jnp.float32)
        for start, end, tab, proj in zip(starts, ends, tables, projs):
            mask = (input_ids >= start) & (input_ids < end)
            local = jnp.clip(input_ids - start, 0, tab.shape[0] - 1)
            e = tab[local]
            if proj is not None:
                e = jnp.einsum('bse,de->bsd', e, proj)
            else:
                e = e * (input_ids != 0)[..., None].astype(e.dtype)
            out = out + jnp.where(mask[..., None], e, 0.0)
        return out * math.sqrt(d_model)

    def _L0_attn_ref(x, log_dt, inv_w_real, w_imaginary, B, P, C, D):
        import jax, jax.numpy as jnp
        import numpy as np
        SEQ_LEN, BATCH, H, N = (1024, 8, 256, 16)

        def _to_c(t):
            return t[..., 0] + 1j * t[..., 1]

        def _s4_kernel(log_dt, inv_w_real, w_imaginary, B, P, C, L):
            dt = jnp.exp(log_dt)
            w = (-jnp.exp(inv_w_real) + 1j * w_imaginary) * dt
            Bc = _to_c(B)
            Cc = _to_c(C)
            Pc = _to_c(P)
            Qc = jnp.conj(Pc)
            Bcat = jnp.concatenate([Bc[None], Pc], axis=0)
            Ccat = jnp.concatenate([Cc[None], Qc], axis=0)
            v = Bcat[:, None] * Ccat[None]
            M = L // 2 + 1
            omega = jnp.exp(-2j * jnp.pi / L * jnp.arange(M)).astype(jnp.complex64)
            z = 2 * (1 - omega) / (1 + omega)
            cauchy = 1.0 / (z[None, None, :] - w[:, :, None])
            r = jnp.einsum('abhn,hnm->abhm', v, cauchy)
            r = r * dt[None, None]
            k_f = r[:1, :1] - r[:1, 1:] * r[1:, :1] / (1 + r[1:, 1:])
            k_f = k_f * 2 / (1 + omega)
            k = jnp.fft.irfft(k_f, n=L, axis=-1)[..., :L]
            return k[0, 0]
        L = x.shape[0]
        residual = x * D
        xc = jnp.transpose(x, (1, 2, 0))
        k = _s4_kernel(log_dt, inv_w_real, w_imaginary, B, P, C, L)
        n = 2 * L
        k_f = jnp.fft.rfft(k, n=n, axis=-1)
        x_f = jnp.fft.rfft(xc, n=n, axis=-1)
        out = jnp.fft.irfft(x_f * k_f, n=n, axis=-1)[..., :L]
        out = jax.nn.silu(jnp.transpose(out, (2, 0, 1)) + residual)
        return out

    def _L0_ffn_ref(x, w_gate, W1, b1, W2, b2):
        import jax, jax.numpy as jnp
        import numpy as np
        D_MODEL = 256
        N_EXPERTS = 8
        TOP_K = 2
        FFN_HIDDEN = 4 * D_MODEL
        B, S, D = x.shape
        flat_x = x.reshape(-1, D)
        gate = jax.nn.softmax(flat_x @ w_gate.T, axis=-1)
        topk_scores, topk_idx = jax.lax.top_k(gate, TOP_K)
        cw = (jax.nn.one_hot(topk_idx, N_EXPERTS, dtype=flat_x.dtype) * topk_scores[..., None]).sum(axis=1)
        h = jax.nn.gelu(jnp.einsum('td,edh->teh', flat_x, W1) + b1, approximate=False)
        y = jnp.einsum('teh,ehd->ted', h, W2) + b2
        out = jnp.einsum('ted,te->td', y, cw)
        return out.reshape(B, S, D)
    h = _L0_tok_ref(x, L0_tok_W, L0_tok_b, L0_tok_cls_token, L0_tok_pos_embed)
    h = jnp.concatenate([h, _L0_txt_ref(x_txt, L0_txt_emb0, L0_txt_emb1, L0_txt_emb2, L0_txt_proj1, L0_txt_proj2)], axis=1)
    h = h + _L0_attn_ref(_layernorm(h, axis=-1), L0_attn_log_dt, L0_attn_inv_w_real, L0_attn_w_imaginary, L0_attn_B, L0_attn_P, L0_attn_C, L0_attn_D)
    h = h + _L0_ffn_ref(_layernorm(h, axis=-1), L0_ffn_w_gate, L0_ffn_W1, L0_ffn_b1, L0_ffn_W2, L0_ffn_b2)
    return h

_drawn_inputs = setup_inputs


def setup_inputs(seed=0):
    import zlib

    import numpy as np

    out = dict(_drawn_inputs(seed))
    spreads = {'L0_ffn_b1': (0.0, 0.554), 'L0_ffn_b2': (0.0, 0.451)}
    factors = {'L0_tok_b': 8.0}
    for name, (base, spread) in spreads.items():
        noise = np.random.default_rng([zlib.crc32(name.encode()), seed]).standard_normal(out[name].shape)
        drawn = base * np.exp(spread * noise) if base else spread * noise
        out[name] = jnp.asarray(drawn.astype(out[name].dtype))
    for name, factor in factors.items():
        out[name] = (out[name] * factor).astype(out[name].dtype)
    return out
```

```python
import concourse.bass as bass
from concourse import mybir
from contextlib import ExitStack

F32 = mybir.dt.float32
F16 = mybir.dt.float16
I32 = mybir.dt.int32
ACT = mybir.ActivationFunctionType
ALU = mybir.AluOpType
AX = mybir.AxisListType

P = 128
L, NCOL, D = 64, 114, 256
TILES, PT = L * NCOL // P, 18
TT = TILES - PT
KC = 6
NS, M = 16, L // 2 + 1
KROWS = 2 * M + 1
E, HID = 8, 1024
FCH = HID // P
NT = 2 * TILES + E - 1
SLOTS = NT * P
ROW = D + E + 1
C_CW, C_ID = D, D + E
TOKENS = TILES * P
WSCALE = 64.0
XSCALE = 64.0
VOCAB, CUT0, CUT1 = 32000, 5000, 15000
EPS = 1e-5
PRM = 3 * 2 * NS + 2 * NS + 2

OT, OH = 0, L * D
OX = OH + TILES * D
ARENA = OX + TILES * ROW
WEXP = 4 * 2048 // 2
WORK = E * WEXP


class Link:

    def __init__(self, eng, sem, base=0):
        self.eng, self.sem, self.base, self.n = eng, sem, base, 0

    def add(self, ins):
        ins.then_inc(self.sem, 1)
        self.n += 1

    def sync(self):
        self.eng.wait_ge(self.sem, self.base + self.n)

    def __call__(self, ins):
        self.add(ins)
        self.sync()


def build(nc, xP, Wp, posrows, patsel, clssel, clsrows, ids, table, P12, prm, zc, basis, ident_d, tri_d,
          tokid, dumid, wg, wts, b1T, b2d, iota8, rev8, pcol, trash, kcol, out):
    slots = nc.dram_tensor("slots", (SLOTS + E * P, ROW), F32, kind="Internal").ap()
    ctx = ExitStack()
    with ctx:
        def sb(name, shape, dt=F32):
            return ctx.enter_context(nc.sbuf_tensor(name, shape, dt))

        def sem(name):
            return ctx.enter_context(nc.semaphore(name))

        A = sb("arena", [P, ARENA])
        A16 = A[:, :].bitcast(F16)
        AI = A[:, :].bitcast(I32)
        Tz = A[:, OT:OH].rearrange("p (t h) -> p t h", h=D)
        H3 = A[:, OH:OX].rearrange("p (j d) -> p j d", d=D)
        X3 = A[:, OX:ARENA].rearrange("p (j r) -> p j r", r=ROW)
        XI3 = AI[:, OX:ARENA].rearrange("p (j r) -> p j r", r=ROW)

        def h_tile(j):
            return A[:, bass.ds(j * D + OH, D)]

        def x_tile(j):
            return A[:, bass.ds(j * ROW + OX, D)]

        taken = [OT]

        def scratch(n):
            taken[0] += n
            assert taken[0] <= OH
            return A[:, taken[0] - n:taken[0]]

        pos_sb = scratch(PT * D)[0:3, :]
        prm_sb = scratch(2 * PRM).rearrange("p (c k) -> p c k", k=PRM)
        zc_sb = scratch(4 * M)
        KF = scratch(2 * KROWS).rearrange("p (c k) -> p c k", k=KROWS)
        big = [scratch(2 * M * NS) for _ in range(6)]
        vec = [scratch(2 * NS) for _ in range(16)]
        frq = [scratch(2 * M) for _ in range(20)]
        psel = scratch(P)[0:3, :]
        ids_f, idx_f, mk0, mk1, mk2, mtmp = [scratch(TT) for _ in range(6)]

        B = sb("ring_arena", [P, 4096])
        Wp_sb = B[:, 0:KC * D].rearrange("p (k d) -> p k d", d=D)
        xP_sb = [B[:, 1536 + 768 * s:1536 + 768 * (s + 1)] for s in range(2)]
        e_sb = [B[:, 3072 + P * s:3072 + P * (s + 1)] for s in range(6)]
        kfT = B[0:KROWS, 0:D]
        eT = B[:, 1536:1536 + 6 * P]
        silu_sb = [B[:, 512 * s:512 * s + 8 * TILES] for s in range(3)]
        xr_sb = [B[:, D * s:D * (s + 1)] for s in range(6)]
        xT_sb = [B[:, 1536 + 768 * s:1536 + 768 * (s + 1)] for s in range(2)]
        stage = [B[:, 2048 * s:2048 * (s + 1)] for s in range(2)]

        ident = sb("ident", [P, P])
        tri = sb("tri", [P, P])
        ones = sb("ones", [P, P])
        basis_sb = sb("basis_sb", [KROWS, 2 * L - 1])
        P12_sb = sb("P12_sb", [P, D])
        csel = sb("csel", [2, P])
        crow = sb("crow", [2, D])
        ids_sb = sb("ids_sb", [P, TT], I32)
        idx = sb("idx", [P, TT], I32)
        mk = sb("mk", [P, 3 * TT])
        stats = [sb(f"stats{s}", [P, 18]) for s in range(2)]
        mv = [sb(f"mv{s}", [P, 6]) for s in range(2)]
        veps = [sb(f"veps{s}", [P, 3]) for s in range(2)]
        eps3 = sb("eps3", [P, 3])
        expo = sb("expo", [P, 3])
        rstd = [sb(f"rstd{s}", [P, 3]) for s in range(2)]
        wg_sb = sb("wg_sb", [P, 2 * E])
        b1_sb = sb("b1_sb", [P, E * FCH])
        iota_sb = sb("iota_sb", [P, E])
        rev_sb = sb("rev_sb", [P, E])
        pcol_sb = sb("pcol_sb", [P, 1])
        trash_sb = sb("trash_sb", [P, E])
        tokid_sb = sb("tokid_sb", [P, TILES], I32)
        kcol_sb = sb("kcol_sb", [P, NT])
        posA = sb("posA", [P, TILES], I32)
        posB = sb("posB", [P, TILES], I32)
        padpos = sb("padpos", [P, E], I32)
        dum = sb("dum", [P, ROW])
        t_exp = sb("t_exp", [P, NT])
        t_expi = sb("t_expi", [P, NT], I32)
        meta_cw = sb("meta_cw", [P, NT])
        meta_id = sb("meta_id", [P, NT], I32)
        junk8 = [sb(f"junk8_{s}", [P, E]) for s in range(2)]
        rid = [sb(f"rid{s}", [P, 1], I32) for s in range(2)]

        GE = TILES * E
        g_log, g_ex, sel1, sel2, selS, g_t, cnt, incl, posf = [
            A[:, OT + GE * n:OT + GE * (n + 1)] for n in range(9)]
        smalls = OT + GE * 9
        zero57, mx, sm, pfa, pfb = [A[:, smalls + TILES * n:smalls + TILES * (n + 1)] for n in range(5)]
        s8 = smalls + 5 * TILES
        tot, pd, inc8, off, padn, pm, ppf, z8 = [A[:, s8 + E * n:s8 + E * (n + 1)] for n in range(8)]
        pdi = AI[:, s8 + 8 * E:s8 + 9 * E]
        pdj = AI[:, s8 + 9 * E:s8 + 10 * E]

        at = [WORK]

        def work(n):
            at[0] += n
            assert at[0] <= ARENA
            return at[0] - n

        xs_at = [work(ROW) for _ in range(2)]
        xs = [A[:, a:a + ROW] for a in xs_at]
        xsI = [AI[:, a:a + ROW] for a in xs_at]
        xh_at = [work(D) for _ in range(2)]
        xhi = [A16[:, 2 * a:2 * a + D] for a in xh_at]
        xlo = [A16[:, 2 * a + D:2 * a + 2 * D] for a in xh_at]
        hg = [A[:, a:a + HID] for a in (work(HID), work(HID))]
        hh_at = [work(HID) for _ in range(2)]
        hhi = [A16[:, 2 * a:2 * a + HID] for a in hh_at]
        hlo = [A16[:, 2 * a + HID:2 * a + 2 * HID] for a in hh_at]
        ys = [A[:, a:a + D] for a in (work(D), work(D))]
        b2_at = work(E * D)
        b2f = A[0:2, b2_at:b2_at + E * D]
        b2l_at = work(E * D)
        b2l = A[0:2, b2l_at:b2l_at + E * D]
        b2p_at = work(E * D)
        b2h = A16[0:2, 2 * b2p_at:2 * b2p_at + E * D]
        b2r = A16[0:2, 2 * b2p_at + E * D:2 * b2p_at + 2 * E * D]
        one16_at = work(P // 2)
        one16 = A16[0:2, 2 * one16_at:2 * one16_at + P]

        PS = ctx.enter_context(nc.psum_tensor("PS", [P, 8 * 512], F32))

        def bank(b, n=512, o=0):
            return PS[:, 512 * b + o:512 * b + o + n]

        names = """const_loaded patch_const_loaded s4_loaded ids_loaded gate_const_loaded
            patch_done h_patch kf_ready kfT_psum kfT_ready toep_done toep_ready s4_step
            idx_ready mask_ready e_ready eT_psum eT_ready text_done h_text ln1_step xn_ready text_step
            conv_done silu_done h1_ready ln2_step xr_ready xT_psum xT_ready gate_done row_kept
            exp_in exp_out gate_step sel_ready ranks_done pos_ready meta_ready
            prefill_done tail_done dummy_ready
            w1_free w2_free w1_hi w2_hi w1_lo w2_lo rows_done
            b2_loaded b2_step b2_ready xt_done x_split gelu_done mm1_done h_split mm2_done y_done
            y_step slot_free meta_step pad_scat tick tick2 var1_ready var2_ready
            rstd1_ready rstd2_ready veps_rstd1_ready veps_rstd2_ready expo_ready""".split()
        S = {n: sem(n) for n in names}
        patch_loaded = [sem(f"patch_loaded{s}") for s in range(2)]
        gathered = [sem(f"gathered{s}") for s in range(3)]
        scat_a = [sem(f"scat_a{s}") for s in range(3)]
        scat_b = [sem(f"scat_b{s}") for s in range(3)]
        w1_loaded, w2_loaded = sem("w1_loaded"), sem("w2_loaded")
        slot_loaded = [sem(f"slot_loaded{s}") for s in range(2)]
        added = [sem(f"added{s}") for s in range(2)]

        block = ctx.enter_context(nc.Block())

        N_S4, N_IDS, N_CONST, N_PC, N_GC = 2, 1, 2, 5, 11

        @block.sync
        def _(sp):
            sp.dma_start(ids_sb[:, :], ids).then_inc(S["ids_loaded"], 16)
            sp.dma_start(prm_sb, prm).then_inc(S["s4_loaded"], 16)
            sp.dma_start(zc_sb, zc).then_inc(S["s4_loaded"], 16)
            sp.dma_start(B[:, 0:KC * D], Wp).then_inc(S["patch_const_loaded"], 16)
            sp.dma_start(pos_sb, posrows).then_inc(S["patch_const_loaded"], 16)
            sp.dma_start(psel, patsel).then_inc(S["patch_const_loaded"], 16)
            sp.dma_start(csel[:, :], clssel).then_inc(S["patch_const_loaded"], 16)
            sp.dma_start(crow[:, :], clsrows).then_inc(S["patch_const_loaded"], 16)
            for s in range(2):
                sp.dma_start(xP_sb[s], xP[s * P:(s + 1) * P, :]).then_inc(patch_loaded[s], 16)
            with sp.Fori(1, PT // 2) as i:
                for s in range(2):
                    sp.wait_ge(S["patch_done"], 2 * i + s - 1)
                    sp.dma_start(xP_sb[s], xP[bass.ds((2 * i + s) * P, P), :]).then_inc(patch_loaded[s], 16)
            sp.wait_ge(S["dummy_ready"], 1)
            sp.wait_ge(S["gate_const_loaded"], 16 * 10)
            sp.dma_start(out[TOKENS:TOKENS + P, :], dum[:, 0:D]).then_inc(S["prefill_done"], 16)
            for n in range(E - 1):
                r = (2 * TILES + n) * P
                sp.dma_start(slots[r:r + P, :], dum[:, :]).then_inc(S["tail_done"], 16)
            sp.wait_ge(S["h1_ready"], 32)
            sp.dma_start(out[0:TOKENS, :].rearrange("(j p) d -> p j d", p=P), H3).then_inc(S["prefill_done"], 16)
            sp.wait_ge(S["meta_ready"], 1)
            sp.wait_ge(S["row_kept"], TILES)
            sp.wait_ge(S["prefill_done"], 32)
            with sp.Fori(0, E) as e:
                sp.wait_ge(S["w1_free"], e + 1)
                sp.dma_start(stage[0], wts[bass.ds(e * 2 * P, P), :]).then_inc(w1_loaded, 16)
                sp.wait_ge(S["w2_free"], e + 1)
                sp.dma_start(stage[1], wts[bass.ds(e * 2 * P + P, P), :]).then_inc(w2_loaded, 16)
            sp.wait_ge(S["rows_done"], 1)
            sp.dma_start(b2f, b2d).then_inc(S["b2_loaded"], 16)
            with sp.Fori(0, NT // 2) as i:
                for s in range(2):
                    sp.wait_ge(S["slot_free"], 2 * i + s + 1)
                    sp.dma_start(xs[s], slots[bass.ds((2 * i + s) * P, P), :]).then_inc(slot_loaded[s], 16)
            sp.wait_ge(S["slot_free"], NT)
            sp.dma_start(xs[0], slots[(NT - 1) * P:NT * P, :]).then_inc(slot_loaded[0], 16)

        @block.gpsimd
        def _(pool):
            nc.gpsimd.memset(eps3[:, :], EPS)
            nc.gpsimd.memset(expo[:, :], -0.5).then_inc(S["expo_ready"], 1)
            pool.wait_ge(S["expo_ready"], 1)
            pool.wait_ge(S["idx_ready"], 1)
            for n in range(TT):
                s = n % 3
                if n >= 3:
                    pool.wait_ge(gathered[s], 16 * (n // 3))
                pool.indirect_dma_start(H3[:, PT + n, :], None, table,
                                        bass.IndirectOffsetOnAxis(ap=idx[:, n:n + 1], axis=0)).then_inc(gathered[s], 16)
            def inv_std(k, st, var_ready, rstd_ready):
                pool.wait_ge(S[var_ready], k + 1)
                var = mv[st][:, :].rearrange("p (s r) -> p s r", r=2)[:, :, 1]
                nc.gpsimd.tensor_tensor(veps[st][:, :], var, eps3[:, :], ALU.add).then_inc(S["veps_" + rstd_ready], 1)
                pool.wait_ge(S["veps_" + rstd_ready], k + 1)
                nc.gpsimd.tensor_tensor(rstd[st][:, :], veps[st][:, :], expo[:, :], ALU.pow).then_inc(S[rstd_ready], 1)

            with pool.Fori(0, TILES // 6) as i:
                for st in range(2):
                    inv_std(2 * i + st, st, "var1_ready", "rstd1_ready")
            inv_std(TILES // 3 - 1, 0, "var1_ready", "rstd1_ready")

            def keep(k, st):
                pool.wait_ge(S["xr_ready"], 3 * k + 3)
                for s in range(3):
                    nc.gpsimd.tensor_copy(x_tile(3 * k + s), xr_sb[3 * st + s]).then_inc(S["row_kept"], 1)

            with pool.Fori(0, TILES // 6) as i:
                for st in range(2):
                    inv_std(2 * i + st, st, "var2_ready", "rstd2_ready")
                for st in range(2):
                    keep(2 * i + st, st)
            inv_std(TILES // 3 - 1, 0, "var2_ready", "rstd2_ready")
            keep(TILES // 3 - 1, 0)
            pool.wait_ge(S["pos_ready"], 1)
            pool.wait_ge(S["tail_done"], 16 * (E - 1))
            for e in range(E):
                pool.indirect_dma_start(slots, bass.IndirectOffsetOnAxis(ap=padpos[:, e:e + 1], axis=0),
                                        dum[:, :], None).then_inc(S["pad_scat"], 16)
            pool.wait_ge(S["row_kept"], TILES)
            for n in range(TILES):
                s = n % 3
                for pos, done in ((posA, scat_a), (posB, scat_b)):
                    if n >= 3:
                        pool.wait_ge(done[s], 16 * (n // 3))
                    pool.indirect_dma_start(slots, bass.IndirectOffsetOnAxis(ap=pos[:, n:n + 1], axis=0),
                                            X3[:, n, :], None).then_inc(done[s], 16)
            pool.wait_ge(S["pad_scat"], 16 * E)
            for s in range(3):
                pool.wait_ge(scat_a[s], 16 * (TILES // 3))
                pool.wait_ge(scat_b[s], 16 * (TILES // 3))
            pool.sem_inc(S["rows_done"], 1)
            pool.wait_ge(S["prefill_done"], 32)

            def add_rows(k, s, before):
                pool.wait_ge(S["y_done"], k + 1)
                if before is not None:
                    pool.wait_ge(added[1 - s], before)
                pool.sem_inc(S["tick2"], 1)
                pool.indirect_dma_start(out, bass.IndirectOffsetOnAxis(ap=rid[s][:, :], axis=0),
                                        ys[s], None, compute_op=ALU.add).then_inc(added[s], 16)

            add_rows(0, 0, None)
            add_rows(1, 1, 16)
            with pool.Fori(1, NT // 2) as i:
                add_rows(2 * i, 0, 16 * i)
                add_rows(2 * i + 1, 1, 16 * i + 16)
            add_rows(NT - 1, 0, 16 * (NT // 2))
            pool.wait_ge(added[0], 16 * (NT // 2 + 1))

        @block.scalar
        def _(act):
            act.dma_start(basis_sb[:, :], basis).then_inc(S["const_loaded"], 16)
            act.dma_start(ident[:, :], ident_d).then_inc(S["const_loaded"], 16)
            act.dma_start(P12_sb[:, :], P12).then_inc(S["const_loaded"], 16)
            for dst, src in ((tri[:, :], tri_d), (wg_sb[:, :], wg), (b1_sb[:, :], b1T), (iota_sb[:, :], iota8),
                             (rev_sb[:, :], rev8), (pcol_sb[:, :], pcol), (trash_sb[:, :], trash),
                             (tokid_sb[:, :], tokid), (kcol_sb[:, :], kcol),
                             (dum[:, C_ID:C_ID + 1].bitcast(I32), dumid)):
                if dst is not None:
                    act.dma_start(dst, src).then_inc(S["gate_const_loaded"], 16)
            act.wait_ge(S["s4_loaded"], 16 * N_S4)
            nc.scalar.activation(prm_sb[:, :, 0:1 + NS], prm_sb[:, :, 0:1 + NS], ACT.Exp).then_inc(S["s4_step"], 1)
            with act.Fori(0, PT // 2) as i:
                for s in range(2):
                    act.wait_ge(S["patch_done"], 2 * i + s + 1)
                    nc.scalar.activation(h_tile(2 * i + s), bank(s, D), ACT.Copy).then_inc(S["h_patch"], 1)
            act.wait_ge(S["kfT_psum"], 1)
            nc.scalar.activation(kfT[:, :], PS[0:KROWS, 1024:1024 + D], ACT.Copy).then_inc(S["kfT_ready"], 1)
            for n in range(L // 2):
                act.wait_ge(S["toep_done"], n + 1)
                nc.scalar.activation(A[:, OT + 512 * n:OT + 512 * (n + 1)], bank(4 + n % 4), ACT.Copy)\
                    .then_inc(S["toep_ready"], 1)

            def text_copy(i, s):
                act.wait_ge(S["eT_psum"], i + 1)
                nc.scalar.activation(eT[:, 3 * P * s:3 * P * (s + 1)], bank(s, 3 * P), ACT.Copy)\
                    .then_inc(S["eT_ready"], 1)

            text_copy(0, 0)
            text_copy(1, 1)
            with act.Fori(1, TT // 6) as i:
                for s in range(2):
                    act.wait_ge(S["text_done"], 2 * i + s - 1)
                    text_copy(2 * i + s, s)
            act.wait_ge(S["text_done"], TT // 3 - 2)
            text_copy(TT // 3 - 1, 0)

            for n in range(32):
                act.wait_ge(S["conv_done"], n + 1)
                if n >= 3:
                    act.wait_ge(S["h1_ready"], n - 2)
                nc.scalar.activation(silu_sb[n % 3], bank(4 + n % 4, 8 * TILES), ACT.Silu)\
                    .then_inc(S["silu_done"], 1)

            def gate_copy(i, s):
                act.wait_ge(S["xT_psum"], i + 1)
                nc.scalar.activation(xT_sb[s][:, 0:512], bank(2 * s), ACT.Copy)
                nc.scalar.activation(xT_sb[s][:, 512:768], bank(2 * s + 1, 256), ACT.Copy)\
                    .then_inc(S["xT_ready"], 1)

            gate_copy(0, 0)
            gate_copy(1, 1)
            with act.Fori(1, TILES // 6) as i:
                for s in range(2):
                    act.wait_ge(S["gate_done"], 2 * i + s - 1)
                    gate_copy(2 * i + s, s)
            act.wait_ge(S["gate_done"], TILES // 3 - 2)
            gate_copy(TILES // 3 - 1, 0)
            act.wait_ge(S["exp_in"], 1)
            nc.scalar.activation(g_ex, g_log, ACT.Exp).then_inc(S["exp_out"], 1)

            act.wait_ge(S["rows_done"], 1)
            with act.Fori(0, E) as e:
                act.wait_ge(w1_loaded, 16 * e + 16)
                nc.scalar.activation(A16[:, bass.ds(e * 8192, 2048)], stage[0], ACT.Copy, scale=WSCALE)\
                    .then_inc(S["w1_hi"], 1)
                act.wait_ge(w2_loaded, 16 * e + 16)
                nc.scalar.activation(A16[:, bass.ds(e * 8192 + 4096, 2048)], stage[1], ACT.Copy, scale=WSCALE)\
                    .then_inc(S["w2_hi"], 1)

            def gelu(k, s, free):
                if free is not None:
                    act.wait_ge(S["h_split"], free)
                e = act.value_load(t_expi[0:1, bass.ds(k, 1)], min_val=0, max_val=E - 1)
                for f in range(FCH):
                    if f % 4 == 0:
                        act.wait_ge(S["mm1_done"], 2 * k + f // 4 + 1)
                    nc.scalar.activation(hg[s][:, P * f:P * (f + 1)], bank(2 + 2 * s, P, P * f) if f < 4 else
                                         bank(3 + 2 * s, P, P * (f - 4)), ACT.Gelu,
                                         bias=b1_sb[:, bass.ds(e * FCH + f, 1)], scale=1.0 / (WSCALE * XSCALE))\
                        .then_inc(S["gelu_done"], 1)

            gelu(0, 0, None)
            gelu(1, 1, None)
            with act.Fori(1, NT // 2) as i:
                gelu(2 * i, 0, 2 * i - 1)
                gelu(2 * i + 1, 1, 2 * i)
            gelu(NT - 1, 0, NT - 2)

        @block.vector
        def _(dve):
            v = nc.vector

            v.memset(ones[:, :], 1.0)
            v.memset(dum[:, 0:C_ID], 0.0).then_inc(S["dummy_ready"], 1)
            dve.wait_ge(S["ids_loaded"], 16)
            t = Link(dve, S["text_step"])
            t(v.tensor_copy(ids_f, ids_sb[:, :]))
            t(v.tensor_scalar(idx_f, ids_f, 0.0, float(VOCAB - 1), ALU.max, ALU.min))
            v.tensor_copy(idx[:, :], idx_f).then_inc(S["idx_ready"], 1)
            root = float(D) ** 0.5
            t.add(v.tensor_scalar(mk0, ids_f, float(CUT0), root, ALU.is_lt, ALU.mult))
            t.add(v.tensor_scalar(mk1, ids_f, float(CUT0), root, ALU.is_ge, ALU.mult))
            t.add(v.tensor_scalar(mk2, ids_f, float(CUT1), root, ALU.is_ge, ALU.mult))
            t(v.tensor_scalar(mtmp, ids_f, 0.0, None, ALU.is_gt))
            t(v.tensor_tensor(mk[:, 0:TT], mk0, mtmp, ALU.mult))
            t(v.tensor_scalar(mtmp, ids_f, float(CUT1), None, ALU.is_lt))
            t(v.tensor_tensor(mk[:, TT:2 * TT], mk1, mtmp, ALU.mult))
            t(v.tensor_scalar(mtmp, ids_f, float(VOCAB), None, ALU.is_lt))
            t(v.tensor_tensor(mk[:, 2 * TT:3 * TT], mk2, mtmp, ALU.mult))

            dve.wait_ge(S["s4_loaded"], 16 * N_S4)
            q = Link(dve, S["s4_step"], 0)
            q.n = 1
            q.sync()

            def s3(a):
                return a.rearrange("p (c n) -> p c n", c=2)

            def pair(at, part):
                return prm_sb[:, :, at:at + 2 * NS].rearrange("p c (n r) -> p c n r", r=2)[:, :, :, part]

            dt = prm_sb[:, :, 0:1].broadcast_to((P, 2, NS))
            ew, wim = prm_sb[:, :, 1:1 + NS], prm_sb[:, :, 1 + NS:1 + 2 * NS]
            o = 1 + 2 * NS
            Br, Bi, Pr, Pi, Cr, Ci = [pair(o + 2 * NS * n, part) for n in range(3) for part in range(2)]
            nwr, wi, bdr, bdi, pdr, pdi_ = [s3(a) for a in vec[0:6]]
            v00r, v00i, v01r, v01i, v10r, v10i, v11 = [s3(a) for a in vec[6:13]]
            t1, t2, t3 = [s3(a) for a in vec[13:16]]
            mul, add, sub = ALU.mult, ALU.add, ALU.subtract
            q.add(v.tensor_tensor(nwr, ew, dt, mul))
            q.add(v.tensor_tensor(wi, wim, dt, mul))
            q.add(v.tensor_tensor(bdr, Br, dt, mul))
            q.add(v.tensor_tensor(bdi, Bi, dt, mul))
            q.add(v.tensor_tensor(pdr, Pr, dt, mul))
            q(v.tensor_tensor(pdi_, Pi, dt, mul))

            def product(outr, outi, ar, ai, br, bi, conj):
                q.add(v.tensor_tensor(t1, ar, br, mul))
                q(v.tensor_tensor(t2, ai, bi, mul))
                q.add(v.tensor_tensor(outr, t1, t2, add if conj else sub))
                q.add(v.tensor_tensor(t3, ai, br, mul))
                q(v.tensor_tensor(outi, ar, bi, mul))
                q(v.tensor_tensor(outi, t3, outi, sub if conj else add))

            product(v00r, v00i, bdr, bdi, Cr, Ci, False)
            product(v01r, v01i, bdr, bdi, Pr, Pi, True)
            product(v10r, v10i, pdr, pdi_, Cr, Ci, False)
            q.add(v.tensor_tensor(t1, pdr, Pr, mul))
            q(v.tensor_tensor(t2, pdi_, Pi, mul))
            q(v.tensor_tensor(v11, t1, t2, add))

            b4 = [a.rearrange("p (c m n) -> p c m n", c=2, n=NS) for a in big]
            den_r, den_i, g1, g2, ca_r, ca_i = b4

            def over_m(a):
                return a.unsqueeze(2).broadcast_to((P, 2, M, NS))

            def const(k):
                return zc_sb[:, k * M:(k + 1) * M].unsqueeze(1).unsqueeze(3).broadcast_to((P, 2, M, NS))

            ar, ai, br, bi = [const(k) for k in range(4)]
            q.add(v.tensor_tensor(g1, over_m(nwr), br, mul))
            q(v.tensor_tensor(g2, over_m(wi), bi, mul))
            q(v.tensor_tensor(g1, g1, g2, add))
            q.add(v.tensor_tensor(den_r, g1, ar, add))
            q(v.tensor_tensor(g2, over_m(nwr), bi, mul))
            q(v.tensor_tensor(den_i, over_m(wi), br, mul))
            q(v.tensor_tensor(g2, g2, den_i, sub))
            q(v.tensor_tensor(den_i, g2, ai, add))
            q.add(v.tensor_tensor(g1, den_r, den_r, mul))
            q(v.tensor_tensor(g2, den_i, den_i, mul))
            q(v.tensor_tensor(g1, g1, g2, add))
            q(v.reciprocal(big[3], big[2]))
            q.add(v.tensor_tensor(ca_r, den_r, g2, mul))
            q(v.tensor_tensor(ca_i, den_i, g2, mul))
            f3 = [a.rearrange("p (c m) -> p c m", c=2) for a in frq]
            s00r, s00i, s01r, s01i, s10r, s10i, s11r, s11i = f3[0:8]
            for outr, outi, vr, vi in ((s00r, s00i, v00r, v00i), (s01r, s01i, v01r, v01i), (s10r, s10i, v10r, v10i)):
                q.add(v.tensor_tensor(g1, over_m(vr), ca_r, mul))
                q.add(v.tensor_tensor(g2, over_m(vi), ca_i, mul))
                q.add(v.tensor_tensor(den_r, over_m(vi), ca_r, mul))
                q(v.tensor_tensor(den_i, over_m(vr), ca_i, mul))
                q.add(v.tensor_tensor(g1, g1, g2, add))
                q(v.tensor_tensor(den_r, den_r, den_i, sub))
                q.add(v.tensor_reduce(outr, g1, AX.X, add))
                q(v.tensor_reduce(outi, den_r, AX.X, add))
            q.add(v.tensor_tensor(g1, over_m(v11), ca_r, mul))
            q(v.tensor_tensor(g2, over_m(v11), ca_i, mul))
            q.add(v.tensor_reduce(s11r, g1, AX.X, add))
            q(v.tensor_reduce(f3[19], g2, AX.X, add))
            q(v.tensor_scalar(s11i, f3[19], -1.0, None, mul))

            b3r = zc_sb[:, 2 * M:3 * M].unsqueeze(1).broadcast_to((P, 2, M))
            b3i = zc_sb[:, 3 * M:4 * M].unsqueeze(1).broadcast_to((P, 2, M))
            u1, u2, nr, ni, mr, mi, dr, di, rr, zr, zi = f3[8:19]

            def cmul(outr, outi, ar, ai, br, bi):
                q.add(v.tensor_tensor(u1, ar, br, mul))
                q(v.tensor_tensor(u2, ai, bi, mul))
                q.add(v.tensor_tensor(outr, u1, u2, sub))
                q.add(v.tensor_tensor(f3[19], ar, bi, mul))
                q(v.tensor_tensor(outi, ai, br, mul))
                q(v.tensor_tensor(outi, f3[19], outi, add))

            cmul(nr, ni, s01r, s01i, s10r, s10i)
            cmul(mr, mi, nr, ni, b3r, b3i)
            cmul(dr, di, s11r, s11i, b3r, b3i)
            q(v.tensor_scalar(dr, dr, 1.0, None, add))
            q.add(v.tensor_tensor(u1, dr, dr, mul))
            q(v.tensor_tensor(u2, di, di, mul))
            q(v.tensor_tensor(u1, u1, u2, add))
            q(v.reciprocal(frq[8 + 8], frq[8]))
            q(v.tensor_scalar(di, di, -1.0, None, mul))
            cmul(zr, zi, mr, mi, dr, di)
            q.add(v.tensor_tensor(zr, zr, rr, mul))
            q(v.tensor_tensor(zi, zi, rr, mul))
            q.add(v.tensor_tensor(KF[:, :, 0:M], s00r, zr, sub))
            q.add(v.tensor_tensor(KF[:, :, M:2 * M], s00i, zi, sub))
            q(v.tensor_copy(KF[:, :, 2 * M:KROWS], prm_sb[:, :, PRM - 1:PRM]))
            dve.sem_inc(S["kf_ready"], 1)

            def stats3(k, st, link, var_ready):
                dve.sem_inc(S["tick"], 1)
                for s in range(3):
                    link.add(v.bn_stats(stats[st][:, 6 * s:6 * s + 6], h_tile(3 * k + s)))
                link.sync()
                dve.sem_inc(S["tick"], 1)
                for s in range(3):
                    last = v.bn_aggr(mv[st][:, 2 * s:2 * s + 2], stats[st][:, 6 * s:6 * s + 6])
                last.then_inc(S[var_ready], 1)

            def norm3(k, st, targets, rstd_ready, signal):
                dve.wait_ge(S[rstd_ready], k + 1)
                for s in range(3):
                    v.tensor_scalar(targets[s], h_tile(3 * k + s), mv[st][:, 2 * s:2 * s + 1],
                                    rstd[st][:, s:s + 1], ALU.subtract, ALU.mult).then_inc(S[signal], 1)

            def masked(i, st):
                for s in range(3):
                    n = 3 * i + s
                    dve.wait_ge(gathered[s], 16 * i + 16)
                    row = A[:, bass.ds(n * D + OH + PT * D, 64)]
                    v.tensor_scalar(e_sb[3 * st + s][:, 0:64], row, mk[:, bass.ds(n + TT, 1)], None, ALU.mult)
                    v.tensor_scalar(e_sb[3 * st + s][:, 64:128], row, mk[:, bass.ds(n + 2 * TT, 1)], None, ALU.mult)\
                        .then_inc(S["e_ready"], 1)

            masked(0, 0)
            masked(1, 1)
            with dve.Fori(0, PT // 6) as i:
                for st in range(2):
                    k = 2 * i + st
                    dve.wait_ge(S["h_patch"], 3 * k + 3)
                    stats3(k, st, Link(dve, S["ln1_step"], 3 * k), "var1_ready")
                for st in range(2):
                    k = 2 * i + st
                    norm3(k, st, [x_tile(3 * k + s) for s in range(3)], "rstd1_ready", "xn_ready")

            def text3(i, st):
                dve.wait_ge(S["text_done"], i + 1)
                link = Link(dve, S["h_text"], 6 * i)
                for s in range(3):
                    n = 3 * i + s
                    src = text_psum(st, s)
                    link.add(v.scalar_tensor_tensor(out=h_tile(PT + n), in0=h_tile(PT + n), scalar=mk[:, bass.ds(n, 1)],
                                                    in1=src, op0=ALU.mult, op1=ALU.add))
                link.sync()
                stats3(PT // 3 + i, st, link, "var1_ready")

            def text_norm(i, st):
                norm3(PT // 3 + i, st, [x_tile(PT + 3 * i + s) for s in range(3)], "rstd1_ready", "xn_ready")

            def text_psum(st, s):
                return bank(2 + 2 * st, D, D * s) if s < 2 else bank(3 + 2 * st, D)

            n3 = TT // 3
            with dve.Fori(0, (n3 - 3) // 2) as i:
                for st in range(2):
                    text3(2 * i + st, st)
                    masked(2 * i + st + 2, st)
                for st in range(2):
                    text_norm(2 * i + st, st)
            text3(n3 - 3, 0)
            masked(n3 - 1, 0)
            text3(n3 - 2, 1)
            text_norm(n3 - 3, 0)
            text_norm(n3 - 2, 1)
            text3(n3 - 1, 0)
            text_norm(n3 - 1, 0)

            for n in range(32):
                dve.wait_ge(S["silu_done"], n + 1)
                hv = H3[:, :, 8 * n:8 * n + 8]
                v.tensor_tensor(hv, hv, silu_sb[n % 3].rearrange("p (e b) -> p b e", b=TILES), ALU.add)\
                    .then_inc(S["h1_ready"], 1)
            dve.wait_ge(S["h1_ready"], 32)

            def ring_stats(k, st):
                stats3(k, st, Link(dve, S["ln2_step"], 3 * k), "var2_ready")

            def ring_norm(k, st):
                norm3(k, st, xr_sb[3 * st:3 * st + 3], "rstd2_ready", "xr_ready")

            def ring_free(k):
                dve.wait_ge(S["row_kept"], 3 * k - 3)
                dve.wait_ge(S["xT_psum"], k - 1)

            for st in range(2):
                ring_stats(st, st)
            for st in range(2):
                ring_norm(st, st)
            with dve.Fori(1, TILES // 6) as i:
                for st in range(2):
                    ring_stats(2 * i + st, st)
                for st in range(2):
                    ring_free(2 * i + st)
                    ring_norm(2 * i + st, st)
            ring_stats(TILES // 3 - 1, 0)
            ring_free(TILES // 3 - 1)
            ring_norm(TILES // 3 - 1, 0)

            def j3(a):
                return a.rearrange("p (j e) -> p j e", e=E)

            def per_tile(a):
                return a.unsqueeze(2).broadcast_to((P, TILES, E))

            def per_expert(a):
                return a.unsqueeze(1).broadcast_to((P, TILES, E))

            g = Link(dve, S["gate_step"])
            dve.wait_ge(S["gate_const_loaded"], 16 * 10)
            dve.wait_ge(S["gate_done"], TILES // 3)
            logits = bank(7, GE)
            g.add(v.memset(zero57, 0.0))
            g(v.tensor_reduce(mx, j3(logits), AX.X, ALU.max))
            v.tensor_tensor(j3(g_log), j3(logits), per_tile(mx), ALU.subtract).then_inc(S["exp_in"], 1)
            dve.wait_ge(S["exp_out"], 1)
            g(v.tensor_reduce(sm, j3(g_ex), AX.X, ALU.add))
            g(v.reciprocal(sm, sm))
            g(v.tensor_tensor(j3(g_ex), j3(g_ex), per_tile(sm), ALU.mult))

            def first_max(scores, sel):
                g(v.tensor_reduce(mx, j3(scores), AX.X, ALU.max))
                g(v.tensor_tensor(j3(g_t), j3(scores), per_tile(mx), ALU.is_equal))
                g(v.tensor_tensor(j3(g_t), j3(g_t), per_expert(rev_sb[:, :]), ALU.mult))
                g(v.tensor_reduce(mx, j3(g_t), AX.X, ALU.max))
                g(v.tensor_tensor(j3(sel), j3(g_t), per_tile(mx), ALU.is_equal))

            first_max(g_ex, sel1)
            g(v.scalar_tensor_tensor(out=g_log, in0=sel1, scalar=-2.0, in1=g_ex, op0=ALU.mult, op1=ALU.add))
            first_max(g_log, sel2)
            g(v.tensor_tensor(selS, sel1, sel2, ALU.add))
            dve.sem_inc(S["sel_ready"], 1)
            g.add(v.tensor_tensor(X3[:, :, C_CW:C_CW + E], j3(g_ex), j3(selS), ALU.mult))
            g(v.tensor_copy(XI3[:, :, C_ID:C_ID + 1], tokid_sb[:, :].unsqueeze(2)))
            dve.wait_ge(S["ranks_done"], 1)
            g(v.tensor_copy(cnt, bank(1, GE)))
            for e in range(E):
                g.add(v.tensor_tensor_scan(j3(incl)[:, :, e], j3(cnt)[:, :, e], zero57, 0.0, ALU.add, ALU.add))
            g.sync()
            g(v.tensor_copy(tot, j3(incl)[:, TILES - 1, :]))
            g(v.tensor_tensor(incl, incl, cnt, ALU.subtract))
            g.add(v.memset(z8, 0.0))
            g(v.tensor_scalar(pdi, tot, float(P - 1), None, ALU.add))
            g(v.tensor_scalar(pdj, pdi, 7, 7, ALU.arith_shift_right, ALU.logical_shift_left))
            g(v.tensor_copy(pd, pdj))
            g(v.tensor_tensor_scan(inc8, pd, z8, 0.0, ALU.add, ALU.add))
            g(v.tensor_tensor(off, inc8, pd, ALU.subtract))
            g(v.tensor_tensor(posf, bank(0, GE), incl, ALU.add))
            g(v.tensor_tensor(j3(posf), j3(posf), per_expert(off), ALU.add))
            g.add(v.tensor_tensor(g_t, posf, sel1, ALU.mult))
            g(v.tensor_tensor(g_log, posf, sel2, ALU.mult))
            g.add(v.tensor_reduce(pfa, j3(g_t), AX.X, ALU.add))
            g(v.tensor_reduce(pfb, j3(g_log), AX.X, ALU.add))
            g.add(v.tensor_copy(posA[:, :], pfa))
            g(v.tensor_copy(posB[:, :], pfb))
            g(v.tensor_tensor(padn, pd, tot, ALU.subtract))
            g.add(v.tensor_scalar(pm, padn, pcol_sb[:, 0:1], None, ALU.is_gt))
            g(v.tensor_tensor(ppf, off, tot, ALU.add))
            g(v.scalar_tensor_tensor(out=ppf, in0=ppf, scalar=pcol_sb[:, 0:1], in1=trash_sb[:, :],
                                     op0=ALU.add, op1=ALU.subtract))
            g(v.tensor_tensor(ppf, ppf, pm, ALU.mult))
            g(v.tensor_tensor(ppf, ppf, trash_sb[:, :], ALU.add))
            g(v.tensor_copy(padpos[:, :], ppf))
            dve.sem_inc(S["pos_ready"], 1)
            g(v.tensor_scalar(t_exp[:, :], kcol_sb[:, :], inc8[:, 0:1], None, ALU.is_ge))
            for e in range(1, E - 1):
                g(v.scalar_tensor_tensor(out=t_exp[:, :], in0=kcol_sb[:, :], scalar=inc8[:, e:e + 1],
                                         in1=t_exp[:, :], op0=ALU.is_ge, op1=ALU.add))
            g(v.tensor_copy(t_expi[:, :], t_exp[:, :]))
            dve.sem_inc(S["meta_ready"], 1)

            dve.sem_inc(S["w1_free"], 1)
            dve.sem_inc(S["w2_free"], 1)
            with dve.Fori(0, E) as e:
                for st, o in (("w1", 0), ("w2", 1)):
                    dve.wait_ge(S[f"{st}_hi"], e + 1)
                    v.scalar_tensor_tensor(out=A16[:, bass.ds(e * 8192 + o * 4096 + 2048, 2048)], in0=stage[o],
                                           scalar=WSCALE, in1=A16[:, bass.ds(e * 8192 + o * 4096, 2048)],
                                           op0=ALU.mult, op1=ALU.subtract).then_inc(S[f"{st}_free"], 1)
            dve.wait_ge(S["w1_free"], E + 1)
            dve.wait_ge(S["w2_free"], E + 1)
            dve.wait_ge(S["b2_loaded"], 16)
            b = Link(dve, S["b2_step"])
            b.add(v.memset(one16, 1.0))
            b(v.tensor_scalar(b2f, b2f, WSCALE, None, ALU.mult))
            b(v.tensor_copy(b2h, b2f))
            b(v.tensor_tensor(b2l, b2f, b2h, ALU.subtract))
            b(v.tensor_scalar(b2l, b2l, pcol_sb[0:2, 0:1], None, ALU.mult))
            b(v.tensor_scalar(junk8[0][0:2, 0:1], pcol_sb[0:2, 0:1], -1.0, 1.0, ALU.mult, ALU.add))
            b(v.scalar_tensor_tensor(out=b2r, in0=b2h, scalar=junk8[0][0:2, 0:1], in1=b2l, op0=ALU.mult, op1=ALU.add))
            dve.sem_inc(S["b2_ready"], 1)

            def split_x(k, s, loaded, free):
                dve.wait_ge(S["xt_done"], k + 1)
                if free is not None:
                    dve.wait_ge(S["mm1_done"], free)
                v.tensor_scalar(xhi[s], bank(s, D), XSCALE, None, ALU.mult).then_inc(S["y_step"], 1)
                dve.wait_ge(slot_loaded[s], loaded)
                dve.wait_ge(S["slot_free"], k + 1)
                v.scalar_tensor_tensor(out=junk8[s][:, :], in0=iota_sb[:, :], scalar=t_exp[:, bass.ds(k, 1)],
                                       in1=xs[s][:, C_CW:C_CW + E], op0=ALU.is_equal, op1=ALU.mult,
                                       accum_out=meta_cw[:, bass.ds(k, 1)])
                v.tensor_copy(meta_id[:, bass.ds(k, 1)], xsI[s][:, C_ID:C_ID + 1]).then_inc(S["slot_free"], 1)
                dve.wait_ge(S["y_step"], k + 1)
                v.scalar_tensor_tensor(out=xlo[s], in0=bank(s, D), scalar=XSCALE, in1=xhi[s], op0=ALU.mult,
                                       op1=ALU.subtract).then_inc(S["x_split"], 1)

            def split_h(k, s, free):
                dve.wait_ge(S["gelu_done"], 8 * k + 8)
                if free is not None:
                    dve.wait_ge(S["mm2_done"], free)
                v.tensor_copy(hhi[s], hg[s]).then_inc(S["meta_step"], 1)
                dve.wait_ge(S["meta_step"], k + 1)
                v.tensor_tensor(hlo[s], hg[s], hhi[s], ALU.subtract).then_inc(S["h_split"], 1)

            def scale_y(k, s, free):
                dve.wait_ge(S["mm2_done"], k + 1)
                dve.wait_ge(S["slot_free"], k + 3)
                if free is not None:
                    dve.wait_ge(added[s], free)
                v.tensor_scalar(ys[s], bank(6 + s, D), meta_cw[:, bass.ds(k, 1)], 1.0 / WSCALE, ALU.mult, ALU.mult)
                v.tensor_copy(rid[s][:, :], meta_id[:, bass.ds(k, 1)]).then_inc(S["y_done"], 1)

            dve.sem_inc(S["slot_free"], 2)
            split_x(0, 0, 16, None)
            split_x(1, 1, 16, None)
            split_h(0, 0, None)
            def step(k, s, half, first):
                split_x(k + 2, s, 16 * half + 32, 2 * k + 2)
                split_h(k + 1, 1 - s, None if first and s == 0 else k)
                scale_y(k, s, None if first else 16 * half)

            step(0, 0, 0, True)
            step(1, 1, 0, True)
            with dve.Fori(1, (NT - 3) // 2) as i:
                step(2 * i, 0, i, False)
                step(2 * i + 1, 1, i, False)
            k = NT - 3
            step(k, 0, k // 2, False)
            split_h(k + 2, 0, k + 1)
            scale_y(k + 1, 1, 16 * (k // 2))
            scale_y(k + 2, 0, 16 * (k // 2) + 16)

        @block.tensor
        def _(pe):
            t = nc.tensor
            pe.wait_ge(S["patch_const_loaded"], 16 * N_PC)

            def patch(j, s, loaded):
                pe.wait_ge(patch_loaded[s], loaded)
                for c in range(KC):
                    t.matmul(bank(s, D), xP_sb[s][:, P * c:P * (c + 1)], Wp_sb[:, c, :], start=c == 0, stop=False)
                t.matmul(bank(s, D), psel[:, :], pos_sb[:, bass.ds(j * D, D)], start=False, stop=True)\
                    .then_inc(S["patch_done"], 1)

            patch(0, 0, 16)
            patch(1, 1, 16)
            with pe.Fori(1, PT // 2) as i:
                for s in range(2):
                    pe.wait_ge(S["h_patch"], 2 * i + s - 1)
                    patch(2 * i + s, s, 16 * i + 16)
            pe.wait_ge(S["const_loaded"], 48)
            pe.wait_ge(S["kf_ready"], 1)
            t.transpose(PS[0:KROWS, 1024:1024 + P], KF[:, 0, :], ident[:, :])
            t.transpose(PS[0:KROWS, 1024 + P:1024 + 2 * P], KF[:, 1, :], ident[:, :]).then_inc(S["kfT_psum"], 1)
            pe.wait_ge(S["kfT_ready"], 1)
            for n in range(L // 2):
                if n >= 4:
                    pe.wait_ge(S["toep_ready"], n - 3)
                for u in range(2):
                    tt = 2 * n + u
                    o = 512 * (4 + n % 4) + D * u
                    for q in (0, 64):
                        last = t.matmul(PS[q:q + 64, o:o + D], basis_sb[:, L - 1 - tt:2 * L - 1 - tt], kfT,
                                        start=True, stop=True)
                last.then_inc(S["toep_done"], 1)

            def turn(i, st):
                pe.wait_ge(S["e_ready"], 3 * i + 3)
                for s in range(3):
                    last = t.transpose(bank(st, P, P * s), e_sb[3 * st + s], ident[:, :])
                last.then_inc(S["eT_psum"], 1)

            def project(i, st, first):
                pe.wait_ge(S["eT_ready"], i + 1)
                for s in range(3):
                    dst = bank(2 + 2 * st, D, D * s) if s < 2 else bank(3 + 2 * st, D)
                    cls = first and s == 0
                    last = t.matmul(dst, eT[:, 3 * P * st + P * s:3 * P * st + P * (s + 1)], P12_sb[:, :],
                                    start=True, stop=not cls)
                    if cls:
                        t.matmul(dst, csel[:, :], crow[:, :], start=False, stop=True)
                last.then_inc(S["text_done"], 1)

            pe.wait_ge(S["toep_ready"], L // 2)
            pe.wait_ge(S["h_patch"], PT)
            turn(0, 0)
            turn(1, 1)
            project(0, 0, True)
            turn(2, 0)
            project(1, 1, False)
            with pe.Fori(1, (TT // 3 - 1) // 2) as i:
                for st in range(2):
                    k = 2 * i + st
                    turn(k + 1, 1 - st)
                    pe.wait_ge(S["h_text"], 6 * k - 9)
                    project(k, st, False)
            pe.wait_ge(S["h_text"], 6 * (TT // 3 - 1) - 9)
            project(TT // 3 - 1, 0, False)

            pe.wait_ge(S["xn_ready"], TILES)
            for n in range(32):
                if n >= 4:
                    pe.wait_ge(S["silu_done"], n - 3)
                for c in range(8):
                    ch = 8 * n + c
                    for q in (0, 64):
                        last = t.matmul(PS[q:q + 64, 512 * (4 + n % 4) + TILES * c:512 * (4 + n % 4) + TILES * (c + 1)],
                                        Tz[q:q + 64, :, ch],
                                        X3[q:q + 64, :, ch], start=True, stop=True)
                last.then_inc(S["conv_done"], 1)

            def turn_rows(i, st):
                pe.wait_ge(S["xr_ready"], 3 * i + 3)
                for s in range(3):
                    for c in range(2):
                        o = (2 * s + c) * P
                        last = t.transpose(bank(2 * st + o // 512, P, o % 512), xr_sb[3 * st + s][:, P * c:P * (c + 1)],
                                           ident[:, :])
                last.then_inc(S["xT_psum"], 1)

            def gate(i, st):
                pe.wait_ge(S["xT_ready"], i + 1)
                for s in range(3):
                    for c in range(2):
                        last = t.matmul(PS[:, bass.ds((3 * i + s) * E + 7 * 512, E)],
                                        xT_sb[st][:, (2 * s + c) * P:(2 * s + c + 1) * P],
                                        wg_sb[:, E * c:E * (c + 1)], start=c == 0, stop=c == 1)
                last.then_inc(S["gate_done"], 1)

            pe.wait_ge(S["gate_const_loaded"], 160)
            pe.wait_ge(S["silu_done"], 32)
            turn_rows(0, 0)
            with pe.Fori(0, TILES // 6) as i:
                turn_rows(2 * i + 1, 1)
                gate(2 * i, 0)
                turn_rows(2 * i + 2, 0)
                gate(2 * i + 1, 1)
            gate(TILES // 3 - 1, 0)
            pe.wait_ge(S["sel_ready"], 1)
            t.matmul(bank(0, GE), tri[:, :], selS, start=True, stop=True)
            t.matmul(bank(1, GE), ones[:, :], selS, start=True, stop=True).then_inc(S["ranks_done"], 1)

            def turn_x(k, s, loaded, free):
                pe.wait_ge(slot_loaded[s], loaded)
                if free is not None:
                    pe.wait_ge(S["x_split"], free)
                for c in range(2):
                    last = t.transpose(bank(s, P, P * c), xs[s][:, P * c:P * (c + 1)], ident[:, :])
                last.then_inc(S["xt_done"], 1)

            def expert_of(k):
                return pe.value_load(t_expi[0:1, bass.ds(k, 1)], min_val=0, max_val=E - 1)

            def w1_product(k, s, free):
                e = expert_of(k)
                pe.wait_ge(S["x_split"], k + 1)
                if free is not None:
                    pe.wait_ge(S["gelu_done"], free)
                for f in range(FCH):
                    dst = bank(2 + 2 * s + f // 4, P, P * (f % 4))
                    for c in range(2):
                        hi = A16[:, bass.ds(e * 8192 + (c * HID + f * P), P)]
                        lo = A16[:, bass.ds(e * 8192 + (2048 + c * HID + f * P), P)]
                        t.matmul(dst, hi, xhi[s][:, P * c:P * (c + 1)], start=c == 0, stop=False)
                        t.matmul(dst, hi, xlo[s][:, P * c:P * (c + 1)], start=False, stop=False)
                        last = t.matmul(dst, lo, xhi[s][:, P * c:P * (c + 1)], start=False, stop=c == 1)
                    if f % 4 == 3:
                        last.then_inc(S["mm1_done"], 1)

            def w2_product(k, s, free):
                e = expert_of(k)
                pe.wait_ge(S["h_split"], k + 1)
                if free is not None:
                    pe.wait_ge(S["y_done"], free)
                dst = bank(6 + s, D)
                for f in range(FCH):
                    hi = A16[:, bass.ds(e * 8192 + (4096 + f * D), D)]
                    lo = A16[:, bass.ds(e * 8192 + (6144 + f * D), D)]
                    t.matmul(dst, hhi[s][:, P * f:P * (f + 1)], hi, start=f == 0, stop=False)
                    t.matmul(dst, hhi[s][:, P * f:P * (f + 1)], lo, start=False, stop=False)
                    t.matmul(dst, hlo[s][:, P * f:P * (f + 1)], hi, start=False, stop=False)
                t.matmul(dst, one16, A16[0:2, bass.ds(e * D + (2 * b2p_at + E * D), D)], start=False, stop=True)\
                    .then_inc(S["mm2_done"], 1)

            pe.wait_ge(S["pos_ready"], 1)
            pe.wait_ge(S["meta_ready"], 1)
            pe.wait_ge(S["b2_ready"], 1)
            turn_x(0, 0, 16, None)
            turn_x(1, 1, 16, None)
            w1_product(0, 0, None)

            def step(k, s, half, first):
                w1_product(k + 1, 1 - s, None if first and s == 0 else 8 * k)
                turn_x(k + 2, s, 16 * half + 32, k + 1)
                w2_product(k, s, None if first else k - 1)

            step(0, 0, 0, True)
            step(1, 1, 0, True)
            with pe.Fori(1, (NT - 3) // 2) as i:
                step(2 * i, 0, i, False)
                step(2 * i + 1, 1, i, False)
            k = NT - 3
            step(k, 0, k // 2, False)
            w1_product(k + 2, 0, 8 * (k + 1))
            w2_product(k + 1, 1, k)
            w2_product(k + 2, 0, k + 1)


def kernel(**inputs):
    import numpy as np
    import concourse.bacc as bacc
    from concourse.bass_utils import run_bass_kernel_spmd as run

    I = {k: np.asarray(v) for k, v in inputs.items()}
    f = np.float32
    half = np.arange(P) // 64
    t_of = np.arange(P) % 64
    arr = {}
    x = I["x"].reshape(L, 3, 6, 16, 6, 16).transpose(2, 4, 0, 1, 3, 5).reshape(2, PT, L, KC, P)
    arr["xP"] = x.transpose(1, 4, 3, 0, 2).reshape(PT * P, KC * P)
    arr["Wp"] = I["L0_tok_W"].T.reshape(KC, P, D).transpose(1, 0, 2).reshape(P, KC * D)
    pos = I["L0_tok_pos_embed"][0]
    arr["posrows"] = np.stack([pos[1:1 + PT].reshape(-1), pos[1 + PT:1 + 2 * PT].reshape(-1), np.tile(I["L0_tok_b"], PT)])
    arr["patsel"] = np.stack([half == 0, half == 1, half >= 0]).astype(f)
    arr["clssel"] = np.stack([half == 0, half == 0]).astype(f)
    arr["clsrows"] = np.stack([I["L0_tok_cls_token"][0, 0], pos[0]])
    txt = I["x_txt"]
    ids = np.full((P, TT), 127999, np.int32)
    ids[:64, 1:] = txt[:, :TT - 1]
    ids[64:, :] = txt[:, TT - 1:]
    arr["ids"] = ids
    table = np.zeros((VOCAB, D), f)
    table[:CUT0] = I["L0_txt_emb0"]
    table[CUT0:CUT1, :64] = I["L0_txt_emb1"]
    table[CUT1:, :64] = I["L0_txt_emb2"]
    arr["table"] = table
    arr["P12"] = np.concatenate([I["L0_txt_proj1"].T, I["L0_txt_proj2"].T], 0)
    parts = [I["L0_attn_log_dt"], I["L0_attn_inv_w_real"], I["L0_attn_w_imaginary"], I["L0_attn_B"].reshape(D, -1),
             I["L0_attn_P"].reshape(D, -1), I["L0_attn_C"].reshape(D, -1), I["L0_attn_D"].reshape(D, 1)]
    arr["prm"] = np.concatenate(parts, 1).reshape(2, P, PRM).transpose(1, 0, 2).reshape(P, 2, PRM)
    th = 2 * np.pi * np.arange(M) / L
    om = np.cos(th) - 1j * np.sin(th)
    om[-1] = -1.0
    arr["zc"] = np.tile(np.concatenate([2 * (1 - om).real, 2 * (1 - om).imag, (1 + om).real, (1 + om).imag])[None], (P, 1)).astype(f)
    lag = L - 1 - np.arange(2 * L - 1)
    w = np.where((np.arange(M) == 0) | (np.arange(M) == M - 1), 1.0, 2.0) * 2.0 / L
    ph = np.outer(np.arange(M), lag) * 2 * np.pi / L
    sn = -w[:, None] * np.sin(ph)
    sn[0] = sn[-1] = 0
    bas = np.concatenate([w[:, None] * np.cos(ph), sn, (lag == 0)[None] * 1.0], 0) * (lag >= 0)
    arr["basis"] = bas.astype(f)
    arr["ident_d"] = np.eye(P, dtype=f)
    arr["tri_d"] = np.triu(np.ones((P, P), f), 1)
    arr["tokid"] = (np.arange(P)[:, None] + P * np.arange(TILES)[None]).astype(np.int32)
    arr["dumid"] = (TOKENS + np.arange(P))[:, None].astype(np.int32)
    arr["wg"] = I["L0_ffn_w_gate"].T.reshape(2, P, E).transpose(1, 0, 2).reshape(P, 2 * E)
    w1 = I["L0_ffn_W1"].reshape(E, 2, P, HID).transpose(0, 2, 1, 3).reshape(E, P, 2048)
    w2 = I["L0_ffn_W2"].reshape(E, FCH, P, D).transpose(0, 2, 1, 3).reshape(E, P, 2048)
    arr["wts"] = np.stack([w1, w2], 1).reshape(E * 2 * P, 2048)
    arr["b1T"] = I["L0_ffn_b1"].reshape(E, FCH, P).transpose(2, 0, 1).reshape(P, E * FCH)
    arr["b2d"] = np.tile(I["L0_ffn_b2"].reshape(1, E * D), (2, 1))
    arr["iota8"] = np.tile(np.arange(E, dtype=f)[None], (P, 1))
    arr["rev8"] = np.tile((E - np.arange(E, dtype=f))[None], (P, 1))
    arr["pcol"] = np.arange(P, dtype=f)[:, None]
    arr["trash"] = (SLOTS + P * np.arange(E)[None] + np.arange(P)[:, None]).astype(f)
    arr["kcol"] = np.tile((P * np.arange(NT, dtype=f))[None], (P, 1))

    nc = bacc.Bacc("TRN2", target_bir_lowering=False, num_devices=1)
    args, feed = [], {}
    for name, a in arr.items():
        a = np.ascontiguousarray(a)
        feed[f"in_{name}"] = a
        args.append(nc.dram_tensor(f"in_{name}", a.shape, mybir.dt.from_np(a.dtype), kind="ExternalInput").ap())
    args.append(nc.dram_tensor("out_rows", (TOKENS + P, D), F32, kind="ExternalOutput").ap())
    build(nc, *args)
    r = run(nc, [feed], core_ids=[0])
    got = r.results[0]["out_rows"][:TOKENS].reshape(TILES, 2, L, D)
    out = np.empty((L, NCOL, D), f)
    out[:, 1:1 + PT] = got[:PT, 0].transpose(1, 0, 2)
    out[:, 1 + PT:1 + 2 * PT] = got[:PT, 1].transpose(1, 0, 2)
    out[:, 0] = got[PT, 0]
    out[:, 1 + 2 * PT:2 * PT + TT] = got[PT + 1:, 0].transpose(1, 0, 2)
    out[:, 2 * PT + TT:] = got[PT:, 1].transpose(1, 0, 2)
    return out
```

```python
import concourse.bass as bass
from concourse import mybir
from contextlib import ExitStack

F32 = mybir.dt.float32
F16 = mybir.dt.float16
I32 = mybir.dt.int32
ACT = mybir.ActivationFunctionType
ALU = mybir.AluOpType
AX = mybir.AxisListType

P = 128
L, NCOL, D = 64, 114, 256
TILES, PT = L * NCOL // P, 18
TT = TILES - PT
KC = 6
NS, M = 16, L // 2 + 1
KROWS = 2 * M + 1
E, HID = 8, 1024
FCH = HID // P
SUB = 2
NT = 2 * TILES // SUB + E - 1
COLS = NT * SUB
TOKENS = TILES * P
POOL_EXPERTS = 5
WSCALE = 64.0
XSCALE = 64.0
VOCAB, CUT0, CUT1 = 32000, 5000, 15000
EPS = 1e-5
PRM = 3 * 2 * NS + 2 * NS + 2

OT, OH = 0, L * D
OX = OH + TILES * D
ARENA = OX + TILES * D
WEXP = 4 * 2048 // 2
WORK = E * WEXP


class Link:

    def __init__(self, eng, sem, base=0):
        self.eng, self.sem, self.base, self.n = eng, sem, base, 0

    def add(self, ins):
        ins.then_inc(self.sem, 1)
        self.n += 1

    def sync(self):
        self.eng.wait_ge(self.sem, self.base + self.n)

    def __call__(self, ins):
        self.add(ins)
        self.sync()


def build(nc, xP, Wp, posrows, patsel, clssel, clsrows, ids, table, P12, prm, zc, basis, ident_d, tri_d,
          iota16_d, jcol, wg, wts, b1T, b2d, iota8, rev8, pcol, kcol, out):
    rows = nc.dram_tensor("rows", (TOKENS + P, D), F32, kind="Internal").ap()
    cws = nc.dram_tensor("cws", (TOKENS + P, E), F32, kind="Internal").ap()
    ctx = ExitStack()
    with ctx:
        def sb(name, shape, dt=F32):
            return ctx.enter_context(nc.sbuf_tensor(name, shape, dt))

        def sem(name):
            return ctx.enter_context(nc.semaphore(name))

        A = sb("arena", [P, ARENA])
        A16 = A[:, :].bitcast(F16)
        AI = A[:, :].bitcast(I32)
        Tz = A[:, OT:OH].rearrange("p (t h) -> p t h", h=D)
        H3 = A[:, OH:OX].rearrange("p (j d) -> p j d", d=D)
        X3 = A[:, OX:ARENA].rearrange("p (j r) -> p j r", r=D)

        def h_tile(j):
            return A[:, bass.ds(j * D + OH, D)]

        def x_tile(j):
            return A[:, bass.ds(j * D + OX, D)]

        taken = [OT]

        def scratch(n):
            taken[0] += n
            assert taken[0] <= OH
            return A[:, taken[0] - n:taken[0]]

        pos_sb = scratch(PT * D)[0:3, :]
        prm_sb = scratch(2 * PRM).rearrange("p (c k) -> p c k", k=PRM)
        zc_sb = scratch(4 * M)
        KF = scratch(2 * KROWS).rearrange("p (c k) -> p c k", k=KROWS)
        big = [scratch(2 * M * NS) for _ in range(6)]
        vec = [scratch(2 * NS) for _ in range(16)]
        frq = [scratch(2 * M) for _ in range(20)]
        psel = scratch(P)[0:3, :]
        ids_f, idx_f, mk0, mk1, mk2, mtmp = [scratch(TT) for _ in range(6)]

        B = sb("ring_arena", [P, 4096])
        Wp_sb = B[:, 0:KC * D].rearrange("p (k d) -> p k d", d=D)
        xP_sb = [B[:, 1536 + 768 * s:1536 + 768 * (s + 1)] for s in range(2)]
        e_sb = [B[:, 3072 + P * s:3072 + P * (s + 1)] for s in range(6)]
        kfT = B[0:KROWS, 0:D]
        eT = B[:, 1536:1536 + 6 * P]
        silu_sb = [B[:, 512 * s:512 * s + 8 * TILES] for s in range(3)]
        stage = [B[:, 2048 * s:2048 * (s + 1)] for s in range(2)]

        ident = sb("ident", [P, P])
        tri = sb("tri", [P, P])
        ones = sb("ones", [P, P])
        basis_sb = sb("basis_sb", [KROWS, 2 * L - 1])
        P12_sb = sb("P12_sb", [P, D])
        csel = sb("csel", [2, P])
        crow = sb("crow", [2, D])
        ids_sb = sb("ids_sb", [P, TT], I32)
        idx = sb("idx", [P, TT], I32)
        mk = sb("mk", [P, 3 * TT])
        stats = [sb(f"stats{s}", [P, 18]) for s in range(3)]
        mv = [sb(f"mv{s}", [P, 6]) for s in range(3)]
        veps = [sb(f"veps{s}", [P, 3]) for s in range(3)]
        eps3 = sb("eps3", [P, 3])
        expo = sb("expo", [P, 3])
        rstd = [sb(f"rstd{s}", [P, 3]) for s in range(3)]
        mv2 = sb("mv_all", [P, 2 * TILES])
        std2 = sb("std_all", [P, TILES])
        eps1 = sb("eps1", [P, 1])
        wg_sb = sb("wg_sb", [P, 2 * E])
        b1_sb = sb("b1_sb", [P, E * FCH])
        iota_sb = sb("iota_sb", [P, E])
        rev_sb = sb("rev_sb", [P, E])
        pcol_sb = sb("pcol_sb", [P, 1])
        iota16 = sb("iota16", [P, P], F16)
        jcol_sb = sb("jcol_sb", [P, TILES])
        kcol_sb = sb("kcol_sb", [P, NT])
        zero_row = sb("zero_row", [P, D])
        t_exp = sb("t_exp", [P, NT])
        t_expi = sb("t_expi", [P, NT], I32)
        sid = sb("sid", [P, COLS], I32)
        meta_cw = sb("meta_cw", [P, COLS])
        junk8 = [sb(f"junk8_{s}", [P, SUB * E]) for s in range(2)]
        gid = [sb(f"gid{s}", [P, SUB], I32) for s in range(2)]
        aid = [sb(f"aid{s}", [P, SUB], I32) for s in range(2)]

        XT = 3 * WEXP
        xT_sb = [A[:, XT + 768 * s:XT + 768 * (s + 1)] for s in range(2)]
        GE = TILES * E
        GS = 6 * WEXP
        g_log, g_ex, sel1, sel2, selS, g_t, cnt, incl, posf = [
            A[:, GS + GE * n:GS + GE * (n + 1)] for n in range(9)]
        gat = [GS + GE * 9]

        def gs(n):
            gat[0] += n
            assert gat[0] <= OX
            return A[:, gat[0] - n:gat[0]]

        zero57, mx, sm, pfa, pfb, loA, loB, hiA, hiB = [gs(TILES) for _ in range(9)]
        tot, pd, inc8, off, z8 = [gs(E) for _ in range(5)]
        pdi, pdj = [gs(E).bitcast(I32) for _ in range(2)]
        pint, lint = [gs(TILES).bitcast(I32) for _ in range(2)]
        pcol1 = gs(1)
        v1, v2, vz = [gs(P) for _ in range(3)]
        oh_lo = [gs(P // 2).bitcast(F16) for _ in range(4)]
        oh_hi = [gs(P).bitcast(F16) for _ in range(4)]

        at = [WORK]

        def work(n):
            at[0] += n
            assert at[0] <= ARENA
            return at[0] - n

        xs = [A[:, a:a + SUB * D] for a in (work(SUB * D), work(SUB * D))]
        xh_at = [work(SUB * D) for _ in range(2)]
        xhi = [A16[:, 2 * a:2 * a + SUB * D] for a in xh_at]
        xlo = [A16[:, 2 * a + SUB * D:2 * a + 2 * SUB * D] for a in xh_at]
        hg_at = work(SUB * HID)
        hg = [A[:, hg_at + 512 * q:hg_at + 512 * (q + 1)] for q in range(4)]
        hh_at = [work(SUB * HID) for _ in range(2)]
        hhi = [A16[:, 2 * a:2 * a + SUB * HID] for a in hh_at]
        hlo = [A16[:, 2 * a + SUB * HID:2 * a + 2 * SUB * HID] for a in hh_at]
        ys = [A[:, a:a + SUB * D] for a in (work(SUB * D), work(SUB * D))]
        b2p_at = work(E * D)
        b2h = A16[0:2, 2 * b2p_at:2 * b2p_at + E * D]
        b2r = A16[0:2, 2 * b2p_at + E * D:2 * b2p_at + 2 * E * D]
        b2f = A[0:2, hh_at[0]:hh_at[0] + E * D]
        b2l = A[0:2, hh_at[1]:hh_at[1] + E * D]
        cwg = [A[:, a:a + SUB * E] for a in (work(SUB * E), work(SUB * E))]
        one16_at = work(P // 2)
        one16 = A16[0:2, 2 * one16_at:2 * one16_at + P]

        PS = ctx.enter_context(nc.psum_tensor("PS", [P, 8 * 512], F32))

        def bank(b, n=512, o=0):
            return PS[:, 512 * b + o:512 * b + o + n]

        names = """const_loaded patch_const_loaded s4_loaded ids_loaded gate_const_loaded
            patch_done h_patch kf_ready kfT_psum kfT_ready toep_done toep_ready toep_copied s4_step
            idx_ready e_ready eT_psum eT_ready text_done h_text ln1_step lnp_step xn_ready text_step
            conv_done silu_done h1_ready ln2_step var2_ready std2_ready rstd2_ready row_ready
            xT_psum xT_ready gate_done rows_dumped cw_ready cw_dumped ids_done
            exp_in exp_out gate_step sel_ready ranks_done hot_ready hot_used map_done
            prefill_done zero_ready zero_rows slots_ready
            w_hi w_scaled w_free_pool w_free_dve
            b2_loaded b2_step b2_ready xt_done x_split x_hi gelu_done mm1_done h_hi h_split mm2_done y_done
            slot_free gid_ready aid_ready tick tick2 tick3 vart_ready rstdt_ready varp_ready rstdp_ready
            vepst vepsp expo_ready""".split()
        S = {n: sem(n) for n in names}
        patch_loaded = [sem(f"patch_loaded{s}") for s in range(2)]
        gathered = [sem(f"gathered{s}") for s in range(3)]
        w_loaded = [sem(f"w_loaded{s}") for s in range(2)]
        row_gathered = [[sem(f"row_gathered{s}{u}") for u in range(SUB)] for s in range(2)]
        cw_gathered = [[sem(f"cw_gathered{s}{u}") for u in range(SUB)] for s in range(2)]
        added = [sem(f"added{u}") for u in range(SUB)]

        block = ctx.enter_context(nc.Block())

        N_S4, N_PC, N_GC = 2, 5, 9
        GROUPS, PER = 3, TILES // 3
        TRIPLES = TT // 3

        def toeplitz_share(k):
            return range(k * (L // 2) // TRIPLES, (k + 1) * (L // 2) // TRIPLES)

        @block.sync
        def _(sp):
            sp.dma_start(ids_sb[:, :], ids).then_inc(S["ids_loaded"], 16)
            sp.dma_start(prm_sb, prm).then_inc(S["s4_loaded"], 16)
            sp.dma_start(zc_sb, zc).then_inc(S["s4_loaded"], 16)
            sp.dma_start(B[:, 0:KC * D], Wp).then_inc(S["patch_const_loaded"], 16)
            sp.dma_start(pos_sb, posrows).then_inc(S["patch_const_loaded"], 16)
            sp.dma_start(psel, patsel).then_inc(S["patch_const_loaded"], 16)
            sp.dma_start(csel[:, :], clssel).then_inc(S["patch_const_loaded"], 16)
            sp.dma_start(crow[:, :], clsrows).then_inc(S["patch_const_loaded"], 16)
            for s in range(2):
                sp.dma_start(xP_sb[s], xP[s * P:(s + 1) * P, :]).then_inc(patch_loaded[s], 16)
            with sp.Fori(1, PT // 2) as i:
                for s in range(2):
                    sp.wait_ge(S["patch_done"], 2 * i + s - 1)
                    sp.dma_start(xP_sb[s], xP[bass.ds((2 * i + s) * P, P), :]).then_inc(patch_loaded[s], 16)
            sp.wait_ge(S["zero_ready"], 1)
            sp.dma_start(out[TOKENS:TOKENS + P, :], zero_row[:, :]).then_inc(S["zero_rows"], 16)
            sp.dma_start(rows[TOKENS:TOKENS + P, :], zero_row[:, :]).then_inc(S["zero_rows"], 16)
            sp.dma_start(cws[TOKENS:TOKENS + P, :], zero_row[:, 0:E]).then_inc(S["zero_rows"], 16)
            quarter = L * D // 4
            for n in range(4):
                sp.wait_ge(S["toep_ready"], (L // 8) * (n + 1))
                o = OT + quarter * n
                sp.dma_start(A[64:128, o:o + quarter], A[0:64, o:o + quarter]).then_inc(S["toep_copied"], 16)
            sp.wait_ge(S["h1_ready"], 32)

            def load_piece(n):
                if n >= 2:
                    by_pool = n - 2 < 2 * POOL_EXPERTS
                    sp.wait_ge(S["w_free_pool" if by_pool else "w_free_dve"],
                               n - 1 if by_pool else n - 1 - 2 * POOL_EXPERTS)
                sp.dma_start(stage[n % 2], wts[n * P:(n + 1) * P, :]).then_inc(w_loaded[n % 2], 16)

            load_piece(0)
            load_piece(1)
            sp.dma_start(out[0:TOKENS, :].rearrange("(p j) d -> p j d", j=TILES), H3).then_inc(S["prefill_done"], 16)
            rows3 = rows[0:TOKENS, :].rearrange("(p j) d -> p j d", j=TILES)
            for g in range(GROUPS):
                sp.wait_ge(S["row_ready"], PER * (g + 1))
                sp.dma_start(rows3[:, PER * g:PER * (g + 1), :], X3[:, PER * g:PER * (g + 1), :])\
                    .then_inc(S["rows_dumped"], 16)
                load_piece(2 + g)
            sp.wait_ge(S["cw_ready"], 1)
            sp.dma_start(cws[0:TOKENS, :].rearrange("(p j) e -> p (j e)", j=TILES), posf).then_inc(S["cw_dumped"], 16)
            sp.wait_ge(S["rows_dumped"], 16 * GROUPS)
            sp.dma_start(b2f, b2d).then_inc(S["b2_loaded"], 16)
            for n in range(5, 2 * E):
                load_piece(n)

        @block.gpsimd
        def _(pool):
            nc.gpsimd.memset(eps3[:, :], EPS)
            nc.gpsimd.memset(expo[:, :], -0.5).then_inc(S["expo_ready"], 1)
            pool.wait_ge(S["expo_ready"], 1)
            pool.wait_ge(S["idx_ready"], 1)
            for n in range(TT):
                s = n % 3
                if n >= 3:
                    pool.wait_ge(gathered[s], 16 * (n // 3))
                pool.indirect_dma_start(H3[:, PT + n, :], None, table,
                                        bass.IndirectOffsetOnAxis(ap=idx[:, n:n + 1], axis=0)).then_inc(gathered[s], 16)
            def inv_std(k, st, w):
                pool.wait_ge(S[f"var{w}_ready"], k + 1)
                var = mv[st][:, :].rearrange("p (s r) -> p s r", r=2)[:, :, 1]
                nc.gpsimd.tensor_tensor(veps[st][:, :], var, eps3[:, :], ALU.add).then_inc(S[f"veps{w}"], 1)
                pool.wait_ge(S[f"veps{w}"], k + 1)
                nc.gpsimd.tensor_tensor(rstd[st][:, :], veps[st][:, :], expo[:, :], ALU.pow)\
                    .then_inc(S[f"rstd{w}_ready"], 1)

            with pool.Fori(0, TT // 6) as i:
                for st in range(2):
                    inv_std(2 * i + st, st, "t")
                inv_std(i, 2, "p")
            inv_std(TT // 3 - 1, 0, "t")

            for n in range(2 * POOL_EXPERTS):
                pool.wait_ge(S["w_hi"], n + 1)
                o = 8192 * (n // 2) + 4096 * (n % 2)
                nc.gpsimd.tensor_tensor(A16[:, o + 2048:o + 4096], stage[n % 2], A16[:, o:o + 2048], ALU.subtract)\
                    .then_inc(S["w_free_pool"], 1)

            def gather(k, s, free):
                if free is not None:
                    pool.wait_ge(S["slot_free"], free)
                    pool.sem_inc(S["tick2"], 1)
                nc.gpsimd.tensor_copy(gid[s][:, :], sid[:, bass.ds(k * SUB, SUB)]).then_inc(S["gid_ready"], 1)
                pool.wait_ge(S["gid_ready"], k + 1)
                pool.sem_inc(S["tick2"], 1)
                for u in range(SUB):
                    at_ = bass.IndirectOffsetOnAxis(ap=gid[s][:, u:u + 1], axis=0)
                    pool.indirect_dma_start(xs[s][:, D * u:D * (u + 1)], None, rows, at_).then_inc(row_gathered[s][u], 16)
                    pool.indirect_dma_start(cwg[s][:, E * u:E * (u + 1)], None, cws, at_).then_inc(cw_gathered[s][u], 16)

            def add_rows(k, s, before):
                pool.wait_ge(S["y_done"], k + 1)
                if before is not None:
                    pool.wait_ge(added[1], before)
                pool.sem_inc(S["tick2"], 1)
                nc.gpsimd.tensor_copy(aid[s][:, :], sid[:, bass.ds(k * SUB, SUB)]).then_inc(S["aid_ready"], 1)
                pool.wait_ge(S["aid_ready"], k + 1)
                pool.sem_inc(S["tick2"], 1)
                for u in range(SUB):
                    if u:
                        pool.wait_ge(added[0], 16 if before is None else before + 16)
                        pool.sem_inc(S["tick2"], 1)
                    pool.indirect_dma_start(out, bass.IndirectOffsetOnAxis(ap=aid[s][:, u:u + 1], axis=0),
                                            ys[s][:, D * u:D * (u + 1)], None, compute_op=ALU.add).then_inc(added[u], 16)

            pool.wait_ge(S["slots_ready"], 1)
            pool.wait_ge(S["zero_rows"], 48)
            pool.wait_ge(S["rows_dumped"], 16 * GROUPS)
            pool.wait_ge(S["cw_dumped"], 16)
            pool.wait_ge(S["prefill_done"], 16)
            gather(0, 0, None)
            gather(1, 1, None)
            gather(2, 0, 1)
            gather(3, 1, 2)
            add_rows(0, 0, None)
            with pool.Fori(0, NT // 2 - 2) as i:
                for s in range(2):
                    k = 2 * i + s + 1
                    gather(k + 3, s, k + 2)
                    add_rows(k, 1 - s, 16 * k)
            for k in range(NT - 3, NT):
                add_rows(k, k % 2, 16 * k)
            for u in range(SUB):
                pool.wait_ge(added[u], 16 * NT)

        @block.scalar
        def _(act):
            act.dma_start(basis_sb[:, :], basis).then_inc(S["const_loaded"], 16)
            act.dma_start(ident[:, :], ident_d).then_inc(S["const_loaded"], 16)
            act.dma_start(P12_sb[:, :], P12).then_inc(S["const_loaded"], 16)
            for dst, src in ((tri[:, :], tri_d), (wg_sb[:, :], wg), (b1_sb[:, :], b1T), (iota_sb[:, :], iota8),
                             (rev_sb[:, :], rev8), (pcol_sb[:, :], pcol), (iota16[:, :], iota16_d),
                             (jcol_sb[:, :], jcol), (kcol_sb[:, :], kcol)):
                act.dma_start(dst, src).then_inc(S["gate_const_loaded"], 16)
            act.wait_ge(S["s4_loaded"], 16 * N_S4)
            nc.scalar.activation(prm_sb[:, :, 0:1 + NS], prm_sb[:, :, 0:1 + NS], ACT.Exp).then_inc(S["s4_step"], 1)
            with act.Fori(0, PT // 2) as i:
                for s in range(2):
                    act.wait_ge(S["patch_done"], 2 * i + s + 1)
                    nc.scalar.activation(h_tile(2 * i + s), bank(s, D), ACT.Copy).then_inc(S["h_patch"], 1)
            act.wait_ge(S["kfT_psum"], 1)
            nc.scalar.activation(kfT[:, :], PS[0:KROWS, 1024:1024 + D], ACT.Copy).then_inc(S["kfT_ready"], 1)

            def toeplitz_copy(n):
                act.wait_ge(S["toep_done"], n + 1)
                nc.scalar.activation(A[0:64, OT + 512 * n:OT + 512 * (n + 1)], PS[0:64, 512 * (6 + n % 2):512 * (7 + n % 2)],
                                     ACT.Copy).then_inc(S["toep_ready"], 1)

            def text_copy(k):
                act.wait_ge(S["eT_psum"], k + 1)
                if k >= 2:
                    act.wait_ge(S["text_done"], k - 1)
                st = k % 2
                nc.scalar.activation(eT[:, 3 * P * st:3 * P * (st + 1)], bank(st, 3 * P), ACT.Copy)\
                    .then_inc(S["eT_ready"], 1)

            text_copy(0)
            for k in range(TRIPLES):
                if k + 1 < TRIPLES:
                    text_copy(k + 1)
                for n in toeplitz_share(k):
                    toeplitz_copy(n)

            for n in range(32):
                act.wait_ge(S["conv_done"], n + 1)
                if n >= 3:
                    act.wait_ge(S["h1_ready"], n - 2)
                nc.scalar.activation(silu_sb[n % 3], bank(4 + n % 4, 8 * TILES), ACT.Silu)\
                    .then_inc(S["silu_done"], 1)

            def std_group(g):
                act.wait_ge(S["var2_ready"], g + 1)
                var = mv2[:, 2 * PER * g:2 * PER * (g + 1)].rearrange("p (j r) -> p j r", r=2)[:, :, 1]
                nc.scalar.activation(std2[:, PER * g:PER * (g + 1)], var, ACT.Sqrt, bias=eps1[:, :])\
                    .then_inc(S["std2_ready"], 1)

            def gate_copy(k):
                act.wait_ge(S["xT_psum"], k + 1)
                if k >= 2:
                    act.wait_ge(S["gate_done"], k - 1)
                s = k % 2
                nc.scalar.activation(xT_sb[s][:, 0:512], bank(2 * s), ACT.Copy)
                nc.scalar.activation(xT_sb[s][:, 512:768], bank(2 * s + 1, 256), ACT.Copy)\
                    .then_inc(S["xT_ready"], 1)

            def weights_high(n):
                act.wait_ge(w_loaded[n % 2], 16 * (n // 2) + 16)
                o = 8192 * (n // 2) + 4096 * (n % 2)
                if n < 2 * POOL_EXPERTS:
                    nc.scalar.activation(stage[n % 2], stage[n % 2], ACT.Copy, scale=WSCALE).then_inc(S["w_scaled"], 1)
                    act.wait_ge(S["w_scaled"], n + 1)
                    nc.scalar.activation(A16[:, o:o + 2048], stage[n % 2], ACT.Copy).then_inc(S["w_hi"], 1)
                else:
                    nc.scalar.activation(A16[:, o:o + 2048], stage[n % 2], ACT.Copy, scale=WSCALE)\
                        .then_inc(S["w_hi"], 1)

            pieces = 0
            for k in range(TILES // 3):
                if k == 0:
                    std_group(0)
                if k == 1:
                    std_group(1)
                if k == PER // 3:
                    std_group(2)
                gate_copy(k)
                if k % 4 == 3:
                    weights_high(pieces)
                    pieces += 1
            act.wait_ge(S["exp_in"], 1)
            nc.scalar.activation(g_ex, g_log, ACT.Exp).then_inc(S["exp_out"], 1)
            act.wait_ge(S["gate_done"], TILES // 3)
            act.wait_ge(S["prefill_done"], 16)
            for n in range(pieces, 2 * E):
                if n == 12:
                    act.wait_ge(S["slots_ready"], 1)
                    act.wait_ge(S["rows_dumped"], 16 * GROUPS)
                    act.wait_ge(S["cw_dumped"], 16)
                weights_high(n)

            def gelu(k, first):
                e = act.value_load(t_expi[0:1, bass.ds(k, 1)], min_val=0, max_val=E - 1)
                for q in range(4):
                    act.wait_ge(S["mm1_done"], 4 * k + q + 1)
                    if not first:
                        act.wait_ge(S["h_split"], 4 * k + q - 3)
                    for c in range(2):
                        nc.scalar.activation(hg[q][:, 256 * c:256 * (c + 1)], bank(2 + q, 256, 256 * c), ACT.Gelu,
                                             bias=b1_sb[:, bass.ds(e * FCH + (2 * q + c), 1)],
                                             scale=1.0 / (WSCALE * XSCALE)).then_inc(S["gelu_done"], 1)

            gelu(0, True)
            with act.Fori(1, NT) as i:
                gelu(i, False)

        @block.vector
        def _(dve):
            v = nc.vector

            v.memset(ones[:, :], 1.0)
            v.memset(eps1[:, :], EPS)
            v.memset(zero_row[:, :], 0.0).then_inc(S["zero_ready"], 1)
            dve.wait_ge(S["ids_loaded"], 16)
            t = Link(dve, S["text_step"])
            t(v.tensor_copy(ids_f, ids_sb[:, :]))
            t(v.tensor_scalar(idx_f, ids_f, 0.0, float(VOCAB - 1), ALU.max, ALU.min))
            v.tensor_copy(idx[:, :], idx_f).then_inc(S["idx_ready"], 1)
            root = float(D) ** 0.5
            t.add(v.tensor_scalar(mk0, ids_f, float(CUT0), root, ALU.is_lt, ALU.mult))
            t.add(v.tensor_scalar(mk1, ids_f, float(CUT0), root, ALU.is_ge, ALU.mult))
            t.add(v.tensor_scalar(mk2, ids_f, float(CUT1), root, ALU.is_ge, ALU.mult))
            t(v.tensor_scalar(mtmp, ids_f, 0.0, None, ALU.is_gt))
            t(v.tensor_tensor(mk[:, 0:TT], mk0, mtmp, ALU.mult))
            t(v.tensor_scalar(mtmp, ids_f, float(CUT1), None, ALU.is_lt))
            t(v.tensor_tensor(mk[:, TT:2 * TT], mk1, mtmp, ALU.mult))
            t(v.tensor_scalar(mtmp, ids_f, float(VOCAB), None, ALU.is_lt))
            t(v.tensor_tensor(mk[:, 2 * TT:3 * TT], mk2, mtmp, ALU.mult))

            dve.wait_ge(S["s4_loaded"], 16 * N_S4)
            q = Link(dve, S["s4_step"], 0)
            q.n = 1
            q.sync()

            def s3(a):
                return a.rearrange("p (c n) -> p c n", c=2)

            def pair(at, part):
                return prm_sb[:, :, at:at + 2 * NS].rearrange("p c (n r) -> p c n r", r=2)[:, :, :, part]

            dt = prm_sb[:, :, 0:1].broadcast_to((P, 2, NS))
            ew, wim = prm_sb[:, :, 1:1 + NS], prm_sb[:, :, 1 + NS:1 + 2 * NS]
            o = 1 + 2 * NS
            Br, Bi, Pr, Pi, Cr, Ci = [pair(o + 2 * NS * n, part) for n in range(3) for part in range(2)]
            nwr, wi, bdr, bdi, pdr, pdi_ = [s3(a) for a in vec[0:6]]
            v00r, v00i, v01r, v01i, v10r, v10i, v11 = [s3(a) for a in vec[6:13]]
            t1, t2, t3 = [s3(a) for a in vec[13:16]]
            mul, add, sub = ALU.mult, ALU.add, ALU.subtract
            q.add(v.tensor_tensor(nwr, ew, dt, mul))
            q.add(v.tensor_tensor(wi, wim, dt, mul))
            q.add(v.tensor_tensor(bdr, Br, dt, mul))
            q.add(v.tensor_tensor(bdi, Bi, dt, mul))
            q.add(v.tensor_tensor(pdr, Pr, dt, mul))
            q(v.tensor_tensor(pdi_, Pi, dt, mul))

            def product(outr, outi, ar, ai, br, bi, conj):
                q.add(v.tensor_tensor(t1, ar, br, mul))
                q(v.tensor_tensor(t2, ai, bi, mul))
                q.add(v.tensor_tensor(outr, t1, t2, add if conj else sub))
                q.add(v.tensor_tensor(t3, ai, br, mul))
                q(v.tensor_tensor(outi, ar, bi, mul))
                q(v.tensor_tensor(outi, t3, outi, sub if conj else add))

            product(v00r, v00i, bdr, bdi, Cr, Ci, False)
            product(v01r, v01i, bdr, bdi, Pr, Pi, True)
            product(v10r, v10i, pdr, pdi_, Cr, Ci, False)
            q.add(v.tensor_tensor(t1, pdr, Pr, mul))
            q(v.tensor_tensor(t2, pdi_, Pi, mul))
            q(v.tensor_tensor(v11, t1, t2, add))

            b4 = [a.rearrange("p (c m n) -> p c m n", c=2, n=NS) for a in big]
            den_r, den_i, g1, g2, ca_r, ca_i = b4

            def over_m(a):
                return a.unsqueeze(2).broadcast_to((P, 2, M, NS))

            def const(k):
                return zc_sb[:, k * M:(k + 1) * M].unsqueeze(1).unsqueeze(3).broadcast_to((P, 2, M, NS))

            ar, ai, br, bi = [const(k) for k in range(4)]
            q.add(v.tensor_tensor(g1, over_m(nwr), br, mul))
            q(v.tensor_tensor(g2, over_m(wi), bi, mul))
            q(v.tensor_tensor(g1, g1, g2, add))
            q.add(v.tensor_tensor(den_r, g1, ar, add))
            q(v.tensor_tensor(g2, over_m(nwr), bi, mul))
            q(v.tensor_tensor(den_i, over_m(wi), br, mul))
            q(v.tensor_tensor(g2, g2, den_i, sub))
            q(v.tensor_tensor(den_i, g2, ai, add))
            q.add(v.tensor_tensor(g1, den_r, den_r, mul))
            q(v.tensor_tensor(g2, den_i, den_i, mul))
            q(v.tensor_tensor(g1, g1, g2, add))
            q(v.reciprocal(big[3], big[2]))
            q.add(v.tensor_tensor(ca_r, den_r, g2, mul))
            q(v.tensor_tensor(ca_i, den_i, g2, mul))
            f3 = [a.rearrange("p (c m) -> p c m", c=2) for a in frq]
            s00r, s00i, s01r, s01i, s10r, s10i, s11r, s11i = f3[0:8]
            for outr, outi, vr, vi in ((s00r, s00i, v00r, v00i), (s01r, s01i, v01r, v01i), (s10r, s10i, v10r, v10i)):
                q.add(v.tensor_tensor(g1, over_m(vr), ca_r, mul))
                q.add(v.tensor_tensor(g2, over_m(vi), ca_i, mul))
                q.add(v.tensor_tensor(den_r, over_m(vi), ca_r, mul))
                q(v.tensor_tensor(den_i, over_m(vr), ca_i, mul))
                q.add(v.tensor_tensor(g1, g1, g2, add))
                q(v.tensor_tensor(den_r, den_r, den_i, sub))
                q.add(v.tensor_reduce(outr, g1, AX.X, add))
                q(v.tensor_reduce(outi, den_r, AX.X, add))
            q.add(v.tensor_tensor(g1, over_m(v11), ca_r, mul))
            q(v.tensor_tensor(g2, over_m(v11), ca_i, mul))
            q.add(v.tensor_reduce(s11r, g1, AX.X, add))
            q(v.tensor_reduce(f3[19], g2, AX.X, add))
            q(v.tensor_scalar(s11i, f3[19], -1.0, None, mul))

            b3r = zc_sb[:, 2 * M:3 * M].unsqueeze(1).broadcast_to((P, 2, M))
            b3i = zc_sb[:, 3 * M:4 * M].unsqueeze(1).broadcast_to((P, 2, M))
            u1, u2, nr, ni, mr, mi, dr, di, rr, zr, zi = f3[8:19]

            def cmul(outr, outi, ar, ai, br, bi):
                q.add(v.tensor_tensor(u1, ar, br, mul))
                q(v.tensor_tensor(u2, ai, bi, mul))
                q.add(v.tensor_tensor(outr, u1, u2, sub))
                q.add(v.tensor_tensor(f3[19], ar, bi, mul))
                q(v.tensor_tensor(outi, ai, br, mul))
                q(v.tensor_tensor(outi, f3[19], outi, add))

            cmul(nr, ni, s01r, s01i, s10r, s10i)
            cmul(mr, mi, nr, ni, b3r, b3i)
            cmul(dr, di, s11r, s11i, b3r, b3i)
            q(v.tensor_scalar(dr, dr, 1.0, None, add))
            q.add(v.tensor_tensor(u1, dr, dr, mul))
            q(v.tensor_tensor(u2, di, di, mul))
            q(v.tensor_tensor(u1, u1, u2, add))
            q(v.reciprocal(frq[8 + 8], frq[8]))
            q(v.tensor_scalar(di, di, -1.0, None, mul))
            cmul(zr, zi, mr, mi, dr, di)
            q.add(v.tensor_tensor(zr, zr, rr, mul))
            q(v.tensor_tensor(zi, zi, rr, mul))
            q.add(v.tensor_tensor(KF[:, :, 0:M], s00r, zr, sub))
            q.add(v.tensor_tensor(KF[:, :, M:2 * M], s00i, zi, sub))
            q(v.tensor_copy(KF[:, :, 2 * M:KROWS], prm_sb[:, :, PRM - 1:PRM]))
            dve.sem_inc(S["kf_ready"], 1)

            def stats3(k, st, link, var_ready):
                dve.sem_inc(S["tick"], 1)
                for s in range(3):
                    link.add(v.bn_stats(stats[st][:, 6 * s:6 * s + 6], h_tile(3 * k + s)))
                link.sync()
                dve.sem_inc(S["tick"], 1)
                for s in range(3):
                    last = v.bn_aggr(mv[st][:, 2 * s:2 * s + 2], stats[st][:, 6 * s:6 * s + 6])
                last.then_inc(S[var_ready], 1)

            def norm3(k, st, count, rstd_ready, signal):
                dve.wait_ge(S[rstd_ready], count + 1)
                for s in range(3):
                    v.tensor_scalar(x_tile(3 * k + s), h_tile(3 * k + s), mv[st][:, 2 * s:2 * s + 1],
                                    rstd[st][:, s:s + 1], ALU.subtract, ALU.mult).then_inc(S[signal], 1)

            def masked(i, st):
                for s in range(3):
                    n = 3 * i + s
                    dve.wait_ge(gathered[s], 16 * i + 16)
                    row = A[:, bass.ds(n * D + OH + PT * D, 64)]
                    v.tensor_scalar(e_sb[3 * st + s][:, 0:64], row, mk[:, bass.ds(n + TT, 1)], None, ALU.mult)
                    v.tensor_scalar(e_sb[3 * st + s][:, 64:128], row, mk[:, bass.ds(n + 2 * TT, 1)], None, ALU.mult)\
                        .then_inc(S["e_ready"], 1)

            masked(0, 0)
            masked(1, 1)

            def text3(i, st):
                dve.wait_ge(S["text_done"], i + 1)
                link = Link(dve, S["h_text"], 6 * i)
                for s in range(3):
                    n = 3 * i + s
                    link.add(v.scalar_tensor_tensor(out=h_tile(PT + n), in0=h_tile(PT + n), scalar=mk[:, bass.ds(n, 1)],
                                                    in1=text_psum(st, s), op0=ALU.mult, op1=ALU.add))
                link.sync()
                stats3(PT // 3 + i, st, link, "vart_ready")

            def text_norm(i, st):
                norm3(PT // 3 + i, st, i, "rstdt_ready", "xn_ready")

            def patch_stats(i):
                dve.wait_ge(S["h_patch"], 3 * i + 3)
                stats3(i, 2, Link(dve, S["lnp_step"], 3 * i), "varp_ready")

            def text_psum(st, s):
                return bank(2 + 2 * st, D, D * s) if s < 2 else bank(3 + 2 * st, D)

            n3 = TT // 3
            with dve.Fori(0, (n3 - 3) // 2) as i:
                for st in range(2):
                    text3(2 * i + st, st)
                    masked(2 * i + st + 2, st)
                patch_stats(i)
                for st in range(2):
                    text_norm(2 * i + st, st)
                norm3(i, 2, i, "rstdp_ready", "xn_ready")
            text3(n3 - 3, 0)
            masked(n3 - 1, 0)
            text3(n3 - 2, 1)
            patch_stats(PT // 3 - 1)
            text_norm(n3 - 3, 0)
            text_norm(n3 - 2, 1)
            norm3(PT // 3 - 1, 2, PT // 3 - 1, "rstdp_ready", "xn_ready")
            text3(n3 - 1, 0)
            text_norm(n3 - 1, 0)

            for n in range(32):
                dve.wait_ge(S["silu_done"], n + 1)
                hv = H3[:, :, 8 * n:8 * n + 8]
                v.tensor_tensor(hv, hv, silu_sb[n % 3].rearrange("p (e b) -> p b e", b=TILES), ALU.add)\
                    .then_inc(S["h1_ready"], 1)
            dve.wait_ge(S["h1_ready"], 32)

            def group_stats(g):
                for k in range(PER * g, PER * (g + 1)):
                    st = k % 3
                    if k >= 3:
                        dve.wait_ge(S["ln2_step"], 2 * k - 4)
                    v.bn_stats(stats[st][:, 0:6], H3[:, k, :]).then_inc(S["ln2_step"], 1)
                    if k > PER * g:
                        group_aggr(k - 1)
                group_aggr(PER * (g + 1) - 1, True)

            def group_aggr(k, last=False):
                dve.wait_ge(S["ln2_step"], 2 * k + 1)
                ins = v.bn_aggr(mv2[:, 2 * k:2 * k + 2], stats[k % 3][:, 0:6])
                ins.then_inc(S["ln2_step"], 1)
                if last:
                    dve.wait_ge(S["ln2_step"], 2 * k + 2)
                    dve.sem_inc(S["var2_ready"], 1)

            def group_rows(g):
                dve.wait_ge(S["std2_ready"], g + 1)
                o = PER * g
                v.reciprocal(std2[:, o:o + PER], std2[:, o:o + PER]).then_inc(S["rstd2_ready"], 1)
                dve.wait_ge(S["rstd2_ready"], g + 1)
                for k in range(o, o + PER):
                    v.tensor_scalar(X3[:, k, :], H3[:, k, :], mv2[:, 2 * k:2 * k + 1], std2[:, k:k + 1],
                                    ALU.subtract, ALU.mult).then_inc(S["row_ready"], 1)

            group_stats(0)
            group_stats(1)
            group_rows(0)
            group_stats(2)
            group_rows(1)
            group_rows(2)

            def j3(a):
                return a.rearrange("p (j e) -> p j e", e=E)

            def per_tile(a):
                return a.unsqueeze(2).broadcast_to((P, TILES, E))

            def per_expert(a):
                return a.unsqueeze(1).broadcast_to((P, TILES, E))

            g = Link(dve, S["gate_step"])
            dve.wait_ge(S["gate_const_loaded"], 16 * N_GC)
            dve.wait_ge(S["prefill_done"], 16)
            dve.wait_ge(S["row_ready"], TILES)
            dve.wait_ge(S["gate_done"], TILES // 3)
            logits = bank(7, GE)
            g.add(v.memset(zero57, 0.0))
            g(v.tensor_reduce(mx, j3(logits), AX.X, ALU.max))
            v.tensor_tensor(j3(g_log), j3(logits), per_tile(mx), ALU.subtract).then_inc(S["exp_in"], 1)
            dve.wait_ge(S["exp_out"], 1)
            g(v.tensor_reduce(sm, j3(g_ex), AX.X, ALU.add))
            g(v.reciprocal(sm, sm))
            g(v.tensor_tensor(j3(g_ex), j3(g_ex), per_tile(sm), ALU.mult))

            def first_max(scores, sel):
                g(v.tensor_reduce(mx, j3(scores), AX.X, ALU.max))
                g(v.tensor_tensor(j3(g_t), j3(scores), per_tile(mx), ALU.is_equal))
                g(v.tensor_tensor(j3(g_t), j3(g_t), per_expert(rev_sb[:, :]), ALU.mult))
                g(v.tensor_reduce(mx, j3(g_t), AX.X, ALU.max))
                g(v.tensor_tensor(j3(sel), j3(g_t), per_tile(mx), ALU.is_equal))

            first_max(g_ex, sel1)
            g(v.scalar_tensor_tensor(out=g_log, in0=sel1, scalar=-2.0, in1=g_ex, op0=ALU.mult, op1=ALU.add))
            first_max(g_log, sel2)
            g(v.tensor_tensor(selS, sel1, sel2, ALU.add))
            dve.sem_inc(S["sel_ready"], 1)
            g(v.tensor_tensor(posf, g_ex, selS, ALU.mult))
            dve.sem_inc(S["cw_ready"], 1)
            dve.wait_ge(S["ranks_done"], 1)
            g(v.tensor_copy(cnt, bank(1, GE)))
            for e in range(E):
                g.add(v.tensor_tensor_scan(j3(incl)[:, :, e], j3(cnt)[:, :, e], zero57, 0.0, ALU.add, ALU.add))
            g.sync()
            g(v.tensor_copy(tot, j3(incl)[:, TILES - 1, :]))
            g(v.tensor_tensor(incl, incl, cnt, ALU.subtract))
            g.add(v.memset(z8, 0.0))
            g(v.tensor_scalar(pdi, tot, float(SUB * P - 1), None, ALU.add))
            g(v.tensor_scalar(pdj, pdi, 8, 8, ALU.arith_shift_right, ALU.logical_shift_left))
            g(v.tensor_copy(pd, pdj))
            g(v.tensor_tensor_scan(inc8, pd, z8, 0.0, ALU.add, ALU.add))
            g(v.tensor_tensor(off, inc8, pd, ALU.subtract))
            g(v.tensor_tensor(cnt, bank(0, GE), incl, ALU.add))
            g(v.tensor_tensor(j3(cnt), j3(cnt), per_expert(off), ALU.add))
            g.add(v.tensor_tensor(g_t, cnt, sel1, ALU.mult))
            g(v.tensor_tensor(g_log, cnt, sel2, ALU.mult))
            g.add(v.tensor_reduce(pfa, j3(g_t), AX.X, ALU.add))
            g(v.tensor_reduce(pfb, j3(g_log), AX.X, ALU.add))
            for pf, lo, hi in ((pfa, loA, hiA), (pfb, loB, hiB)):
                g(v.tensor_copy(pint, pf))
                g.add(v.tensor_scalar(lint, pint, P - 1, None, ALU.bitwise_and))
                g(v.tensor_scalar(pint, pint, 7, None, ALU.arith_shift_right))
                g.add(v.tensor_copy(lo, lint))
                g(v.tensor_copy(hi, pint))
            g(v.tensor_scalar(pcol1, pcol_sb[:, :], 1.0, None, ALU.add))

            def one_hots(j, turns):
                for r, (lo, hi) in turns:
                    v.tensor_scalar(oh_lo[r], iota16[:, :], lo[:, bass.ds(j, 1)], None, ALU.is_equal)
                    v.tensor_scalar(oh_hi[r][:, 0:P], iota16[:, :], hi[:, bass.ds(j, 1)], pcol1, ALU.is_equal, ALU.mult)
                    v.tensor_scalar(oh_hi[r][:, P:2 * P], iota16[:, :], hi[:, bass.ds(j, 1)], jcol_sb[:, bass.ds(j, 1)],
                                    ALU.is_equal, ALU.mult).then_inc(S["hot_ready"], 1)

            both = ((loA, hiA), (loB, hiB))
            one_hots(0, [(0, both[0]), (1, both[1])])
            one_hots(1, [(2, both[0]), (3, both[1])])
            with dve.Fori(1, TILES // 2) as i:
                for h in range(2):
                    dve.wait_ge(S["hot_used"], 4 * i + 2 * h - 2)
                    dve.sem_inc(S["tick"], 1)
                    one_hots(2 * i + h, [(2 * h, both[0]), (2 * h + 1, both[1])])
            dve.wait_ge(S["hot_used"], 2 * TILES - 4)
            one_hots(TILES - 1, [(0, both[0]), (1, both[1])])
            g(v.tensor_scalar(t_exp[:, :], kcol_sb[:, :], inc8[:, 0:1], None, ALU.is_ge))
            for e in range(1, E - 1):
                g(v.scalar_tensor_tensor(out=t_exp[:, :], in0=kcol_sb[:, :], scalar=inc8[:, e:e + 1],
                                         in1=t_exp[:, :], op0=ALU.is_ge, op1=ALU.add))
            g(v.tensor_copy(t_expi[:, :], t_exp[:, :]))
            dve.wait_ge(S["map_done"], 1)
            g.add(v.tensor_copy(v1, bank(2, P)))
            g(v.tensor_copy(v2, bank(2, P, P)))
            g(v.tensor_scalar(vz, v1, 0.0, float(TOKENS + TILES), ALU.is_equal, ALU.mult))
            g(v.tensor_scalar(v2, v2, float(TILES), None, ALU.subtract))
            g(v.scalar_tensor_tensor(out=v2, in0=v1, scalar=float(TILES), in1=v2, op0=ALU.mult, op1=ALU.add))
            g(v.tensor_tensor(v2, v2, vz, ALU.add))
            g(v.tensor_scalar(vz, v1, 0.0, pcol_sb[:, 0:1], ALU.is_equal, ALU.mult))
            g(v.tensor_tensor(v2, v2, vz, ALU.add))
            g(v.tensor_copy(sid[:, :], v2))
            dve.sem_inc(S["slots_ready"], 1)

            for n in range(2 * POOL_EXPERTS, 2 * E):
                dve.wait_ge(S["w_hi"], n + 1)
                o = 8192 * (n // 2) + 4096 * (n % 2)
                v.scalar_tensor_tensor(out=A16[:, o + 2048:o + 4096], in0=stage[n % 2], scalar=WSCALE,
                                       in1=A16[:, o:o + 2048], op0=ALU.mult, op1=ALU.subtract)\
                    .then_inc(S["w_free_dve"], 1)
            dve.wait_ge(S["w_free_pool"], 2 * POOL_EXPERTS)
            dve.wait_ge(S["w_free_dve"], 2 * E - 2 * POOL_EXPERTS)
            dve.wait_ge(S["b2_loaded"], 16)
            b = Link(dve, S["b2_step"])
            dve.wait_ge(S["rows_dumped"], 16 * GROUPS)
            b.add(v.memset(one16, 1.0))
            b(v.tensor_scalar(b2f, b2f, WSCALE, None, ALU.mult))
            b(v.tensor_copy(b2h, b2f))
            b(v.tensor_tensor(b2l, b2f, b2h, ALU.subtract))
            b(v.tensor_scalar(b2l, b2l, pcol_sb[0:2, 0:1], None, ALU.mult))
            b(v.tensor_scalar(junk8[0][0:2, 0:1], pcol_sb[0:2, 0:1], -1.0, 1.0, ALU.mult, ALU.add))
            b(v.scalar_tensor_tensor(out=b2r, in0=b2h, scalar=junk8[0][0:2, 0:1], in1=b2l, op0=ALU.mult, op1=ALU.add))
            dve.sem_inc(S["b2_ready"], 1)

            def split_x(k, s, gathered_, free):
                dve.wait_ge(S["xt_done"], k + 1)
                for u in range(SUB):
                    dve.wait_ge(cw_gathered[s][u], gathered_)
                    if free is not None and u == 0:
                        dve.wait_ge(S["slot_free"], k - 1)
                    last = v.scalar_tensor_tensor(out=junk8[s][:, E * u:E * (u + 1)], in0=iota_sb[:, :],
                                           scalar=t_exp[:, bass.ds(k, 1)], in1=cwg[s][:, E * u:E * (u + 1)],
                                           op0=ALU.is_equal, op1=ALU.mult,
                                           accum_out=meta_cw[:, bass.ds(k * SUB + u, 1)])
                last.then_inc(S["slot_free"], 1)
                if free is not None:
                    dve.wait_ge(S["mm1_done"], free)
                v.tensor_scalar(xhi[s], bank(s), XSCALE, None, ALU.mult).then_inc(S["x_hi"], 1)
                dve.wait_ge(S["x_hi"], k + 1)
                v.scalar_tensor_tensor(out=xlo[s], in0=bank(s), scalar=XSCALE, in1=xhi[s], op0=ALU.mult,
                                       op1=ALU.subtract).then_inc(S["x_split"], 1)

            def split_h(k, s, free):
                if free is not None:
                    dve.wait_ge(S["mm2_done"], free)
                for q in range(4):
                    dve.wait_ge(S["gelu_done"], 8 * k + 2 * q + 2)
                    v.tensor_copy(hhi[s][:, 512 * q:512 * (q + 1)], hg[q]).then_inc(S["h_hi"], 1)
                    dve.wait_ge(S["h_hi"], 4 * k + q + 1)
                    v.tensor_tensor(hlo[s][:, 512 * q:512 * (q + 1)], hg[q], hhi[s][:, 512 * q:512 * (q + 1)],
                                    ALU.subtract).then_inc(S["h_split"], 1)

            def scale_y(k, s, free):
                dve.wait_ge(S["mm2_done"], k + 1)
                dve.wait_ge(S["x_hi"], k + 1)
                if free is not None:
                    dve.wait_ge(added[1], free)
                for u in range(SUB):
                    last = v.tensor_scalar(ys[s][:, D * u:D * (u + 1)], bank(6 + s, D, D * u),
                                           meta_cw[:, bass.ds(k * SUB + u, 1)], 1.0 / WSCALE, ALU.mult, ALU.mult)
                last.then_inc(S["y_done"], 1)

            split_x(0, 0, 16, None)
            split_x(1, 1, 16, None)
            split_h(0, 0, None)

            def step(k, s, half, first):
                split_x(k + 2, s, 16 * half + 32, 4 * k + 4)
                split_h(k + 1, 1 - s, None if first and s == 0 else k)
                scale_y(k, s, None if first else 16 * k - 16)

            step(0, 0, 0, True)
            step(1, 1, 0, True)
            with dve.Fori(1, NT // 2 - 1) as i:
                step(2 * i, 0, i, False)
                step(2 * i + 1, 1, i, False)
            split_h(NT - 1, 1, NT - 2)
            scale_y(NT - 2, 0, 16 * (NT - 3))
            scale_y(NT - 1, 1, 16 * (NT - 2))

        @block.tensor
        def _(pe):
            t = nc.tensor
            pe.wait_ge(S["patch_const_loaded"], 16 * N_PC)

            def patch(j, s, loaded):
                pe.wait_ge(patch_loaded[s], loaded)
                for c in range(KC):
                    t.matmul(bank(s, D), xP_sb[s][:, P * c:P * (c + 1)], Wp_sb[:, c, :], start=c == 0, stop=False)
                t.matmul(bank(s, D), psel[:, :], pos_sb[:, bass.ds(j * D, D)], start=False, stop=True)\
                    .then_inc(S["patch_done"], 1)

            patch(0, 0, 16)
            patch(1, 1, 16)
            with pe.Fori(1, PT // 2) as i:
                for s in range(2):
                    pe.wait_ge(S["h_patch"], 2 * i + s - 1)
                    patch(2 * i + s, s, 16 * i + 16)
            pe.wait_ge(S["const_loaded"], 48)
            pe.wait_ge(S["kf_ready"], 1)
            t.transpose(PS[0:KROWS, 1024:1024 + P], KF[:, 0, :], ident[:, :])
            t.transpose(PS[0:KROWS, 1024 + P:1024 + 2 * P], KF[:, 1, :], ident[:, :]).then_inc(S["kfT_psum"], 1)
            pe.wait_ge(S["kfT_ready"], 1)

            def toeplitz(n):
                if n >= 2:
                    pe.wait_ge(S["toep_ready"], n - 1)
                for u in range(2):
                    tt = 2 * n + u
                    o = 512 * (6 + n % 2) + D * u
                    last = t.matmul(PS[0:64, o:o + D], basis_sb[:, L - 1 - tt:2 * L - 1 - tt], kfT,
                                    start=True, stop=True)
                last.then_inc(S["toep_done"], 1)

            def turn(i, st):
                pe.wait_ge(S["e_ready"], 3 * i + 3)
                for s in range(3):
                    last = t.transpose(bank(st, P, P * s), e_sb[3 * st + s], ident[:, :])
                last.then_inc(S["eT_psum"], 1)

            def project(i, st, first):
                pe.wait_ge(S["eT_ready"], i + 1)
                for s in range(3):
                    dst = bank(2 + 2 * st, D, D * s) if s < 2 else bank(3 + 2 * st, D)
                    cls = first and s == 0
                    last = t.matmul(dst, eT[:, 3 * P * st + P * s:3 * P * st + P * (s + 1)], P12_sb[:, :],
                                    start=True, stop=not cls)
                    if cls:
                        t.matmul(dst, csel[:, :], crow[:, :], start=False, stop=True)
                last.then_inc(S["text_done"], 1)

            pe.wait_ge(S["h_patch"], PT)
            turn(0, 0)
            for k in range(TRIPLES):
                if k + 1 < TRIPLES:
                    turn(k + 1, (k + 1) % 2)
                for n in toeplitz_share(k):
                    toeplitz(n)
                if k >= 2:
                    pe.wait_ge(S["h_text"], 6 * k - 9)
                project(k, k % 2, k == 0)

            pe.wait_ge(S["xn_ready"], TILES)
            pe.wait_ge(S["toep_copied"], 64)
            for n in range(32):
                if n >= 4:
                    pe.wait_ge(S["silu_done"], n - 3)
                for c in range(8):
                    ch = 8 * n + c
                    for q in (0, 64):
                        last = t.matmul(PS[q:q + 64, 512 * (4 + n % 4) + TILES * c:512 * (4 + n % 4) + TILES * (c + 1)],
                                        Tz[q:q + 64, :, ch],
                                        X3[q:q + 64, :, ch], start=True, stop=True)
                last.then_inc(S["conv_done"], 1)

            def turn_rows(k):
                pe.wait_ge(S["row_ready"], 3 * k + 3)
                for s in range(3):
                    for c in range(2):
                        o = (2 * s + c) * P
                        last = t.transpose(bank(2 * (k % 2) + o // 512, P, o % 512), X3[:, 3 * k + s, P * c:P * (c + 1)],
                                           ident[:, :])
                last.then_inc(S["xT_psum"], 1)

            def gate(k):
                pe.wait_ge(S["xT_ready"], k + 1)
                for s in range(3):
                    for c in range(2):
                        last = t.matmul(bank(7, E, (3 * k + s) * E), xT_sb[k % 2][:, (2 * s + c) * P:(2 * s + c + 1) * P],
                                        wg_sb[:, E * c:E * (c + 1)], start=c == 0, stop=c == 1)
                last.then_inc(S["gate_done"], 1)

            pe.wait_ge(S["gate_const_loaded"], 16 * N_GC)
            pe.wait_ge(S["silu_done"], 32)
            turn_rows(0)
            for k in range(TILES // 3):
                if k + 1 < TILES // 3:
                    turn_rows(k + 1)
                gate(k)
            pe.wait_ge(S["sel_ready"], 1)
            t.matmul(bank(0, GE), tri[:, :], selS, start=True, stop=True)
            t.matmul(bank(1, GE), ones[:, :], selS, start=True, stop=True).then_inc(S["ranks_done"], 1)

            def invert(r, first=False, last=False):
                t.matmul(bank(2, 2 * P), oh_lo[r], oh_hi[r], start=first, stop=last).then_inc(S["hot_used"], 1)

            pe.wait_ge(S["hot_ready"], 2)
            invert(0, first=True)
            invert(1)
            pe.wait_ge(S["hot_ready"], 4)
            invert(2)
            invert(3)
            with pe.Fori(1, TILES // 2) as i:
                for h in range(2):
                    pe.wait_ge(S["hot_ready"], 4 * i + 2 * h + 2)
                    invert(2 * h)
                    invert(2 * h + 1)
            pe.wait_ge(S["hot_ready"], 2 * TILES)
            invert(0)
            t.matmul(bank(2, 2 * P), oh_lo[1], oh_hi[1], start=False, stop=True).then_inc(S["map_done"], 1)

            def turn_x(k, s, gathered_, free):
                for u in range(SUB):
                    pe.wait_ge(row_gathered[s][u], gathered_)
                if free is not None:
                    pe.wait_ge(S["x_split"], free)
                for u in range(SUB):
                    for c in range(2):
                        last = t.transpose(bank(s, P, 2 * P * c + P * u), xs[s][:, D * u + P * c:D * u + P * (c + 1)],
                                           ident[:, :])
                last.then_inc(S["xt_done"], 1)

            def expert_of(k):
                return pe.value_load(t_expi[0:1, bass.ds(k, 1)], min_val=0, max_val=E - 1)

            def w1_product(k, s, e, first):
                pe.wait_ge(S["x_split"], k + 1)
                for q in range(4):
                    if not first:
                        pe.wait_ge(S["gelu_done"], 8 * k + 2 * q - 6)
                    for f in (2 * q, 2 * q + 1):
                        dst = bank(2 + q, 256, 256 * (f % 2))
                        for c in range(2):
                            hi = A16[:, bass.ds(e * 8192 + (c * HID + f * P), P)]
                            lo = A16[:, bass.ds(e * 8192 + (2048 + c * HID + f * P), P)]
                            t.matmul(dst, hi, xhi[s][:, 256 * c:256 * (c + 1)], start=c == 0, stop=False)
                            t.matmul(dst, hi, xlo[s][:, 256 * c:256 * (c + 1)], start=False, stop=False)
                            last = t.matmul(dst, lo, xhi[s][:, 256 * c:256 * (c + 1)], start=False, stop=c == 1)
                    last.then_inc(S["mm1_done"], 1)

            def w2_product(k, s, e, free):
                if free is not None:
                    pe.wait_ge(S["y_done"], free)
                pe.wait_ge(S["h_split"], 4 * k + 4)
                for u in range(SUB):
                    dst = bank(6 + s, D, D * u)
                    for f in range(FCH):
                        hi = A16[:, bass.ds(e * 8192 + (4096 + f * D), D)]
                        lo = A16[:, bass.ds(e * 8192 + (6144 + f * D), D)]
                        o = 256 * f + P * u
                        t.matmul(dst, hhi[s][:, o:o + P], hi, start=f == 0, stop=False)
                        t.matmul(dst, hhi[s][:, o:o + P], lo, start=False, stop=False)
                        t.matmul(dst, hlo[s][:, o:o + P], hi, start=False, stop=False)
                    last = t.matmul(dst, one16, A16[0:2, bass.ds(e * D + (2 * b2p_at + E * D), D)], start=False, stop=True)
                last.then_inc(S["mm2_done"], 1)

            pe.wait_ge(S["slots_ready"], 1)
            pe.wait_ge(S["b2_ready"], 1)
            turn_x(0, 0, 16, None)
            turn_x(1, 1, 16, None)
            w1_product(0, 0, expert_of(0), True)

            def step(k, s, half, e0, e1, first):
                w1_product(k + 1, 1 - s, e1, False)
                turn_x(k + 2, s, 16 * half + 32, k + 1)
                w2_product(k, s, e0, None if first else k - 1)

            ex = [expert_of(k) for k in range(3)]
            step(0, 0, 0, ex[0], ex[1], True)
            step(1, 1, 0, ex[1], ex[2], True)
            with pe.Fori(1, NT // 2 - 1) as i:
                ex = [expert_of(2 * i + n) for n in range(3)]
                step(2 * i, 0, i, ex[0], ex[1], False)
                step(2 * i + 1, 1, i, ex[1], ex[2], False)
            ex = [expert_of(NT - 2), expert_of(NT - 1)]
            w1_product(NT - 1, 1, ex[1], False)
            w2_product(NT - 2, 0, ex[0], NT - 3)
            w2_product(NT - 1, 1, ex[1], NT - 2)


def kernel(**inputs):
    import numpy as np
    import concourse.bacc as bacc
    from concourse.bass_utils import run_bass_kernel_spmd as run

    I = {k: np.asarray(v) for k, v in inputs.items()}
    f = np.float32
    half = np.arange(P) // 64
    t_of = np.arange(P) % 64
    arr = {}
    x = I["x"].reshape(L, 3, 6, 16, 6, 16).transpose(2, 4, 0, 1, 3, 5).reshape(2, PT, L, KC, P)
    arr["xP"] = x.transpose(1, 4, 3, 0, 2).reshape(PT * P, KC * P)
    arr["Wp"] = I["L0_tok_W"].T.reshape(KC, P, D).transpose(1, 0, 2).reshape(P, KC * D)
    pos = I["L0_tok_pos_embed"][0]
    arr["posrows"] = np.stack([pos[1:1 + PT].reshape(-1), pos[1 + PT:1 + 2 * PT].reshape(-1), np.tile(I["L0_tok_b"], PT)])
    arr["patsel"] = np.stack([half == 0, half == 1, half >= 0]).astype(f)
    arr["clssel"] = np.stack([half == 0, half == 0]).astype(f)
    arr["clsrows"] = np.stack([I["L0_tok_cls_token"][0, 0], pos[0]])
    txt = I["x_txt"]
    ids = np.full((P, TT), 127999, np.int32)
    ids[:64, 1:] = txt[:, :TT - 1]
    ids[64:, :] = txt[:, TT - 1:]
    arr["ids"] = ids
    table = np.zeros((VOCAB, D), f)
    table[:CUT0] = I["L0_txt_emb0"]
    table[CUT0:CUT1, :64] = I["L0_txt_emb1"]
    table[CUT1:, :64] = I["L0_txt_emb2"]
    arr["table"] = table
    arr["P12"] = np.concatenate([I["L0_txt_proj1"].T, I["L0_txt_proj2"].T], 0)
    parts = [I["L0_attn_log_dt"], I["L0_attn_inv_w_real"], I["L0_attn_w_imaginary"], I["L0_attn_B"].reshape(D, -1),
             I["L0_attn_P"].reshape(D, -1), I["L0_attn_C"].reshape(D, -1), I["L0_attn_D"].reshape(D, 1)]
    arr["prm"] = np.concatenate(parts, 1).reshape(2, P, PRM).transpose(1, 0, 2).reshape(P, 2, PRM)
    th = 2 * np.pi * np.arange(M) / L
    om = np.cos(th) - 1j * np.sin(th)
    om[-1] = -1.0
    arr["zc"] = np.tile(np.concatenate([2 * (1 - om).real, 2 * (1 - om).imag, (1 + om).real, (1 + om).imag])[None], (P, 1)).astype(f)
    lag = L - 1 - np.arange(2 * L - 1)
    w = np.where((np.arange(M) == 0) | (np.arange(M) == M - 1), 1.0, 2.0) * 2.0 / L
    ph = np.outer(np.arange(M), lag) * 2 * np.pi / L
    sn = -w[:, None] * np.sin(ph)
    sn[0] = sn[-1] = 0
    bas = np.concatenate([w[:, None] * np.cos(ph), sn, (lag == 0)[None] * 1.0], 0) * (lag >= 0)
    arr["basis"] = bas.astype(f)
    arr["ident_d"] = np.eye(P, dtype=f)
    arr["tri_d"] = np.triu(np.ones((P, P), f), 1)
    arr["iota16_d"] = np.tile(np.arange(P)[None], (P, 1)).astype(np.float16)
    arr["jcol"] = np.tile(np.arange(TILES, dtype=f)[None], (P, 1))
    arr["wg"] = I["L0_ffn_w_gate"].T.reshape(2, P, E).transpose(1, 0, 2).reshape(P, 2 * E)
    w1 = I["L0_ffn_W1"].reshape(E, 2, P, HID).transpose(0, 2, 1, 3).reshape(E, P, 2048)
    w2 = I["L0_ffn_W2"].reshape(E, FCH, P, D).transpose(0, 2, 1, 3).reshape(E, P, 2048)
    arr["wts"] = np.stack([w1, w2], 1).reshape(E * 2 * P, 2048)
    arr["b1T"] = I["L0_ffn_b1"].reshape(E, FCH, P).transpose(2, 0, 1).reshape(P, E * FCH)
    arr["b2d"] = np.tile(I["L0_ffn_b2"].reshape(1, E * D), (2, 1))
    arr["iota8"] = np.tile(np.arange(E, dtype=f)[None], (P, 1))
    arr["rev8"] = np.tile((E - np.arange(E, dtype=f))[None], (P, 1))
    arr["pcol"] = np.arange(P, dtype=f)[:, None]
    arr["kcol"] = np.tile((SUB * P * np.arange(NT, dtype=f))[None], (P, 1))

    nc = bacc.Bacc("TRN2", target_bir_lowering=False, num_devices=1)
    args, feed = [], {}
    for name, a in arr.items():
        a = np.ascontiguousarray(a)
        feed[f"in_{name}"] = a
        args.append(nc.dram_tensor(f"in_{name}", a.shape, mybir.dt.from_np(a.dtype), kind="ExternalInput").ap())
    args.append(nc.dram_tensor("out_rows", (TOKENS + P, D), F32, kind="ExternalOutput").ap())
    build(nc, *args)
    r = run(nc, [feed], core_ids=[0])
    got = r.results[0]["out_rows"][:TOKENS].reshape(2, L, TILES, D).transpose(2, 0, 1, 3)
    out = np.empty((L, NCOL, D), f)
    out[:, 1:1 + PT] = got[:PT, 0].transpose(1, 0, 2)
    out[:, 1 + PT:1 + 2 * PT] = got[:PT, 1].transpose(1, 0, 2)
    out[:, 0] = got[PT, 0]
    out[:, 1 + 2 * PT:2 * PT + TT] = got[PT + 1:, 0].transpose(1, 0, 2)
    out[:, 2 * PT + TT:] = got[PT:, 1].transpose(1, 0, 2)
    return out
```

```python
import concourse.bass as bass
from concourse import mybir
from contextlib import ExitStack

F32 = mybir.dt.float32
F16 = mybir.dt.float16
I32 = mybir.dt.int32
ACT = mybir.ActivationFunctionType
ALU = mybir.AluOpType
AX = mybir.AxisListType

P = 128
L, NCOL, D = 64, 114, 256
TILES, PT = L * NCOL // P, 18
TT = TILES - PT
KC = 6
NS, M = 16, L // 2 + 1
KROWS = 2 * M + 1
E, HID = 8, 1024
FCH = HID // P
SUB = 2
NT = 2 * TILES // SUB + E - 1
COLS = NT * SUB
TOKENS = TILES * P
CHUNK = 1024
PIECES = list(range(6)) + list(range(8, 14)) + [6, 15, 7, 14]
CONV_CHUNKS, POOL_CHUNKS, MAP_CHUNKS, CHUNKS = 12, 22, 26, 4 * E
BATCH = 3
WSCALE, XSCALE = 64.0, 64.0
EARLY, EARLY_TILES = 160, 6
VOCAB, CUT0, CUT1 = 32000, 5000, 15000
EPS = 1e-5
PRM = 3 * 2 * NS + 2 * NS + 2

OT, OH = 0, L * D
OX = OH + TILES * D
ARENA = OX + TILES * D
WEXP = 4 * 2048 // 2
WORK = E * WEXP


class Link:

    def __init__(self, eng, sem, base=0):
        self.eng, self.sem, self.base, self.n = eng, sem, base, 0

    def add(self, ins):
        ins.then_inc(self.sem, 1)
        self.n += 1

    def sync(self):
        self.eng.wait_ge(self.sem, self.base + self.n)

    def __call__(self, ins):
        self.add(ins)
        self.sync()


def build(nc, xP, Wp, posrows, patsel, clssel, clsrows, ids, table, P12, prm, zc, basis, ident_d, tri_d,
          iota16_d, rowid1_d, wg, wts, b1T, b2d, iota8, rev8, pad_row_d, kcol, out):
    rows = nc.dram_tensor("rows", (TOKENS + P, 2 * D), F16, kind="Internal").ap()
    cws = nc.dram_tensor("cws", (TOKENS + P, E), F32, kind="Internal").ap()
    ctx = ExitStack()
    with ctx:
        def sb(name, shape, dt=F32):
            return ctx.enter_context(nc.sbuf_tensor(name, shape, dt))

        def sem(name):
            return ctx.enter_context(nc.semaphore(name))

        A = sb("arena", [P, ARENA])
        A16 = A[:, :].bitcast(F16)
        Tz = A[:, OT:OH].rearrange("p (h t) -> p h t", t=L)
        H3 = A[:, OH:OX].rearrange("p (j d) -> p j d", d=D)
        X3 = A[:, OX:ARENA].rearrange("p (j r) -> p j r", r=D)
        X16 = A16[:, 2 * OX:2 * ARENA].rearrange("p (j w r) -> p j w r", w=2, r=D)

        def h_tile(j):
            return A[:, bass.ds(j * D + OH, D)]

        def x_tile(j):
            return A[:, bass.ds(j * D + OX, D)]

        taken = [OT]

        def scratch(n):
            taken[0] += n
            assert taken[0] <= OH
            return A[:, taken[0] - n:taken[0]]

        pos_sb = scratch(PT * D)[0:3, :]
        prm_sb = scratch(2 * PRM).rearrange("p (c k) -> p c k", k=PRM)
        zc_sb = scratch(4 * M)
        KF = scratch(2 * P).rearrange("p (c k) -> p c k", k=P)
        big = [scratch(2 * M * NS) for _ in range(6)]
        vec = [scratch(2 * NS) for _ in range(16)]
        frq = [scratch(2 * M) for _ in range(20)]
        psel = scratch(P)[0:3, :]
        ids_f, idx_f, mk0, mk1, mk2, mtmp = [scratch(TT) for _ in range(6)]

        def s3(a):
            return a.rearrange("p (c n) -> p c n", c=2)

        def over_m(a):
            return a.unsqueeze(2).broadcast_to((P, 2, M, NS))

        b4 = [a.rearrange("p (c m n) -> p c m n", c=2, n=NS) for a in big]
        p4 = [A[:, OX + 2 * M * NS * n:OX + 2 * M * NS * (n + 1)].rearrange("p (c m n) -> p c m n", c=2, n=NS)
              for n in range(4)]

        B = sb("ring_arena", [P, 4096])
        Wp_sb = B[:, 0:KC * D].rearrange("p (k d) -> p k d", d=D)
        xP_sb = [B[:, 1536 + 768 * s:1536 + 768 * (s + 1)] for s in range(2)]
        E_AT = 1536 + 2 * 768
        e_sb = [B[:, E_AT + P * s:E_AT + P * (s + 1)] for s in range(6)]
        e3 = [B[:, E_AT + 3 * P * s:E_AT + 3 * P * (s + 1)].rearrange("p (s w d) -> p s w d", s=3, w=2)
              for s in range(2)]
        kfT = B[:, 0:D]
        eT = B[:, 1536:1536 + 6 * P]
        silu_sb = [B[:, 8 * TILES * s:8 * TILES * (s + 1)] for s in range(2)]
        stage = [B[:, CHUNK * (s + 1):CHUNK * (s + 2)] for s in range(3)]

        ident = sb("ident", [P, P])
        ident16 = sb("ident16", [P, P], F16)
        tri = sb("tri", [P, P])
        ones = sb("ones", [P, P])
        basis_sb = sb("basis_sb", [P, 2 * L - 1])
        P12_sb = sb("P12_sb", [P, D])
        csel = sb("csel", [2, P])
        crow = sb("crow", [2, D])
        ids_sb = sb("ids_sb", [P, TT], I32)
        idx = sb("idx", [P, TT], I32)
        mk = sb("mk", [P, 3 * TT])
        MK = mk[:, :].rearrange("p (w n) -> p w n", n=TT)
        stats = [sb(f"stats{s}", [P, 18]) for s in range(3)]
        mv = [sb(f"mv{s}", [P, 6]) for s in range(3)]
        veps = [sb(f"veps{s}", [P, 3]) for s in range(3)]
        eps3 = sb("eps3", [P, 3])
        expo = sb("expo", [P, 3])
        rstd = [sb(f"rstd{s}", [P, 3]) for s in range(3)]
        stats_all = sb("stats_all", [P, TILES * 12])
        mv2 = sb("mv_all", [P, 2 * TILES])
        std2 = sb("std_all", [P, TILES])
        eps1 = sb("eps1", [P, 1])
        wg_sb = sb("wg_sb", [P, 2 * E])
        wgs = sb("wgs", [P, 2 * E])
        wg_hi = sb("wg_hi", [P, 2 * E], F16)
        wg_lo = sb("wg_lo", [P, 2 * E], F16)
        b1_sb = sb("b1_sb", [P, E * FCH])
        iota_sb = sb("iota_sb", [P, E])
        rev_sb = sb("rev_sb", [P, E])
        pad_row = sb("pad_row", [P, 1])
        iota16 = sb("iota16", [P, P], F16)
        rowid1 = sb("rowid1", [P, TILES])
        kcol_sb = sb("kcol_sb", [P, NT])
        zero_row = sb("zero_row", [P, D])
        t_exp = sb("t_exp", [P, NT])
        t_expi = sb("t_expi", [P, NT], I32)
        sid = sb("sid", [P, COLS], I32)
        meta_cw = sb("meta_cw", [P, COLS])
        junk8 = [sb(f"junk8_{s}", [P, SUB * E]) for s in range(2)]
        gid = [sb(f"gid{s}", [P, SUB], I32) for s in range(2)]
        aid = [sb(f"aid{s}", [P, SUB], I32) for s in range(2)]

        xT_sb = [A16[:, 6 * 4096 + 1536 * s:6 * 4096 + 1536 * (s + 1)] for s in range(2)]
        XT = 7 * 2048
        x64 = [A[:, XT + 768 * s:XT + 768 * (s + 1)] for s in range(2)]
        GE = TILES * E
        assert XT + 4 * GE <= OH and 3 * GE <= 2048
        g_log, g_ex, sel1, sel2 = [A[:, XT + GE * n:XT + GE * (n + 1)] for n in range(4)]
        selS, g_t, posf = [A[:, 7 * WEXP + GE * n:7 * WEXP + GE * (n + 1)] for n in range(3)]
        cnt, incl = g_ex, g_log
        gat = [0]

        def gs(n):
            gat[0] += n
            assert gat[0] <= CHUNK
            return B[:, gat[0] - n:gat[0]]

        zero57, mx, sm, pfa, pfb = [gs(TILES) for _ in range(5)]
        lo2 = gs(2 * TILES).rearrange("p (w j) -> p w j", w=2)
        hi2 = gs(2 * TILES).rearrange("p (w j) -> p w j", w=2)
        tot, pd, inc8, off, z8 = [gs(E) for _ in range(5)]
        pdi, pdj = [gs(E).bitcast(I32) for _ in range(2)]
        pint, lint = [gs(TILES).bitcast(I32) for _ in range(2)]
        slot_id, vz = gs(P), gs(P)

        at = [WORK]

        def work(n):
            at[0] += n
            assert at[0] <= ARENA
            return at[0] - n

        xs = [A16[:, 2 * a:2 * a + 2 * SUB * D] for a in (work(SUB * D), work(SUB * D))]
        xhl = [A16[:, 2 * a:2 * a + 2 * SUB * D] for a in (work(SUB * D), work(SUB * D))]
        xhi = [a[:, 0:SUB * D] for a in xhl]
        xlo = [a[:, SUB * D:2 * SUB * D] for a in xhl]
        hg_at = work(SUB * HID)
        hg = [A[:, hg_at + 512 * q:hg_at + 512 * (q + 1)] for q in range(4)]
        hh_at = [work(SUB * HID) for _ in range(2)]
        hhi = [A16[:, 2 * a:2 * a + SUB * HID] for a in hh_at]
        hlo = [A16[:, 2 * a + SUB * HID:2 * a + 2 * SUB * HID] for a in hh_at]
        ys = [A[:, a:a + SUB * D] for a in (work(SUB * D), work(SUB * D))]
        b2_at = work(E * D)
        HOT = 2 * BATCH * P
        hot_lo = [A[:, hg_at + HOT * s:hg_at + HOT * (s + 1)] for s in range(3)]
        hot_hi = [A[:, hg_at + HOT * (3 + s):hg_at + HOT * (4 + s)] for s in range(3)]
        cwg = [A[:, a:a + SUB * E] for a in (work(SUB * E), work(SUB * E))]

        PS = ctx.enter_context(nc.psum_tensor("PS", [P, 8 * 512], F32))

        PS16 = PS[:, :].bitcast(F16)

        def bank(b, n=512, o=0):
            return PS[:, 512 * b + o:512 * b + o + n]

        names = """const_loaded patch_const_loaded s4_loaded ids_loaded gate_const_loaded
            patch_done h_patch kf_zero kf_ready kfT_psum kfT_ready toep_done toep_ready s4_step ca_ready s10_step
            idx_ready masks_ready e_ready eT_psum eT_ready text_done h_text lnp_step xn_ready text_step
            conv_done silu_done h1_ready early_stats ln2_step var2_ready std2_ready
            rstd2_ready x64_ready xhi_ready xhi_dve row_ready
            xT_psum xT_ready gate_done rows_dumped cw_ready cw_dumped
            exp_in exp_out wg_step wg_ready gate_step sel_ready ranks_done lo_split lo_diff lo_sq lo_ready
            hi_ready hot_used map_done
            prefill_done zero_ready zero_rows slots_ready
            w_hi w_scaled w_free_pool w_free_dve
            b2_loaded y_biased xt_done x_split gelu_done mm1_done h_hi h_split mm2_done y_done
            slot_free gid_ready aid_ready dve_tick pool_tick vart_ready rstdt_ready varp_ready rstdp_ready
            vepst vepsp expo_ready""".split()
        S = {n: sem(n) for n in names}
        toep_copied = [sem(f"toep_copied{n}") for n in range(4)]
        patch_loaded = [sem(f"patch_loaded{s}") for s in range(2)]
        gathered = [sem(f"gathered{s}") for s in range(3)]
        w_loaded = [sem(f"w_loaded{s}") for s in range(3)]
        row_gathered = [[sem(f"row_gathered{s}{u}") for u in range(SUB)] for s in range(2)]
        cw_gathered = [[sem(f"cw_gathered{s}{u}") for u in range(SUB)] for s in range(2)]
        added = [sem(f"added{u}") for u in range(SUB)]

        block = ctx.enter_context(nc.Block())

        N_S4, N_PC, N_CONST, N_GC = 2, 3, 5, 9
        TRIPLES2 = TILES // 3
        LN_CHUNKS = {10: CONV_CHUNKS}
        BATCHES = TILES // BATCH

        def chunk_at(n):
            return 4096 * PIECES[n // 2] + CHUNK * (n % 2)

        BOUNDS = [0, 9, 27, 57]
        GROUPS = 3
        TRIPLES = TT // 3

        def toeplitz_share(k):
            return range(3 * k, min(3 * (k + 1), L // 2))

        @block.sync
        def _(sp):
            sp.dma_start(prm_sb, prm).then_inc(S["s4_loaded"], 16)
            sp.dma_start(ids_sb[:, :], ids).then_inc(S["ids_loaded"], 16)
            sp.dma_start(zc_sb, zc).then_inc(S["s4_loaded"], 16)
            sp.dma_start(B[:, 0:KC * D], Wp).then_inc(S["patch_const_loaded"], 16)
            sp.dma_start(pos_sb, posrows).then_inc(S["patch_const_loaded"], 16)
            sp.dma_start(psel, patsel).then_inc(S["patch_const_loaded"], 16)
            for s in range(2):
                sp.dma_start(xP_sb[s], xP[s * P:(s + 1) * P, :]).then_inc(patch_loaded[s], 16)
            with sp.Fori(1, PT // 2) as i:
                for s in range(2):
                    sp.wait_ge(S["patch_done"], 2 * i + s - 1)
                    sp.dma_start(xP_sb[s], xP[bass.ds((2 * i + s) * P, P), :]).then_inc(patch_loaded[s], 16)
            sp.wait_ge(S["zero_ready"], 1)
            sp.dma_start(out[TOKENS:TOKENS + P, :], zero_row[:, :]).then_inc(S["zero_rows"], 16)
            sp.dma_start(rows[TOKENS:TOKENS + P, :], zero_row[:, :].bitcast(F16)).then_inc(S["zero_rows"], 16)
            sp.dma_start(cws[TOKENS:TOKENS + P, :], zero_row[:, 0:E]).then_inc(S["zero_rows"], 16)
            quarter = L * D // 4
            sp.wait_ge(S["toep_ready"], L // 2)
            for n in range(4):
                o = OT + quarter * n
                sp.dma_start(A[64:128, o:o + quarter], A[0:64, o:o + quarter]).then_inc(toep_copied[n], 16)
            sp.wait_ge(S["text_done"], TRIPLES)
            for n in range(CHUNKS):
                if n == CHUNKS - 4:
                    sp.wait_ge(S["rows_dumped"], 16 * GROUPS)
                    sp.dma_start(A[:, b2_at:b2_at + E * D], b2d).then_inc(S["b2_loaded"], 16)
                m = n - 3
                if m >= POOL_CHUNKS:
                    sp.wait_ge(S["w_free_dve"], m - POOL_CHUNKS + 1)
                elif m >= 0:
                    sp.wait_ge(S["w_free_pool"], m + 1)
                piece, c = PIECES[n // 2], n % 2
                sp.dma_start(stage[n % 3], wts[piece * P:(piece + 1) * P, CHUNK * c:CHUNK * (c + 1)])\
                    .then_inc(w_loaded[n % 3], 16)

        @block.gpsimd
        def _(pool):
            nc.gpsimd.memset(eps3[:, :], EPS)
            nc.gpsimd.memset(expo[:, :], -0.5).then_inc(S["expo_ready"], 1)
            pool.wait_ge(S["expo_ready"], 1)
            pool.wait_ge(S["idx_ready"], 1)
            for n in range(TT):
                s = n % 3
                if n >= 3:
                    pool.wait_ge(gathered[s], 16 * (n // 3))
                pool.indirect_dma_start(H3[:, PT + n, :], None, table,
                                        bass.IndirectOffsetOnAxis(ap=idx[:, n:n + 1], axis=0)).then_inc(gathered[s], 16)
            pool.wait_ge(S["ca_ready"], 1)
            ca_r, ca_i = b4[4:6]
            v10r, v10i = s3(vec[10]), s3(vec[11])
            g = Link(pool, S["s10_step"])
            tt = nc.gpsimd.tensor_tensor
            g.add(tt(p4[0], over_m(v10r), ca_r, ALU.mult))
            g.add(tt(p4[1], over_m(v10i), ca_i, ALU.mult))
            g.add(tt(p4[2], over_m(v10i), ca_r, ALU.mult))
            g(tt(p4[3], over_m(v10r), ca_i, ALU.mult))
            g.add(tt(p4[0], p4[0], p4[1], ALU.add))
            g(tt(p4[2], p4[2], p4[3], ALU.subtract))

            def inv_std(k, st, w):
                pool.wait_ge(S[f"var{w}_ready"], k + 1)
                var = mv[st][:, :].rearrange("p (s r) -> p s r", r=2)[:, :, 1]
                nc.gpsimd.tensor_tensor(veps[st][:, :], var, eps3[:, :], ALU.add).then_inc(S[f"veps{w}"], 1)
                pool.wait_ge(S[f"veps{w}"], k + 1)
                nc.gpsimd.tensor_tensor(rstd[st][:, :], veps[st][:, :], expo[:, :], ALU.pow)\
                    .then_inc(S[f"rstd{w}_ready"], 1)

            def masked(k, st, turned):
                if turned is not None:
                    pool.wait_ge(S["eT_psum"], turned)
                    pool.sem_inc(S["pool_tick"], 1)
                rows_ = A[:, bass.ds(3 * D * k + OH + PT * D, 3 * D)].rearrange("p (s d) -> p s d", d=D)[:, :, 0:64]
                m2 = MK[:, :, bass.ds(3 * k, 3)]
                for w in range(2):
                    last = nc.gpsimd.tensor_tensor(e3[st][:, :, w, :], rows_,
                                                   m2[:, 1 + w, :].unsqueeze(2).broadcast_to((P, 3, 64)), ALU.mult)
                last.then_inc(S["e_ready"], 1)

            pool.wait_ge(S["masks_ready"], 1)
            for s in range(3):
                pool.wait_ge(gathered[s], 16 * TRIPLES)
            masked(0, 0, None)
            masked(1, 1, None)
            with pool.Fori(0, (TRIPLES - 3) // 2) as i:
                for st in range(2):
                    masked(2 * i + st + 2, st, 2 * i + st + 1)
                    inv_std(2 * i + st, st, "t")
                inv_std(i, 2, "p")
            masked(TRIPLES - 1, 0, TRIPLES - 2)
            inv_std(TRIPLES - 3, 0, "t")
            inv_std(TRIPLES - 2, 1, "t")
            inv_std(PT // 3 - 1, 2, "p")
            inv_std(TRIPLES - 1, 0, "t")

            def weights_low(n):
                pool.wait_ge(S["w_hi"], n + 1)
                o = chunk_at(n)
                nc.gpsimd.tensor_tensor(A16[:, o + 2048:o + 2048 + CHUNK], stage[n % 3], A16[:, o:o + CHUNK], ALU.subtract)\
                    .then_inc(S["w_free_pool"], 1)

            for n in range(CONV_CHUNKS):
                weights_low(n)
            for k in range(TRIPLES2):
                pool.wait_ge(S["xhi_dve" if k % 2 else "xhi_ready"], k // 2 + 1)
                nc.gpsimd.tensor_tensor(X16[:, 3 * k:3 * k + 3, 1, :], x64[k % 2].rearrange("p (s d) -> p s d", d=D),
                                        X16[:, 3 * k:3 * k + 3, 0, :], ALU.subtract).then_inc(S["row_ready"], 1)
                if k - 2 in LN_CHUNKS:
                    weights_low(LN_CHUNKS[k - 2])
            for n in range(CONV_CHUNKS + len(LN_CHUNKS), POOL_CHUNKS):
                weights_low(n)

            def low_differences(b, s, used):
                if used is not None:
                    pool.wait_ge(S["hot_used"], used)
                    pool.sem_inc(S["pool_tick"], 1)
                nc.gpsimd.tensor_tensor(
                    hot_lo[s].rearrange("p (w j l) -> p w j l", w=2, j=BATCH),
                    iota16[:, :].unsqueeze(1).unsqueeze(1).broadcast_to((P, 2, BATCH, P)),
                    lo2[:, :, bass.ds(BATCH * b, BATCH)].unsqueeze(3).broadcast_to((P, 2, BATCH, P)),
                    ALU.subtract).then_inc(S["lo_diff"], 1)

            pool.wait_ge(S["lo_split"], 1)
            pool.wait_ge(S["rows_dumped"], 16 * GROUPS)
            low_differences(0, 0, None)
            low_differences(1, 1, None)
            low_differences(2, 2, None)
            with pool.Fori(1, BATCHES // 3) as i:
                for s in range(3):
                    low_differences(3 * i + s, s, 3 * i + s - 2)
            low_differences(BATCHES - 1, 0, BATCHES - 3)

            def gather(k, s, free):
                if free is not None:
                    pool.wait_ge(S["slot_free"], free)
                    pool.sem_inc(S["pool_tick"], 1)
                nc.gpsimd.tensor_copy(gid[s][:, :], sid[:, bass.ds(k * SUB, SUB)]).then_inc(S["gid_ready"], 1)
                pool.wait_ge(S["gid_ready"], k + 1)
                pool.sem_inc(S["pool_tick"], 1)
                for u in range(SUB):
                    at_ = bass.IndirectOffsetOnAxis(ap=gid[s][:, u:u + 1], axis=0)
                    pool.indirect_dma_start(xs[s][:, 2 * D * u:2 * D * (u + 1)], None, rows, at_).then_inc(row_gathered[s][u], 16)
                    pool.indirect_dma_start(cwg[s][:, E * u:E * (u + 1)], None, cws, at_).then_inc(cw_gathered[s][u], 16)

            def add_rows(k, s, before):
                pool.wait_ge(S["y_done"], k + 1)
                if before is not None:
                    pool.wait_ge(added[1], before)
                pool.sem_inc(S["pool_tick"], 1)
                nc.gpsimd.tensor_copy(aid[s][:, :], sid[:, bass.ds(k * SUB, SUB)]).then_inc(S["aid_ready"], 1)
                pool.wait_ge(S["aid_ready"], k + 1)
                pool.sem_inc(S["pool_tick"], 1)
                for u in range(SUB):
                    if u:
                        pool.wait_ge(added[0], 16 if before is None else before + 16)
                        pool.sem_inc(S["pool_tick"], 1)
                    pool.indirect_dma_start(out, bass.IndirectOffsetOnAxis(ap=aid[s][:, u:u + 1], axis=0),
                                            ys[s][:, D * u:D * (u + 1)], None, compute_op=ALU.add).then_inc(added[u], 16)

            pool.wait_ge(S["slots_ready"], 1)
            pool.wait_ge(S["zero_rows"], 48)
            pool.wait_ge(S["rows_dumped"], 16 * GROUPS)
            pool.wait_ge(S["cw_dumped"], 16)
            pool.wait_ge(S["prefill_done"], 16)
            gather(0, 0, None)
            gather(1, 1, None)
            gather(2, 0, 1)
            gather(3, 1, 2)
            add_rows(0, 0, None)
            with pool.Fori(0, NT // 2 - 2) as i:
                for s in range(2):
                    k = 2 * i + s + 1
                    gather(k + 3, s, k + 2)
                    add_rows(k, 1 - s, 16 * k)
            for k in range(NT - 3, NT):
                add_rows(k, k % 2, 16 * k)
            for u in range(SUB):
                pool.wait_ge(added[u], 16 * NT)

        @block.scalar
        def _(act):
            act.wait_ge(S["s4_loaded"], 16 * N_S4)
            nc.scalar.activation(prm_sb[:, :, 0:1 + NS], prm_sb[:, :, 0:1 + NS], ACT.Exp).then_inc(S["s4_step"], 1)
            for dst, src in ((basis_sb[:, :], basis), (ident[:, :], ident_d), (P12_sb[:, :], P12), (csel[:, :], clssel),
                             (crow[:, :], clsrows)):
                act.dma_start(dst, src).then_inc(S["const_loaded"], 16)
            for dst, src in ((tri[:, :], tri_d), (wg_sb[:, :], wg), (b1_sb[:, :], b1T), (iota_sb[:, :], iota8),
                             (rev_sb[:, :], rev8), (pad_row[:, :], pad_row_d), (iota16[:, :], iota16_d),
                             (rowid1[:, :], rowid1_d), (kcol_sb[:, :], kcol)):
                act.dma_start(dst, src).then_inc(S["gate_const_loaded"], 16)
            with act.Fori(0, PT // 2) as i:
                for s in range(2):
                    act.wait_ge(S["patch_done"], 2 * i + s + 1)
                    nc.scalar.activation(h_tile(2 * i + s), bank(s, D), ACT.Copy).then_inc(S["h_patch"], 1)
            def text_copy(k):
                act.wait_ge(S["eT_psum"], k + 1)
                if k >= 2:
                    act.wait_ge(S["text_done"], k - 1)
                st = k % 2
                nc.scalar.activation(eT[:, 3 * P * st:3 * P * (st + 1)], bank(st, 3 * P), ACT.Copy)\
                    .then_inc(S["eT_ready"], 1)

            def toeplitz_copy(n):
                act.wait_ge(S["toep_done"], n + 1)
                nc.scalar.activation(Tz[0:64, :, 2 * n:2 * n + 2], PS[0:64, 512 * (6 + n % 2):512 * (7 + n % 2)]
                                     .rearrange("p (t h) -> p h t", t=2), ACT.Copy).then_inc(S["toep_ready"], 1)

            text_copy(0)
            text_copy(1)
            act.wait_ge(S["kfT_psum"], 1)
            nc.scalar.activation(kfT[:, :], PS[:, 3072:3072 + D], ACT.Copy).then_inc(S["kfT_ready"], 1)
            for k in range(TRIPLES):
                if 0 < k < TRIPLES - 1:
                    text_copy(k + 1)
                for n in toeplitz_share(k):
                    toeplitz_copy(n)

            def weights_high(n):
                act.wait_ge(w_loaded[n % 3], 16 * (n // 3) + 16)
                o = chunk_at(n)
                if n < POOL_CHUNKS:
                    nc.scalar.activation(stage[n % 3], stage[n % 3], ACT.Copy, scale=WSCALE).then_inc(S["w_scaled"], 1)
                    act.wait_ge(S["w_scaled"], n + 1)
                    nc.scalar.activation(A16[:, o:o + CHUNK], stage[n % 3], ACT.Copy).then_inc(S["w_hi"], 1)
                else:
                    nc.scalar.activation(A16[:, o:o + CHUNK], stage[n % 3], ACT.Copy, scale=WSCALE)\
                        .then_inc(S["w_hi"], 1)

            for n in range(32):
                act.wait_ge(S["conv_done"], n + 1)
                if n >= 2:
                    act.wait_ge(S["h1_ready"], n - 1)
                nc.scalar.activation(silu_sb[n % 2], bank(4 + n % 4, 8 * TILES), ACT.Silu)\
                    .then_inc(S["silu_done"], 1)
                if n % 2 == 1 and 3 <= n <= 2 * CONV_CHUNKS:
                    weights_high(n // 2 - 1)
            weights_high(CONV_CHUNKS - 1)
            act.wait_ge(S["h1_ready"], 32)
            act.dma_start(out[0:TOKENS, :].rearrange("(p j) d -> p j d", j=TILES), H3).then_inc(S["prefill_done"], 16)

            def std_group(g):
                act.wait_ge(S["var2_ready"], g + 1)
                var = mv2[:, 2 * BOUNDS[g]:2 * BOUNDS[g + 1]].rearrange("p (j r) -> p j r", r=2)[:, :, 1]
                nc.scalar.activation(std2[:, BOUNDS[g]:BOUNDS[g + 1]], var, ACT.Sqrt, bias=eps1[:, :])\
                    .then_inc(S["std2_ready"], 1)

            def gate_copy(k):
                act.wait_ge(S["xT_psum"], k + 1)
                if k >= 2:
                    act.wait_ge(S["gate_done"], k - 1)
                s = k % 2
                nc.scalar.activation(xT_sb[s], PS16[:, 2048 * s:2048 * s + 1536], ACT.Copy).then_inc(S["xT_ready"], 1)

            def rows_high(k):
                if k % 2:
                    return
                act.wait_ge(S["x64_ready"], k + 1)
                nc.scalar.activation(X16[:, 3 * k:3 * k + 3, 0, :], x64[k % 2].rearrange("p (s d) -> p s d", d=D), ACT.Copy)\
                    .then_inc(S["xhi_ready"], 1)

            rows3 = rows[0:TOKENS, :].rearrange("(p j) d -> p j d", j=TILES)
            std_group(0)
            std_group(1)
            rows_high(0)
            rows_high(1)
            for k in range(TRIPLES2):
                if k == 3:
                    std_group(2)
                if k + 2 < TRIPLES2:
                    rows_high(k + 2)
                gate_copy(k)
                if k in LN_CHUNKS:
                    act.wait_ge(S["prefill_done"], 16)
                    act.wait_ge(S["x64_ready"], 6)
                    weights_high(LN_CHUNKS[k])
                for g in range(GROUPS):
                    if 3 * (k + 1) == BOUNDS[g + 1]:
                        act.wait_ge(S["row_ready"], k + 1)
                        act.dma_start(rows3[:, BOUNDS[g]:BOUNDS[g + 1], :],
                                      X16[:, BOUNDS[g]:BOUNDS[g + 1], :, :].rearrange("p j w r -> p j (w r)"))\
                            .then_inc(S["rows_dumped"], 16)
            act.wait_ge(S["exp_in"], 1)
            nc.scalar.activation(g_ex, g_log, ACT.Exp, scale=1.0 / (WSCALE * XSCALE)).then_inc(S["exp_out"], 1)
            act.wait_ge(S["prefill_done"], 16)
            act.wait_ge(S["x64_ready"], TRIPLES2)
            act.wait_ge(S["gate_done"], TRIPLES2)
            for n in range(CONV_CHUNKS + len(LN_CHUNKS), POOL_CHUNKS):
                weights_high(n)
            act.wait_ge(S["cw_ready"], 1)
            act.dma_start(cws[0:TOKENS, :].rearrange("(p j) e -> p (j e)", j=TILES), posf).then_inc(S["cw_dumped"], 16)
            act.wait_ge(S["rows_dumped"], 16 * GROUPS)
            act.wait_ge(S["cw_dumped"], 16)
            act.wait_ge(S["lo_split"], 1)
            for n in range(POOL_CHUNKS, MAP_CHUNKS):
                weights_high(n)

            def low_hots(b, s):
                act.wait_ge(S["lo_diff"], b + 1)
                nc.scalar.activation(hot_lo[s], hot_lo[s], ACT.Square).then_inc(S["lo_sq"], 1)
                act.wait_ge(S["lo_sq"], b + 1)
                nc.scalar.activation(hot_lo[s], hot_lo[s], ACT.Relu, scale=-1.0, bias=ones[:, 0:1])\
                    .then_inc(S["lo_ready"], 1)

            with act.Fori(0, BATCHES // 3) as i:
                for s in range(3):
                    low_hots(3 * i + s, s)
            low_hots(BATCHES - 1, 0)
            for n in range(MAP_CHUNKS, CHUNKS):
                weights_high(n)

            def gelu(k, first):
                e = act.value_load(t_expi[0:1, bass.ds(k, 1)], min_val=0, max_val=E - 1)
                for q in range(4):
                    act.wait_ge(S["mm1_done"], 4 * k + q + 1)
                    if not first:
                        act.wait_ge(S["h_split"], 4 * k + q - 3)
                    for c in range(2):
                        nc.scalar.activation(hg[q][:, 256 * c:256 * (c + 1)], bank(2 + q, 256, 256 * c), ACT.Gelu,
                                             bias=b1_sb[:, bass.ds(e * FCH + (2 * q + c), 1)],
                                             scale=1.0 / (WSCALE * XSCALE)).then_inc(S["gelu_done"], 1)

            act.wait_ge(S["slots_ready"], 1)
            gelu(0, True)
            with act.Fori(1, NT) as i:
                gelu(i, False)

        @block.vector
        def _(dve):
            v = nc.vector

            v.memset(ones[:, :], 1.0)
            v.memset(eps1[:, :], EPS)
            v.memset(zero_row[:, :], 0.0).then_inc(S["zero_ready"], 1)
            dve.wait_ge(S["ids_loaded"], 16)
            t = Link(dve, S["text_step"])
            t(v.tensor_copy(ids_f, ids_sb[:, :]))
            t(v.tensor_scalar(idx_f, ids_f, 0.0, float(VOCAB - 1), ALU.max, ALU.min))
            v.tensor_copy(idx[:, :], idx_f).then_inc(S["idx_ready"], 1)
            root = float(D) ** 0.5
            t.add(v.tensor_scalar(mk0, ids_f, float(CUT0), root, ALU.is_lt, ALU.mult))
            t.add(v.tensor_scalar(mk1, ids_f, float(CUT0), root, ALU.is_ge, ALU.mult))
            t.add(v.tensor_scalar(mk2, ids_f, float(CUT1), root, ALU.is_ge, ALU.mult))
            t(v.tensor_scalar(mtmp, ids_f, 0.0, None, ALU.is_gt))
            t(v.tensor_tensor(mk[:, 0:TT], mk0, mtmp, ALU.mult))
            t(v.tensor_scalar(mtmp, ids_f, float(CUT1), None, ALU.is_lt))
            t(v.tensor_tensor(mk[:, TT:2 * TT], mk1, mtmp, ALU.mult))
            t(v.tensor_scalar(mtmp, ids_f, float(VOCAB), None, ALU.is_lt))
            t(v.tensor_tensor(mk[:, 2 * TT:3 * TT], mk2, mtmp, ALU.mult))
            dve.sem_inc(S["masks_ready"], 1)

            v.memset(KF, 0.0).then_inc(S["kf_zero"], 1)

            dve.wait_ge(S["s4_loaded"], 16 * N_S4)
            q = Link(dve, S["s4_step"], 0)
            q.n = 1
            q.sync()

            def pair(at, part):
                return prm_sb[:, :, at:at + 2 * NS].rearrange("p c (n r) -> p c n r", r=2)[:, :, :, part]

            dt = prm_sb[:, :, 0:1].broadcast_to((P, 2, NS))
            ew, wim = prm_sb[:, :, 1:1 + NS], prm_sb[:, :, 1 + NS:1 + 2 * NS]
            o = 1 + 2 * NS
            Br, Bi, Pr, Pi, Cr, Ci = [pair(o + 2 * NS * n, part) for n in range(3) for part in range(2)]
            nwr, wi, bdr, bdi, pdr, pdi_ = [s3(a) for a in vec[0:6]]
            v00r, v00i, v01r, v01i, v10r, v10i, v11 = [s3(a) for a in vec[6:13]]
            t1, t2, t3 = [s3(a) for a in vec[13:16]]
            mul, add, sub = ALU.mult, ALU.add, ALU.subtract
            q.add(v.tensor_tensor(nwr, ew, dt, mul))
            q.add(v.tensor_tensor(wi, wim, dt, mul))
            q.add(v.tensor_tensor(bdr, Br, dt, mul))
            q.add(v.tensor_tensor(bdi, Bi, dt, mul))
            q.add(v.tensor_tensor(pdr, Pr, dt, mul))
            q(v.tensor_tensor(pdi_, Pi, dt, mul))

            def product(outr, outi, ar, ai, br, bi, conj):
                q.add(v.tensor_tensor(t1, ar, br, mul))
                q(v.tensor_tensor(t2, ai, bi, mul))
                q.add(v.tensor_tensor(outr, t1, t2, add if conj else sub))
                q.add(v.tensor_tensor(t3, ai, br, mul))
                q(v.tensor_tensor(outi, ar, bi, mul))
                q(v.tensor_tensor(outi, t3, outi, sub if conj else add))

            product(v00r, v00i, bdr, bdi, Cr, Ci, False)
            product(v01r, v01i, bdr, bdi, Pr, Pi, True)
            product(v10r, v10i, pdr, pdi_, Cr, Ci, False)
            q.add(v.tensor_tensor(t1, pdr, Pr, mul))
            q(v.tensor_tensor(t2, pdi_, Pi, mul))
            q(v.tensor_tensor(v11, t1, t2, add))

            den_r, den_i, g1, g2, ca_r, ca_i = b4

            def const(k):
                return zc_sb[:, k * M:(k + 1) * M].unsqueeze(1).unsqueeze(3).broadcast_to((P, 2, M, NS))

            ar, ai, br, bi = [const(k) for k in range(4)]
            q.add(v.tensor_tensor(g1, over_m(nwr), br, mul))
            q(v.tensor_tensor(g2, over_m(wi), bi, mul))
            q(v.tensor_tensor(g1, g1, g2, add))
            q.add(v.tensor_tensor(den_r, g1, ar, add))
            q(v.tensor_tensor(g2, over_m(nwr), bi, mul))
            q(v.tensor_tensor(den_i, over_m(wi), br, mul))
            q(v.tensor_tensor(g2, g2, den_i, sub))
            q(v.tensor_tensor(den_i, g2, ai, add))
            q.add(v.tensor_tensor(g1, den_r, den_r, mul))
            q(v.tensor_tensor(g2, den_i, den_i, mul))
            q(v.tensor_tensor(g1, g1, g2, add))
            q(v.reciprocal(big[3], big[2]))
            q.add(v.tensor_tensor(ca_r, den_r, g2, mul))
            q(v.tensor_tensor(ca_i, den_i, g2, mul))
            f3 = [a.rearrange("p (c m) -> p c m", c=2) for a in frq]
            s00r, s00i, s01r, s01i, s10r, s10i, s11r, s11i = f3[0:8]
            dve.sem_inc(S["ca_ready"], 1)
            for outr, outi, vr, vi in ((s00r, s00i, v00r, v00i), (s01r, s01i, v01r, v01i)):
                q.add(v.tensor_tensor(g1, over_m(vr), ca_r, mul))
                q.add(v.tensor_tensor(g2, over_m(vi), ca_i, mul))
                q.add(v.tensor_tensor(den_r, over_m(vi), ca_r, mul))
                q(v.tensor_tensor(den_i, over_m(vr), ca_i, mul))
                q.add(v.tensor_tensor(g1, g1, g2, add))
                q(v.tensor_tensor(den_r, den_r, den_i, sub))
                q.add(v.tensor_reduce(outr, g1, AX.X, add))
                q(v.tensor_reduce(outi, den_r, AX.X, add))
            q.add(v.tensor_tensor(g1, over_m(v11), ca_r, mul))
            q(v.tensor_tensor(g2, over_m(v11), ca_i, mul))
            q.add(v.tensor_reduce(s11r, g1, AX.X, add))
            q(v.tensor_reduce(f3[19], g2, AX.X, add))
            q(v.tensor_scalar(s11i, f3[19], -1.0, None, mul))
            dve.wait_ge(S["s10_step"], 6)
            q.add(v.tensor_reduce(s10r, p4[0], AX.X, add))
            q(v.tensor_reduce(s10i, p4[2], AX.X, add))

            b3r = zc_sb[:, 2 * M:3 * M].unsqueeze(1).broadcast_to((P, 2, M))
            b3i = zc_sb[:, 3 * M:4 * M].unsqueeze(1).broadcast_to((P, 2, M))
            u1, u2, nr, ni, mr, mi, dr, di, rr, zr, zi = f3[8:19]

            def cmul(outr, outi, ar, ai, br, bi):
                q.add(v.tensor_tensor(u1, ar, br, mul))
                q(v.tensor_tensor(u2, ai, bi, mul))
                q.add(v.tensor_tensor(outr, u1, u2, sub))
                q.add(v.tensor_tensor(f3[19], ar, bi, mul))
                q(v.tensor_tensor(outi, ai, br, mul))
                q(v.tensor_tensor(outi, f3[19], outi, add))

            cmul(nr, ni, s01r, s01i, s10r, s10i)
            cmul(mr, mi, nr, ni, b3r, b3i)
            cmul(dr, di, s11r, s11i, b3r, b3i)
            q(v.tensor_scalar(dr, dr, 1.0, None, add))
            q.add(v.tensor_tensor(u1, dr, dr, mul))
            q(v.tensor_tensor(u2, di, di, mul))
            q(v.tensor_tensor(u1, u1, u2, add))
            q(v.reciprocal(frq[8 + 8], frq[8]))
            q(v.tensor_scalar(di, di, -1.0, None, mul))
            cmul(zr, zi, mr, mi, dr, di)
            q.add(v.tensor_tensor(zr, zr, rr, mul))
            q(v.tensor_tensor(zi, zi, rr, mul))
            dve.wait_ge(S["kf_zero"], 1)
            q.add(v.tensor_tensor(KF[:, :, 0:M], s00r, zr, sub))
            q.add(v.tensor_tensor(KF[:, :, M:2 * M], s00i, zi, sub))
            q(v.tensor_copy(KF[:, :, 2 * M:KROWS], prm_sb[:, :, PRM - 1:PRM]))
            dve.sem_inc(S["kf_ready"], 1)

            def stats3(k, st, link, var_ready):
                dve.sem_inc(S["dve_tick"], 1)
                for s in range(3):
                    link.add(v.bn_stats(stats[st][:, 6 * s:6 * s + 6], h_tile(3 * k + s)))
                link.sync()
                dve.sem_inc(S["dve_tick"], 1)
                for s in range(3):
                    last = v.bn_aggr(mv[st][:, 2 * s:2 * s + 2], stats[st][:, 6 * s:6 * s + 6])
                last.then_inc(S[var_ready], 1)

            def norm3(k, st, count, rstd_ready, signal):
                dve.wait_ge(S[rstd_ready], count + 1)
                for s in range(3):
                    v.tensor_scalar(x_tile(3 * k + s), h_tile(3 * k + s), mv[st][:, 2 * s:2 * s + 1],
                                    rstd[st][:, s:s + 1], ALU.subtract, ALU.mult).then_inc(S[signal], 1)

            def text3(i, st):
                dve.wait_ge(S["text_done"], i + 1)
                link = Link(dve, S["h_text"], 6 * i)
                for s in range(3):
                    n = 3 * i + s
                    link.add(v.scalar_tensor_tensor(out=h_tile(PT + n), in0=h_tile(PT + n), scalar=mk[:, bass.ds(n, 1)],
                                                    in1=text_psum(st, s), op0=ALU.mult, op1=ALU.add))
                link.sync()
                stats3(PT // 3 + i, st, link, "vart_ready")

            def text_norm(i, st):
                norm3(PT // 3 + i, st, i, "rstdt_ready", "xn_ready")

            def patch_stats(i):
                dve.wait_ge(S["h_patch"], 3 * i + 3)
                stats3(i, 2, Link(dve, S["lnp_step"], 3 * i), "varp_ready")

            def text_psum(st, s):
                return bank(2 + 2 * st, D, D * s) if s < 2 else bank(3 + 2 * st, D)

            n3 = TT // 3
            with dve.Fori(0, (n3 - 3) // 2) as i:
                for st in range(2):
                    text3(2 * i + st, st)
                patch_stats(i)
                for st in range(2):
                    text_norm(2 * i + st, st)
                norm3(i, 2, i, "rstdp_ready", "xn_ready")
            text3(n3 - 3, 0)
            text3(n3 - 2, 1)
            patch_stats(PT // 3 - 1)
            text_norm(n3 - 3, 0)
            text_norm(n3 - 2, 1)
            norm3(PT // 3 - 1, 2, PT // 3 - 1, "rstdp_ready", "xn_ready")
            text3(n3 - 1, 0)
            text_norm(n3 - 1, 0)

            w_ = Link(dve, S["wg_step"])
            dve.wait_ge(S["const_loaded"], 16 * N_CONST)
            dve.wait_ge(S["gate_const_loaded"], 16 * N_GC)
            w_.add(v.tensor_copy(ident16[:, :], ident[:, :]))
            w_(v.tensor_scalar(wgs[:, :], wg_sb[:, :], WSCALE, None, ALU.mult))
            w_(v.tensor_copy(wg_hi[:, :], wgs[:, :]))
            v.tensor_tensor(wg_lo[:, :], wgs[:, :], wg_hi[:, :], ALU.subtract).then_inc(S["wg_ready"], 1)

            for n in range(32):
                dve.wait_ge(S["silu_done"], n + 1)
                hv = H3[:, :, 8 * n:8 * n + 8]
                v.tensor_tensor(hv, hv, silu_sb[n % 2].rearrange("p (e b) -> p b e", b=TILES), ALU.add)\
                    .then_inc(S["h1_ready"], 1)
                first = EARLY // 8 + 1
                if n >= first:
                    dve.wait_ge(S["h1_ready"], EARLY // 8)
                    for k in range(EARLY_TILES * (n - first), min(EARLY_TILES * (n - first + 1), TILES)):
                        v.bn_stats(stats_all[:, 12 * k:12 * k + 6], H3[:, k, 0:EARLY]).then_inc(S["early_stats"], 1)
            dve.wait_ge(S["h1_ready"], 32)

            def group_stats(g):
                for k in range(BOUNDS[g], BOUNDS[g + 1]):
                    v.bn_stats(stats_all[:, 12 * k + 6:12 * k + 12], H3[:, k, EARLY:D]).then_inc(S["ln2_step"], 1)
                    if k > BOUNDS[g]:
                        group_aggr(k - 1)
                group_aggr(BOUNDS[g + 1] - 1, True)

            def group_aggr(k, last=False):
                dve.wait_ge(S["ln2_step"], 2 * k + 1)
                ins = v.bn_aggr(mv2[:, 2 * k:2 * k + 2], stats_all[:, 12 * k:12 * k + 12])
                ins.then_inc(S["ln2_step"], 1)
                if last:
                    dve.wait_ge(S["ln2_step"], 2 * k + 2)
                    dve.sem_inc(S["var2_ready"], 1)

            def group_rows(g):
                dve.wait_ge(S["std2_ready"], g + 1)
                part = std2[:, BOUNDS[g]:BOUNDS[g + 1]]
                v.reciprocal(part, part).then_inc(S["rstd2_ready"], 1)
                dve.wait_ge(S["rstd2_ready"], 2 * g + 1)
                v.tensor_scalar(part, part, XSCALE, None, ALU.mult).then_inc(S["rstd2_ready"], 1)
                dve.wait_ge(S["rstd2_ready"], 2 * g + 2)
                for k in range(BOUNDS[g] // 3, BOUNDS[g + 1] // 3):
                    if k >= 2:
                        dve.wait_ge(S["row_ready"], k - 1)
                    for s in range(3):
                        j = 3 * k + s
                        last = v.tensor_scalar(x64[k % 2][:, D * s:D * (s + 1)], H3[:, j, :], mv2[:, 2 * j:2 * j + 1],
                                               std2[:, j:j + 1], ALU.subtract, ALU.mult)
                    last.then_inc(S["x64_ready"], 1)
                    if k % 2:
                        dve.wait_ge(S["x64_ready"], k + 1)
                        v.tensor_copy(X16[:, 3 * k:3 * k + 3, 0, :], x64[1].rearrange("p (s d) -> p s d", d=D))\
                            .then_inc(S["xhi_dve"], 1)

            dve.wait_ge(S["early_stats"], TILES)
            group_stats(0)
            group_stats(1)
            group_rows(0)
            group_stats(2)
            group_rows(1)
            group_rows(2)

            def j3(a):
                return a.rearrange("p (j e) -> p j e", e=E)

            def per_tile(a):
                return a.unsqueeze(2).broadcast_to((P, TILES, E))

            def per_expert(a):
                return a.unsqueeze(1).broadcast_to((P, TILES, E))

            g = Link(dve, S["gate_step"])
            dve.wait_ge(S["gate_const_loaded"], 16 * N_GC)
            dve.wait_ge(S["prefill_done"], 16)
            dve.wait_ge(S["row_ready"], TRIPLES2)
            dve.wait_ge(S["gate_done"], TILES // 3)
            logits = bank(7, GE)
            g.add(v.memset(zero57, 0.0))
            g(v.tensor_reduce(mx, j3(logits), AX.X, ALU.max))
            v.tensor_tensor(j3(g_log), j3(logits), per_tile(mx), ALU.subtract).then_inc(S["exp_in"], 1)
            dve.wait_ge(S["exp_out"], 1)
            g(v.tensor_reduce(sm, j3(g_ex), AX.X, ALU.add))
            g(v.reciprocal(sm, sm))
            g(v.tensor_tensor(j3(g_ex), j3(g_ex), per_tile(sm), ALU.mult))

            def first_max(scores, sel):
                g(v.tensor_reduce(mx, j3(scores), AX.X, ALU.max))
                g(v.tensor_tensor(j3(g_t), j3(scores), per_tile(mx), ALU.is_equal))
                g(v.tensor_tensor(j3(g_t), j3(g_t), per_expert(rev_sb[:, :]), ALU.mult))
                g(v.tensor_reduce(mx, j3(g_t), AX.X, ALU.max))
                g(v.tensor_tensor(j3(sel), j3(g_t), per_tile(mx), ALU.is_equal))

            first_max(g_ex, sel1)
            g(v.scalar_tensor_tensor(out=g_log, in0=sel1, scalar=-2.0, in1=g_ex, op0=ALU.mult, op1=ALU.add))
            first_max(g_log, sel2)
            g(v.tensor_tensor(selS, sel1, sel2, ALU.add))
            dve.sem_inc(S["sel_ready"], 1)
            g(v.tensor_tensor(posf, g_ex, selS, ALU.mult))
            dve.sem_inc(S["cw_ready"], 1)
            dve.wait_ge(S["ranks_done"], 1)
            g(v.tensor_copy(cnt, bank(1, GE)))
            for e in range(E):
                g.add(v.tensor_tensor_scan(j3(incl)[:, :, e], j3(cnt)[:, :, e], zero57, 0.0, ALU.add, ALU.add))
            g.sync()
            g(v.tensor_copy(tot, j3(incl)[:, TILES - 1, :]))
            g(v.tensor_tensor(incl, incl, cnt, ALU.subtract))
            g.add(v.memset(z8, 0.0))
            g(v.tensor_scalar(pdi, tot, float(SUB * P - 1), None, ALU.add))
            g(v.tensor_scalar(pdj, pdi, 8, 8, ALU.arith_shift_right, ALU.logical_shift_left))
            g(v.tensor_copy(pd, pdj))
            g(v.tensor_tensor_scan(inc8, pd, z8, 0.0, ALU.add, ALU.add))
            g(v.tensor_tensor(off, inc8, pd, ALU.subtract))
            g(v.tensor_tensor(cnt, bank(0, GE), incl, ALU.add))
            g(v.tensor_tensor(j3(cnt), j3(cnt), per_expert(off), ALU.add))
            g.add(v.tensor_tensor(g_t, cnt, sel1, ALU.mult))
            g(v.tensor_tensor(g_log, cnt, sel2, ALU.mult))
            g.add(v.tensor_reduce(pfa, j3(g_t), AX.X, ALU.add))
            g(v.tensor_reduce(pfb, j3(g_log), AX.X, ALU.add))
            for w, pf in enumerate((pfa, pfb)):
                g(v.tensor_copy(pint, pf))
                g.add(v.tensor_scalar(lint, pint, P - 1, None, ALU.bitwise_and))
                g(v.tensor_scalar(pint, pint, 7, None, ALU.arith_shift_right))
                g.add(v.tensor_copy(lo2[:, w, :], lint))
                g(v.tensor_copy(hi2[:, w, :], pint))
            dve.sem_inc(S["lo_split"], 1)
            dve.wait_ge(S["rows_dumped"], 16 * GROUPS)

            def high_hots(b, s, used):
                if used is not None:
                    dve.wait_ge(S["hot_used"], used)
                    dve.sem_inc(S["dve_tick"], 1)
                for w in range(2):
                    for u in range(BATCH):
                        o = P * (BATCH * w + u)
                        last = v.tensor_scalar(hot_hi[s][:, o:o + P], iota16[:, :], hi2[:, w, bass.ds(BATCH * b + u, 1)],
                                               rowid1[:, bass.ds(BATCH * b + u, 1)], ALU.is_equal, ALU.mult)
                last.then_inc(S["hi_ready"], 1)

            def weights_low(n):
                dve.wait_ge(S["w_hi"], n + 1)
                o = chunk_at(n)
                v.scalar_tensor_tensor(out=A16[:, o + 2048:o + 2048 + CHUNK], in0=stage[n % 3], scalar=WSCALE,
                                       in1=A16[:, o:o + CHUNK], op0=ALU.mult, op1=ALU.subtract)\
                    .then_inc(S["w_free_dve"], 1)

            high_hots(0, 0, None)
            high_hots(1, 1, None)
            high_hots(2, 2, None)
            for n in range(POOL_CHUNKS, MAP_CHUNKS):
                weights_low(n)
            with dve.Fori(1, BATCHES // 3) as i:
                for s in range(3):
                    high_hots(3 * i + s, s, 3 * i + s - 2)
            high_hots(BATCHES - 1, 0, BATCHES - 3)
            g(v.tensor_scalar(t_exp[:, :], kcol_sb[:, :], inc8[:, 0:1], None, ALU.is_ge))
            for e in range(1, E - 1):
                g(v.scalar_tensor_tensor(out=t_exp[:, :], in0=kcol_sb[:, :], scalar=inc8[:, e:e + 1],
                                         in1=t_exp[:, :], op0=ALU.is_ge, op1=ALU.add))
            g(v.tensor_copy(t_expi[:, :], t_exp[:, :]))
            dve.wait_ge(S["map_done"], 1)
            g(v.tensor_copy(slot_id, bank(2, P)))
            g(v.tensor_scalar(vz, slot_id, 0.0, pad_row[:, 0:1], ALU.is_equal, ALU.mult))
            g(v.scalar_tensor_tensor(out=slot_id, in0=slot_id, scalar=1.0, in1=vz, op0=ALU.subtract, op1=ALU.add))
            g(v.tensor_copy(sid[:, :], slot_id))
            dve.sem_inc(S["slots_ready"], 1)

            for n in range(MAP_CHUNKS, CHUNKS):
                weights_low(n)

            def split_x(k, s, gathered_, free):
                dve.wait_ge(S["xt_done"], k + 1)
                for u in range(SUB):
                    dve.wait_ge(cw_gathered[s][u], gathered_)
                    if free is not None and u == 0:
                        dve.wait_ge(S["slot_free"], k - 1)
                    last = v.scalar_tensor_tensor(out=junk8[s][:, E * u:E * (u + 1)], in0=iota_sb[:, :],
                                           scalar=t_exp[:, bass.ds(k, 1)], in1=cwg[s][:, E * u:E * (u + 1)],
                                           op0=ALU.is_equal, op1=ALU.mult,
                                           accum_out=meta_cw[:, bass.ds(k * SUB + u, 1)])
                last.then_inc(S["slot_free"], 1)
                if free is not None:
                    dve.wait_ge(S["mm1_done"], free)
                v.tensor_copy(xhl[s], PS16[:, 1024 * s:1024 * (s + 1)]).then_inc(S["x_split"], 1)

            def split_h(k, s, free):
                if free is not None:
                    dve.wait_ge(S["mm2_done"], free)
                for q in range(4):
                    dve.wait_ge(S["gelu_done"], 8 * k + 2 * q + 2)
                    v.tensor_copy(hhi[s][:, 512 * q:512 * (q + 1)], hg[q]).then_inc(S["h_hi"], 1)
                    dve.wait_ge(S["h_hi"], 4 * k + q + 1)
                    v.tensor_tensor(hlo[s][:, 512 * q:512 * (q + 1)], hg[q], hhi[s][:, 512 * q:512 * (q + 1)],
                                    ALU.subtract).then_inc(S["h_split"], 1)

            def scale_y(k, s, free):
                dve.wait_ge(S["mm2_done"], k + 1)
                dve.wait_ge(S["slot_free"], k + 1)
                if free is not None:
                    dve.wait_ge(added[1], free)
                e = dve.value_load(t_expi[0:1, bass.ds(k, 1)], min_val=0, max_val=E - 1)
                b2 = A[:, bass.ds(e * D + b2_at, D)]
                v.scalar_tensor_tensor(out=ys[s].rearrange("p (u d) -> p u d", u=SUB),
                                       in0=bank(6 + s).rearrange("p (u d) -> p u d", u=SUB), scalar=1.0 / WSCALE,
                                       in1=b2.unsqueeze(1).broadcast_to((P, SUB, D)), op0=ALU.mult, op1=ALU.add)\
                    .then_inc(S["y_biased"], 1)
                dve.wait_ge(S["y_biased"], k + 1)
                dve.sem_inc(S["dve_tick"], 1)
                for u in range(SUB):
                    y = ys[s][:, D * u:D * (u + 1)]
                    last = v.tensor_scalar(y, y, meta_cw[:, bass.ds(k * SUB + u, 1)], None, ALU.mult)
                last.then_inc(S["y_done"], 1)

            dve.wait_ge(S["b2_loaded"], 16)
            split_x(0, 0, 16, None)
            split_x(1, 1, 16, None)
            split_h(0, 0, None)

            def step(k, s, half, first):
                split_x(k + 2, s, 16 * half + 32, 4 * k + 4)
                split_h(k + 1, 1 - s, None if first and s == 0 else k)
                scale_y(k, s, None if first else 16 * k - 16)

            step(0, 0, 0, True)
            step(1, 1, 0, True)
            with dve.Fori(1, NT // 2 - 1) as i:
                step(2 * i, 0, i, False)
                step(2 * i + 1, 1, i, False)
            split_h(NT - 1, 1, NT - 2)
            scale_y(NT - 2, 0, 16 * (NT - 3))
            scale_y(NT - 1, 1, 16 * (NT - 2))

        @block.tensor
        def _(pe):
            t = nc.tensor
            pe.wait_ge(S["patch_const_loaded"], 16 * N_PC)

            def patch(j, s, loaded):
                pe.wait_ge(patch_loaded[s], loaded)
                for c in range(KC):
                    t.matmul(bank(s, D), xP_sb[s][:, P * c:P * (c + 1)], Wp_sb[:, c, :], start=c == 0, stop=False)
                t.matmul(bank(s, D), psel[:, :], pos_sb[:, bass.ds(j * D, D)], start=False, stop=True)\
                    .then_inc(S["patch_done"], 1)

            patch(0, 0, 16)
            patch(1, 1, 16)
            with pe.Fori(1, PT // 2) as i:
                for s in range(2):
                    pe.wait_ge(S["h_patch"], 2 * i + s - 1)
                    patch(2 * i + s, s, 16 * i + 16)
            def turn(i, st):
                pe.wait_ge(S["e_ready"], i + 1)
                for s in range(3):
                    last = t.transpose(bank(st, P, P * s), e_sb[3 * st + s], ident[:, :])
                last.then_inc(S["eT_psum"], 1)

            def project(i, st, first):
                pe.wait_ge(S["eT_ready"], i + 1)
                for s in range(3):
                    dst = bank(2 + 2 * st, D, D * s) if s < 2 else bank(3 + 2 * st, D)
                    cls = first and s == 0
                    last = t.matmul(dst, eT[:, 3 * P * st + P * s:3 * P * st + P * (s + 1)], P12_sb[:, :],
                                    start=True, stop=not cls)
                    if cls:
                        t.matmul(dst, csel[:, :], crow[:, :], start=False, stop=True)
                last.then_inc(S["text_done"], 1)

            pe.wait_ge(S["const_loaded"], 16 * N_CONST)
            pe.wait_ge(S["h_patch"], PT)
            turn(0, 0)
            turn(1, 1)
            project(0, 0, True)
            pe.wait_ge(S["kf_ready"], 1)
            t.transpose(PS[:, 3072:3072 + P], KF[:, 0, :], ident[:, :])
            t.transpose(PS[:, 3072 + P:3072 + 2 * P], KF[:, 1, :], ident[:, :]).then_inc(S["kfT_psum"], 1)
            pe.wait_ge(S["kfT_ready"], 1)

            def toeplitz(n):
                if n >= 2:
                    pe.wait_ge(S["toep_ready"], n - 1)
                for u in range(2):
                    tt = 2 * n + u
                    o = 512 * (6 + n % 2) + D * u
                    last = t.matmul(PS[0:64, o:o + D], basis_sb[:, L - 1 - tt:2 * L - 1 - tt], kfT,
                                    start=True, stop=True)
                last.then_inc(S["toep_done"], 1)

            for k in range(TRIPLES):
                if 0 < k < TRIPLES - 1:
                    turn(k + 1, (k + 1) % 2)
                if k >= 2:
                    pe.wait_ge(S["h_text"], 6 * k - 9)
                if k:
                    project(k, k % 2, False)
                for n in toeplitz_share(k):
                    toeplitz(n)

            pe.wait_ge(S["xn_ready"], TILES)
            for n in range(32):
                if n % 8 == 0:
                    pe.wait_ge(toep_copied[n // 8], 16)
                if n >= 4:
                    pe.wait_ge(S["silu_done"], n - 3)
                for c in range(8):
                    ch = 8 * n + c
                    for q in (0, 64):
                        last = t.matmul(bank(4 + n % 4, TILES, TILES * c)[q:q + 64, :], Tz[q:q + 64, ch, :],
                                        X3[q:q + 64, :, ch], start=True, stop=True)
                last.then_inc(S["conv_done"], 1)

            def turn_rows(k):
                pe.wait_ge(S["row_ready"], k + 1)
                for s in range(3):
                    for w in range(2):
                        for c in range(2):
                            o = 2048 * (k % 2) + P * (4 * s + 2 * w + c)
                            last = t.transpose(PS16[:, o:o + P], X16[:, 3 * k + s, w, P * c:P * (c + 1)], ident16[:, :])
                last.then_inc(S["xT_psum"], 1)

            def gate(k):
                pe.wait_ge(S["xT_ready"], k + 1)
                for s in range(3):
                    dst = bank(7, E, (3 * k + s) * E)
                    for c in range(2):
                        o = P * (4 * s + c)
                        hi, lo = xT_sb[k % 2][:, o:o + P], xT_sb[k % 2][:, o + 2 * P:o + 3 * P]
                        t.matmul(dst, hi, wg_hi[:, E * c:E * (c + 1)], start=c == 0, stop=False)
                        t.matmul(dst, hi, wg_lo[:, E * c:E * (c + 1)], start=False, stop=False)
                        last = t.matmul(dst, lo, wg_hi[:, E * c:E * (c + 1)], start=False, stop=c == 1)
                last.then_inc(S["gate_done"], 1)

            pe.wait_ge(S["wg_ready"], 1)
            pe.wait_ge(S["silu_done"], 32)
            turn_rows(0)
            for k in range(TRIPLES2):
                if k + 1 < TRIPLES2:
                    turn_rows(k + 1)
                gate(k)
            pe.wait_ge(S["sel_ready"], 1)
            t.matmul(bank(0, GE), tri[:, :], selS, start=True, stop=True)
            t.matmul(bank(1, GE), ones[:, :], selS, start=True, stop=True).then_inc(S["ranks_done"], 1)

            def invert(b, s, first=False, last=False):
                pe.wait_ge(S["lo_ready"], b + 1)
                pe.wait_ge(S["hi_ready"], b + 1)
                for u in range(2 * BATCH):
                    ins = t.matmul(bank(2, P), hot_lo[s][:, P * u:P * (u + 1)], hot_hi[s][:, P * u:P * (u + 1)],
                                   start=first and u == 0, stop=last and u == 2 * BATCH - 1)
                ins.then_inc(S["map_done" if last else "hot_used"], 1)

            invert(0, 0, first=True)
            with pe.Fori(0, BATCHES // 3 - 1) as i:
                for s in range(3):
                    invert(3 * i + s + 1, (s + 1) % 3)
            invert(BATCHES - 3, 1)
            invert(BATCHES - 2, 2)
            invert(BATCHES - 1, 0, last=True)

            def turn_x(k, s, gathered_, free):
                for u in range(SUB):
                    pe.wait_ge(row_gathered[s][u], gathered_)
                if free is not None:
                    pe.wait_ge(S["x_split"], free)
                for u in range(SUB):
                    for w in range(2):
                        for c in range(2):
                            o = 1024 * s + 512 * w + 2 * P * c + P * u
                            last = t.transpose(PS16[:, o:o + P], xs[s][:, 512 * u + 256 * w + P * c:512 * u + 256 * w + P * (c + 1)],
                                               ident16[:, :])
                last.then_inc(S["xt_done"], 1)

            def experts_of(k, n):
                return nc.values_load_multi_w_load_instructions(t_expi[0:1, bass.ds(k, n)], engines=[mybir.EngineType.PE],
                                                                min_val=0, max_val=E - 1)[1]

            def w1_product(k, s, e, first):
                pe.wait_ge(S["x_split"], k + 1)
                for q in range(4):
                    if not first:
                        pe.wait_ge(S["gelu_done"], 8 * k + 2 * q - 6)
                    for f in (2 * q, 2 * q + 1):
                        dst = bank(2 + q, 256, 256 * (f % 2))
                        for c in range(2):
                            hi = A16[:, bass.ds(e * 8192 + (c * HID + f * P), P)]
                            lo = A16[:, bass.ds(e * 8192 + (2048 + c * HID + f * P), P)]
                            t.matmul(dst, hi, xhi[s][:, 256 * c:256 * (c + 1)], start=c == 0, stop=False)
                            t.matmul(dst, hi, xlo[s][:, 256 * c:256 * (c + 1)], start=False, stop=False)
                            last = t.matmul(dst, lo, xhi[s][:, 256 * c:256 * (c + 1)], start=False, stop=c == 1)
                    last.then_inc(S["mm1_done"], 1)

            def w2_product(k, s, e, free):
                if free is not None:
                    pe.wait_ge(S["y_done"], free)
                pe.wait_ge(S["h_split"], 4 * k + 4)
                for u in range(SUB):
                    dst = bank(6 + s, D, D * u)
                    for f in range(FCH):
                        hi = A16[:, bass.ds(e * 8192 + (4096 + f * D), D)]
                        lo = A16[:, bass.ds(e * 8192 + (6144 + f * D), D)]
                        o = 256 * f + P * u
                        t.matmul(dst, hhi[s][:, o:o + P], hi, start=f == 0, stop=False)
                        t.matmul(dst, hhi[s][:, o:o + P], lo, start=False, stop=False)
                        last = t.matmul(dst, hlo[s][:, o:o + P], hi, start=False, stop=f == FCH - 1)
                last.then_inc(S["mm2_done"], 1)

            pe.wait_ge(S["slots_ready"], 1)
            pe.wait_ge(S["w_free_pool"], POOL_CHUNKS)
            pe.wait_ge(S["w_free_dve"], CHUNKS - POOL_CHUNKS)
            turn_x(0, 0, 16, None)
            turn_x(1, 1, 16, None)
            w1_product(0, 0, experts_of(0, 1)[0], True)

            def step(k, s, half, e0, e1, first):
                w1_product(k + 1, 1 - s, e1, False)
                turn_x(k + 2, s, 16 * half + 32, k + 1)
                w2_product(k, s, e0, None if first else k - 1)

            ex = experts_of(0, 3)
            step(0, 0, 0, ex[0], ex[1], True)
            step(1, 1, 0, ex[1], ex[2], True)
            with pe.Fori(1, NT // 2 - 1) as i:
                ex = experts_of(2 * i, 3)
                step(2 * i, 0, i, ex[0], ex[1], False)
                step(2 * i + 1, 1, i, ex[1], ex[2], False)
            ex = experts_of(NT - 2, 2)
            w1_product(NT - 1, 1, ex[1], False)
            w2_product(NT - 2, 0, ex[0], NT - 3)
            w2_product(NT - 1, 1, ex[1], NT - 2)


def kernel(**inputs):
    import numpy as np
    import concourse.bacc as bacc
    from concourse.bass_utils import run_bass_kernel_spmd as run

    I = {k: np.asarray(v) for k, v in inputs.items()}
    f = np.float32
    half = np.arange(P) // 64
    arr = {}
    x = I["x"].reshape(L, 3, 6, 16, 6, 16).transpose(2, 4, 0, 1, 3, 5).reshape(2, PT, L, KC, P)
    arr["xP"] = x.transpose(1, 4, 3, 0, 2).reshape(PT * P, KC * P)
    arr["Wp"] = I["L0_tok_W"].T.reshape(KC, P, D).transpose(1, 0, 2).reshape(P, KC * D)
    pos = I["L0_tok_pos_embed"][0]
    arr["posrows"] = np.stack([pos[1:1 + PT].reshape(-1), pos[1 + PT:1 + 2 * PT].reshape(-1), np.tile(I["L0_tok_b"], PT)])
    arr["patsel"] = np.stack([half == 0, half == 1, half >= 0]).astype(f)
    arr["clssel"] = np.stack([half == 0, half == 0]).astype(f)
    arr["clsrows"] = np.stack([I["L0_tok_cls_token"][0, 0], pos[0]])
    txt = I["x_txt"]
    ids = np.full((P, TT), 127999, np.int32)
    ids[:64, 1:] = txt[:, :TT - 1]
    ids[64:, :] = txt[:, TT - 1:]
    arr["ids"] = ids
    table = np.zeros((VOCAB, D), f)
    table[:CUT0] = I["L0_txt_emb0"]
    table[CUT0:CUT1, :64] = I["L0_txt_emb1"]
    table[CUT1:, :64] = I["L0_txt_emb2"]
    arr["table"] = table
    arr["P12"] = np.concatenate([I["L0_txt_proj1"].T, I["L0_txt_proj2"].T], 0)
    parts = [I["L0_attn_log_dt"], I["L0_attn_inv_w_real"], I["L0_attn_w_imaginary"], I["L0_attn_B"].reshape(D, -1),
             I["L0_attn_P"].reshape(D, -1), I["L0_attn_C"].reshape(D, -1), I["L0_attn_D"].reshape(D, 1)]
    arr["prm"] = np.concatenate(parts, 1).reshape(2, P, PRM).transpose(1, 0, 2).reshape(P, 2, PRM)
    th = 2 * np.pi * np.arange(M) / L
    om = np.cos(th) - 1j * np.sin(th)
    om[-1] = -1.0
    arr["zc"] = np.tile(np.concatenate([2 * (1 - om).real, 2 * (1 - om).imag, (1 + om).real, (1 + om).imag])[None], (P, 1)).astype(f)
    lag = L - 1 - np.arange(2 * L - 1)
    w = np.where((np.arange(M) == 0) | (np.arange(M) == M - 1), 1.0, 2.0) * 2.0 / L
    ph = np.outer(np.arange(M), lag) * 2 * np.pi / L
    sn = -w[:, None] * np.sin(ph)
    sn[0] = sn[-1] = 0
    bas = np.concatenate([w[:, None] * np.cos(ph), sn, (lag == 0)[None] * 1.0], 0) * (lag >= 0)
    arr["basis"] = np.concatenate([bas, np.zeros((P - KROWS, 2 * L - 1))], 0).astype(f)
    arr["ident_d"] = np.eye(P, dtype=f)
    arr["tri_d"] = np.triu(np.ones((P, P), f), 1)
    arr["iota16_d"] = np.tile(np.arange(P)[None], (P, 1)).astype(np.float16)
    arr["rowid1_d"] = (TILES * np.arange(P)[:, None] + np.arange(TILES)[None] + 1).astype(f)
    arr["wg"] = I["L0_ffn_w_gate"].T.reshape(2, P, E).transpose(1, 0, 2).reshape(P, 2 * E)
    w1 = I["L0_ffn_W1"].reshape(E, 2, P, HID).transpose(0, 2, 1, 3).reshape(E, P, 2048)
    w2 = I["L0_ffn_W2"].reshape(E, FCH, P, D).transpose(0, 2, 1, 3).reshape(E, P, 2048)
    arr["wts"] = np.stack([w1, w2], 1).reshape(E * 2 * P, 2048)
    arr["b1T"] = I["L0_ffn_b1"].reshape(E, FCH, P).transpose(2, 0, 1).reshape(P, E * FCH)
    arr["b2d"] = np.tile(I["L0_ffn_b2"].reshape(1, E * D), (P, 1))
    arr["iota8"] = np.tile(np.arange(E, dtype=f)[None], (P, 1))
    arr["rev8"] = np.tile((E - np.arange(E, dtype=f))[None], (P, 1))
    arr["pad_row_d"] = TOKENS + 1 + np.arange(P, dtype=f)[:, None]
    arr["kcol"] = np.tile((SUB * P * np.arange(NT, dtype=f))[None], (P, 1))

    nc = bacc.Bacc("TRN2", target_bir_lowering=False, num_devices=1)
    args, feed = [], {}
    for name, a in arr.items():
        a = np.ascontiguousarray(a)
        feed[f"in_{name}"] = a
        args.append(nc.dram_tensor(f"in_{name}", a.shape, mybir.dt.from_np(a.dtype), kind="ExternalInput").ap())
    args.append(nc.dram_tensor("out_rows", (TOKENS + P, D), F32, kind="ExternalOutput").ap())
    build(nc, *args)
    r = run(nc, [feed], core_ids=[0])
    got = r.results[0]["out_rows"][:TOKENS].reshape(2, L, TILES, D).transpose(2, 0, 1, 3)
    out = np.empty((L, NCOL, D), f)
    out[:, 1:1 + PT] = got[:PT, 0].transpose(1, 0, 2)
    out[:, 1 + PT:1 + 2 * PT] = got[:PT, 1].transpose(1, 0, 2)
    out[:, 0] = got[PT, 0]
    out[:, 1 + 2 * PT:2 * PT + TT] = got[PT + 1:, 0].transpose(1, 0, 2)
    out[:, 2 * PT + TT:] = got[PT:, 1].transpose(1, 0, 2)
    return out
```
